# Optimizing a Trainium2 kernel written in Bass

```python
import numpy as np
import jax
import jax.numpy as jnp

def _softmax(x, axis=-1):
    return jax.nn.softmax(x, axis=axis)

def _gelu(x):
    return jax.nn.gelu(x, approximate=True)

def _silu(x):
    return jax.nn.silu(x)

def _sigmoid(x):
    return jax.nn.sigmoid(x)

def _layernorm(x, axis=-1, eps=1e-05):
    m = jnp.mean(x, axis=axis, keepdims=True)
    v = jnp.var(x, axis=axis, keepdims=True)
    return (x - m) / jnp.sqrt(v + eps)

def _scatter_add(tgt, idx, src, axis=0):
    return tgt.at[idx].add(src)

def _segment_sum(src, seg, n):
    return jax.ops.segment_sum(src, seg, n)
kernel_name = 'mk_seq_postln_d1_jaxref_r4_b8af93'

def setup_inputs(seed: int=0):
    np.random.seed(seed)
    _w = jnp.asarray

    def _L0_attn_setup():
        import jax, jax.numpy as jnp
        import numpy as np
        OFFSETS = sorted(set(range(0, 33)) | {48, 64, 96, 128, 192, 64, 96, 128, 192, 256, 384})
        B, N, D, H = (2, 512, 256, 16)
        HD = D // H

        def _shift(t, delta, n):
            if delta == 0:
                return t
            if delta >= n:
                return jnp.zeros_like(t)
            return jnp.pad(t[:, :, :n - delta], ((0, 0), (0, 0), (delta, 0), (0, 0)))
        key = jax.random.key(seed)
        ks = jax.random.split(key, 4)
        x = jax.random.normal(ks[0], (B, N, D), jnp.float32)
        Wqkv = jax.random.normal(ks[1], (D, 3 * D), jnp.float32) * D ** (-0.5)
        bqkv = jnp.zeros((3 * D,), jnp.float32)
        Wout = jax.random.normal(ks[2], (D, D), jnp.float32) * D ** (-0.5)
        bout = jnp.zeros((D,), jnp.float32)
        Wgate = jax.random.normal(ks[3], (D, D), jnp.float32) * D ** (-0.5)
        bgate = jnp.full((D,), 2.0, jnp.float32)
        alphas = np.linspace(0.2, 2.0, H, dtype=np.float32)
        deltas = np.log1p(np.asarray(OFFSETS, dtype=np.float32))
        pos_bias = jnp.asarray(-deltas[:, None] * alphas[None, :], jnp.float32)
        return dict(x=x, Wqkv=Wqkv, bqkv=bqkv, Wout=Wout, bout=bout, Wgate=Wgate, bgate=bgate, pos_bias=pos_bias)
    _L0_attn_in = _L0_attn_setup()

    def _L0_ffn_setup():
        import jax, jax.numpy as jnp
        import numpy as np
        B, T, C, E, K, CAP, H = (8, 512, 256, 8, 2, 1024, 1024)
        key = jax.random.key(seed)
        ks = jax.random.split(key, 6)
        s = 0.02
        return {'x': jax.random.normal(ks[0], (B, T, C), jnp.float32), 'rw1': s * jax.random.normal(ks[1], (C, H), jnp.float32), 'rb1': jnp.zeros((H,), jnp.float32), 'rw2': s * jax.random.normal(ks[2], (H, E), jnp.float32), 'rb2': jnp.zeros((E,), jnp.float32), 'ew1': s * jax.random.normal(ks[3], (E, C, H), jnp.float32), 'eb1': jnp.zeros((E, H), jnp.float32), 'ew2': s * jax.random.normal(ks[4], (E, H, C), jnp.float32), 'eb2': jnp.zeros((E, C), jnp.float32)}
    _L0_ffn_in = _L0_ffn_setup()
    _d = {'L0_attn_x': _L0_attn_in['x'], 'L0_attn_Wqkv': _L0_attn_in['Wqkv'], 'L0_attn_bqkv': _L0_attn_in['bqkv'], 'L0_attn_Wout': _L0_attn_in['Wout'], 'L0_attn_bout': _L0_attn_in['bout'], 'L0_attn_Wgate': _L0_attn_in['Wgate'], 'L0_attn_bgate': _L0_attn_in['bgate'], 'L0_attn_pos_bias': _L0_attn_in['pos_bias'], 'L0_ffn_rw1': _L0_ffn_in['rw1'], 'L0_ffn_rb1': _L0_ffn_in['rb1'], 'L0_ffn_rw2': _L0_ffn_in['rw2'], 'L0_ffn_rb2': _L0_ffn_in['rb2'], 'L0_ffn_ew1': _L0_ffn_in['ew1'], 'L0_ffn_eb1': _L0_ffn_in['eb1'], 'L0_ffn_ew2': _L0_ffn_in['ew2'], 'L0_ffn_eb2': _L0_ffn_in['eb2']}
    _x0 = _d['L0_attn_x']
    _d['L0_attn_x'] = jax.random.normal(jax.random.fold_in(jax.random.key(seed), 1), (16, 512, 256), dtype=_x0.dtype)
    del _x0
    return _d

def reference(L0_attn_x, L0_attn_Wqkv, L0_attn_bqkv, L0_attn_Wout, L0_attn_bout, L0_attn_Wgate, L0_attn_bgate, L0_attn_pos_bias, L0_ffn_rw1, L0_ffn_rb1, L0_ffn_rw2, L0_ffn_rb2, L0_ffn_ew1, L0_ffn_eb1, L0_ffn_ew2, L0_ffn_eb2):

    def _L0_attn_ref(x, Wqkv, bqkv, Wout, bout, Wgate, bgate, pos_bias):
        import jax, jax.numpy as jnp
        import numpy as np
        OFFSETS = sorted(set(range(0, 33)) | {48, 64, 96, 128, 192, 64, 96, 128, 192, 256, 384})
        B, N, D, H = (2, 512, 256, 16)
        HD = D // H

        def _shift(t, delta, n):
            if delta == 0:
                return t
            if delta >= n:
                return jnp.zeros_like(t)
            return jnp.pad(t[:, :, :n - delta], ((0, 0), (0, 0), (delta, 0), (0, 0)))
        b, n, d = x.shape
        scale = HD ** (-0.5)
        qkv = x @ Wqkv + bqkv
        q, k, v = jnp.split(qkv, 3, axis=-1)
        q = q.reshape(b, n, H, HD).transpose(0, 2, 1, 3)
        k = k.reshape(b, n, H, HD).transpose(0, 2, 1, 3)
        v = v.reshape(b, n, H, HD).transpose(0, 2, 1, 3)
        scores = jnp.stack([jnp.einsum('bhnd,bhnd->bhn', q, _shift(k, delta, n)) for delta in OFFSETS], axis=-1) * scale
        scores = scores + pos_bias.T[None, :, None, :]
        invalid = jnp.arange(n)[:, None] < jnp.asarray(OFFSETS)[None, :]
        scores = jnp.where(invalid[None, None], -jnp.inf, scores)
        alpha = jax.nn.softmax(scores, axis=-1)
        out = jnp.zeros_like(q)
        for i, delta in enumerate(OFFSETS):
            out = out + alpha[..., i:i + 1] * _shift(v, delta, n)
        flat = out.transpose(0, 2, 1, 3).reshape(b, n, d)
        gate = jax.nn.sigmoid(x @ Wgate + bgate)
        return flat * gate @ Wout + bout

    def _L0_ffn_ref(x, rw1, rb1, rw2, rb2, ew1, eb1, ew2, eb2):
        import jax, jax.numpy as jnp
        import numpy as np
        B, T, C, E, K, CAP, H = (8, 512, 256, 8, 2, 1024, 1024)
        Bx, Tx, Cx = x.shape
        N = Bx * Tx
        logits = jax.nn.relu(x @ rw1 + rb1) @ rw2 + rb2
        vals, ids = jax.lax.top_k(logits, K)
        probs = jax.nn.softmax(vals, axis=-1)
        ids_f = ids.reshape(N * K)
        probs_f = probs.reshape(N * K)
        xr = jnp.repeat(x.reshape(N, Cx), K, axis=0)
        m = jax.nn.one_hot(ids_f, E, dtype=jnp.int32)
        pos = jnp.cumsum(m, axis=0) - 1
        pos_tok = jnp.take_along_axis(pos, ids_f[:, None], axis=1)[:, 0]
        keep = (pos_tok < CAP).astype(x.dtype)
        pos_c = jnp.clip(pos_tok, 0, CAP - 1)
        disp = jnp.zeros((E, CAP, Cx), x.dtype).at[ids_f, pos_c].add(xr * keep[:, None])
        h = jax.nn.relu(jnp.einsum('enc,ech->enh', disp, ew1) + eb1[:, None, :])
        eo = jnp.einsum('enh,ehc->enc', h, ew2) + eb2[:, None, :]
        y = eo[ids_f, pos_c] * (probs_f * keep)[:, None]
        return y.reshape(Bx, Tx, K, Cx).sum(axis=2)
    x = L0_attn_x
    x = _layernorm(x + _L0_attn_ref(x, L0_attn_Wqkv, L0_attn_bqkv, L0_attn_Wout, L0_attn_bout, L0_attn_Wgate, L0_attn_bgate, L0_attn_pos_bias), axis=-1)
    x = _layernorm(x + _L0_ffn_ref(x, L0_ffn_rw1, L0_ffn_rb1, L0_ffn_rw2, L0_ffn_rb2, L0_ffn_ew1, L0_ffn_eb1, L0_ffn_ew2, L0_ffn_eb2), axis=-1)
    return x

_drawn_inputs = setup_inputs


def setup_inputs(seed=0):
    import zlib

    import numpy as np

    out = dict(_drawn_inputs(seed))
    spreads = {'L0_attn_bqkv': (0.0, 0.1),
     'L0_attn_bout': (0.0, 0.1),
     'L0_attn_bgate': (2.0, 0.6),
     'L0_ffn_rb1': (0.0, 0.1),
     'L0_ffn_rb2': (0.0, 0.1),
     'L0_ffn_eb1': (0.0, 0.422),
     'L0_ffn_eb2': (0.0, 0.1)}
    factors = {}
    for name, (base, spread) in spreads.items():
        noise = np.random.default_rng([zlib.crc32(name.encode()), seed]).standard_normal(out[name].shape)
        drawn = base * np.exp(spread * noise) if base else spread * noise
        out[name] = jnp.asarray(drawn.astype(out[name].dtype))
    for name, factor in factors.items():
        out[name] = (out[name] * factor).astype(out[name].dtype)
    return out
```

```python
import concourse.bass as bass
from concourse import mybir
from contextlib import ExitStack


FP32 = mybir.dt.float32
F16 = mybir.dt.float16
U32 = mybir.dt.uint32
I32 = mybir.dt.int32
ALU = mybir.AluOpType
ACT = mybir.ActivationFunctionType
AX = mybir.AxisListType

P = 128
B, N, D, H = 16, 512, 256, 16
HD = D // H
TILES = N // P
CT = D // P
OFFSETS = sorted(set(range(0, 33)) | {48, 64, 96, 128, 192, 256, 384})
NOFF = len(OFFSETS)
NEAR = 32
FAR_STEP = 16
E, CAP, FF = 8, 1024, 1024
HT = FF // P
TOK = B * N
SLOTS = E * CAP
LN_EPS = 1e-5
WS = 64.0
NEG = -1e30
NEG16 = -30000.0
DROPPED = 65536.0
PAIRS = H // 2
STACK = 64
MROW = 3 * HD
KST = MROW + 1
VW = 2 * HD + 1
COL = {0: 0, 1: 512, 3: 896, 2: 1024}
SCW = 1280
GP_BANKS, ST_BANKS = 3, 4

FILLERS = {
    0: [("proj", "x")], 1: [("proj", "qk")], 2: [("proj", "vg")],
    3: [("outp", "t")], 4: [("outp", "w")],
    5: [("maxp", "near0"), ("outp", "y")], 6: [("maxp", "near1")], 7: [("maxp", "near2")], 8: [("maxp", "near3")],
    9: [("maxp", "far0")], 10: [("maxp", "far1")], 11: [("maxp", "t"), ("rout", "t")],
    12: [("rout", "h0"), ("rout", "h1")], 13: [("rout", "h2"), ("rout", "h3")],
    14: [("rout", "l")], 15: [("rout", "c")],
}
UNITS = {("proj", "x"): 2, ("proj", "qk"): 4, ("proj", "vg"): 4, ("outp", "t"): 2, ("outp", "w"): 2,
         ("outp", "y"): 0, ("maxp", "near0"): 2, ("maxp", "near1"): 2, ("maxp", "near2"): 2,
         ("maxp", "near3"): 2, ("maxp", "far0"): 2, ("maxp", "far1"): 2, ("maxp", "t"): 1,
         ("rout", "t"): 2, ("rout", "h0"): 2, ("rout", "h1"): 2, ("rout", "h2"): 2, ("rout", "h3"): 2,
         ("rout", "l"): 1, ("rout", "c"): 1}
AHEAD = {"proj": 1, "maxp": 1, "outp": -1, "rout": -1}
FIRST_LOOP, LAST_LOOP = 2, 13


class Apart:

    def __init__(self, eng, passed):
        self.eng, self.passed = eng, passed

    def wait_ge(self, sem, value):
        self.eng.wait_ge(sem, value)
        if not isinstance(value, int):
            self.eng.sem_inc(self.passed, 1)


class Batch:

    def __init__(self, i, c):
        self.i, self.c = i, c

    def at(self, k, plus=0):
        v = k * self.c + plus
        return v if self.i is None else self.i * (2 * k) + v

    def half(self, k, plus=0):
        v = k * (self.c // 2) + plus
        return v if self.i is None else self.i * k + v

    @property
    def par(self):
        return self.c % 2

    def shift(self, d):
        return Batch(self.i, self.c + d)

    def in_range(self):
        return self.i is not None or 0 <= self.c < B


def wait(eng, sem, value):
    if not isinstance(value, int) or value > 0:
        eng.wait_ge(sem, value)


def iterations():
    return range(-1, B + 1)


def parts_of(it):
    for k in range(H):
        for stage, part in FILLERS[k]:
            if 0 <= it + AHEAD[stage] < B:
                yield stage, part


def gp_table():
    table = {}
    count = [0] * GP_BANKS
    for it in iterations():
        u = 0
        for stage, part in parts_of(it):
            for k in range(UNITS[stage, part]):
                table[it, stage, part, k] = (u % GP_BANKS, count[u % GP_BANKS])
                count[u % GP_BANKS] += 1
                u += 1
    return table


GP = gp_table()
GP_PER = (GP[3, "proj", "x", 0][1] - GP[2, "proj", "x", 0][1])
assert sum(UNITS.values()) == GP_PER * GP_BANKS


def gp_slot(n, stage, part, k):
    if n.i is None:
        return GP[n.c - AHEAD[stage], stage, part, k]
    bank, before = GP[FIRST_LOOP, stage, part, k]
    it = n.shift(-AHEAD[stage])
    return bank, it.at(GP_PER, before - FIRST_LOOP * GP_PER)


def run_iterations(eng, head, part, last):
    def one(it):
        for k in range(H):
            if it.in_range():
                head(it, k)
            for stage, name in FILLERS[k]:
                n = it.shift(AHEAD[stage])
                if n.in_range():
                    part[stage](n, name)
        if it.in_range():
            last(it)

    for c in range(-1, FIRST_LOOP):
        one(Batch(None, c))
    with eng.Fori(FIRST_LOOP // 2, (LAST_LOOP + 1) // 2) as i:
        one(Batch(i, 0))
        one(Batch(i, 1))
    for c in range(LAST_LOOP + 1, B + 1):
        one(Batch(None, c))


def build(nc, x, Wqkv, bqkv, Wout, bout, Wgate, bgate, pos_bias,
          rw1, rb1, rw2, rb2, ew1, eb1, ew2, eb2, out):
    x_rows = x.rearrange("b n d -> (b n) d")
    out_rows = out.rearrange("b n d -> (b n) d")

    def dram(name, shape, dt):
        return nc.dram_tensor(name, shape, dt, kind="Internal").ap()

    bias_vec = dram("bias_vec", (H, P, P + N), FP32)
    near_vec = dram("near_vec", (H, 32, 96), F16)
    far_vec = dram("far_vec", (H, 32, 64), F16)
    qk_dram = [dram(f"qk_dram{i}", (4, D, N), F16) for i in range(2)]
    m_dram = [dram(f"m_dram{i}", (H, N), F16) for i in range(2)]
    xln = dram("xln", (TOK, D), FP32)
    disp = dram("disp", (SLOTS, 2 * D), F16)
    eo = dram("eo", (SLOTS, D), FP32)

    outer = ExitStack()
    with outer:
        def keep(name, shape, dt):
            return outer.enter_context(nc.sbuf_tensor(name, shape, dt))

        ident = keep("ident", [P, P], F16)
        gslot = keep("gslot", [P, TOK // P * 2], U32)
        gweight = keep("gweight", [P, TOK // P * 2], FP32)
        attention(nc, locals())
        experts(nc, locals())
        combine(nc, locals())


def attention(nc, g):
    ctx = ExitStack()
    with ctx:
        def sb(name, shape, dt):
            return ctx.enter_context(nc.sbuf_tensor(name, shape, dt))

        def pb(name, shape, dt):
            return ctx.enter_context(nc.psum_tensor(name, shape, dt))

        def sem(name):
            return ctx.enter_context(nc.semaphore(name))

        ident, gslot, gweight = g["ident"], g["gslot"], g["gweight"]
        xln, disp, qk_dram = g["xln"], g["disp"], g["qk_dram"]
        m_dram = g["m_dram"]
        bias_vec, near_vec, far_vec = g["bias_vec"], g["near_vec"], g["far_vec"]
        pos_bias = g["pos_bias"]

        score_bias = sb("score_bias", [P, 2, PAIRS, N], FP32)
        near_mask = sb("near_mask", [P, PAIRS, 2 * NEAR], F16)
        far_mask = sb("far_mask", [P, 2, PAIRS, 32], F16)
        sel_first = sb("sel_first", [P, P], F16)
        sel_rest = sb("sel_rest", [P, P], F16)
        before_mat = sb("before_mat", [P, P], F16)
        ones_mat = sb("ones_mat", [P, P], F16)
        wqk = sb("wqk", [P, 2, CT, 2 * D], F16)
        wvg = sb("wvg", [P, 2, CT, 2 * D], F16)
        wout = sb("wout", [P, 2, CT, D], F16)
        wr1 = sb("wr1", [P, 2, CT, FF], F16)
        wr2 = sb("wr2", [P, HT, 2 * E], F16)
        bqk = sb("bqk", [P, 4], FP32)
        bvg = sb("bvg", [P, 2 * D], FP32)
        bo = sb("bo", [P, D], FP32)
        br1 = sb("br1", [P, HT], FP32)
        br2 = sb("br2", [P, TILES, E], FP32)
        expert_id = sb("expert_id", [P, E], FP32)
        expert_row = sb("expert_row", [P, TILES, E], FP32)
        taken = sb("taken", [P, E], FP32)

        xin = sb("xin", [P, TILES, D], FP32)
        x16 = sb("x16", [P, 2, TILES, D], F16)
        featT = sb("featT", [P, 2, CT, N], F16)
        qk32 = sb("qk32", [P, 2, N], FP32)
        qk16 = sb("qk16", [P, 2, 4, N], F16)
        qs = [sb(f"qs{i}", [P, PAIRS, N], F16) for i in range(2)]
        ks = [sb(f"ks{i}", [P, PAIRS, N], F16) for i in range(2)]
        vg32 = sb("vg32", [P, 2, 2 * D], FP32)
        vs = [sb(f"vs{i}", [P, TILES, H, VW], F16) for i in range(2)]
        eg = [sb(f"eg{i}", [P, TILES * H, HD], FP32) for i in range(2)]
        m_near = sb("m_near", [P, TILES, 2, PAIRS], F16)
        m_far = sb("m_far", [P, TILES, 2, PAIRS], F16)
        m_nearT = sb("m_nearT", [H, N], F16)
        mT = sb("mT", [H, N], F16)
        sc = sb("sc", [P, 2, SCW], FP32)
        p16 = sb("p16", [P, 2, 2, SCW], F16)
        ob = sb("ob", [P, TILES, H, VW], FP32)
        og = sb("og", [P, TILES * H, HD], FP32)
        og16 = sb("og16", [P, 2, TILES, D], F16)
        xres = sb("xres", [P, TILES, D], FP32)
        y32 = sb("y32", [P, TILES, D], FP32)
        stats = sb("stats", [P, TILES, 6], FP32)
        mv = sb("mv", [P, TILES, 2], FP32)
        veps = sb("veps", [P, TILES], FP32)
        halfneg = sb("halfneg", [P, TILES], FP32)
        rstd = sb("rstd", [P, TILES], FP32)
        y16 = sb("y16", [P, TILES, 2 * D], F16)
        hid32 = sb("hid32", [P, 2, N], FP32)
        hid16 = sb("hid16", [P, 2, HT, N], F16)
        oden = hid16[:, 0, 0:4, :].rearrange("q h t -> q (h t)").bitcast(FP32).rearrange("q (a d) -> q a d", d=HD)
        lg = sb("lg", [P, TILES, E], FP32)
        top = sb("top", [P, TILES, 8], FP32)
        topi = sb("topi", [P, TILES, 8], U32)
        topf = sb("topf", [P, TILES, 2], FP32)
        onehot = sb("onehot", [P, TILES, 2, E], FP32)
        chosen = sb("chosen", [P, TILES, E], F16)
        rpos = sb("rpos", [P, TILES, E], FP32)
        rover = sb("rover", [P, TILES, E], FP32)
        rprod = sb("rprod", [P, TILES, 2, E], FP32)
        rslot = sb("rslot", [P, TILES, 2], FP32)
        sidx = sb("sidx", [P, TILES, 2], U32)
        rkeep = sb("rkeep", [P, TILES, 2], FP32)
        rdiff = sb("rdiff", [P, TILES], FP32)
        rexp = sb("rexp", [P, TILES], FP32)
        rprob = sb("rprob", [P, TILES, 2], FP32)

        gp = [pb(f"gp{i}", [P, 512], FP32) for i in range(GP_BANKS)]
        st = [pb(f"st{i}", [P, 512], FP32) for i in range(ST_BANKS)]
        opv = pb("opv", [P, 2, TILES, VW], FP32)

        setup(nc, g, locals())

        sp_passed, dve_passed, pool_passed = sem("sp_passed"), sem("dve_passed"), sem("pool_passed")
        x_loaded, xres_loaded = sem("x_loaded"), sem("xres_loaded")
        xh_ready, xl_ready = sem("xh_ready"), sem("xl_ready")
        gp_full = [sem(f"gp_full{i}") for i in range(GP_BANKS)]
        gp_drained = [sem(f"gp_drained{i}") for i in range(GP_BANKS)]
        st_full = [sem(f"st_full{i}") for i in range(ST_BANKS)]
        st_drained = [sem(f"st_drained{i}") for i in range(ST_BANKS)]
        qk_hi, qk_split, qk_stored = sem("qk_hi"), sem("qk_split"), sem("qk_stored")
        stack_in = [sem(f"stack_in{i}") for i in range(2)]
        v_hi, v_split, eg_ready = sem("v_hi"), sem("v_split"), sem("eg_ready")
        m_copied, m_stored = sem("m_copied"), sem("m_stored")
        m_in = [sem(f"m_in{i}") for i in range(2)]
        exp_ready, plo_ready, pv_done = sem("exp_ready"), sem("plo_ready"), sem("pv_done")
        o_drained = sem("o_drained")
        og_step, og_ready, og_hi, og_lo = sem("og_step"), sem("og_ready"), sem("og_hi"), sem("og_lo")
        xres_ready, ln_step, var_ready, veps_ready = sem("xres_ready"), sem("ln_step"), sem("var_ready"), sem("veps_ready")
        rstd_ready, y_ready = sem("rstd_ready"), sem("y_ready")
        yh_ready, yl_ready, y_stored = sem("yh_ready"), sem("yl_ready"), sem("y_stored")
        hid_hi, hid_lo = sem("hid_hi"), sem("hid_lo")
        r_step, chosen_ready = sem("r_step"), sem("chosen_ready")
        diff_ready, rexp_ready, sidx_ready = sem("diff_ready"), sem("rexp_ready"), sem("sidx_ready")
        scattered = sem("scattered")

        def full(eng, n, stage, part, k):
            bank, before = gp_slot(n, stage, part, k)
            eng.wait_ge(gp_full[bank], before + 1)
            return gp[bank]

        def drained(eng, n, stage, part, k):
            bank, before = gp_slot(n, stage, part, k)
            eng.wait_ge(gp_drained[bank], before + 1)

        def gp_done(instruction, n, stage, part, k):
            instruction.then_inc(gp_drained[gp_slot(n, stage, part, k)[0]], 1)

        def feat_used_by_proj(eng, n):
            ahead = n.shift(2)
            full(eng, ahead if ahead.in_range() else Batch(None, B - 1), "proj", "vg", TILES - 1)

        def feat_used_before_proj(eng, n):
            if n.i is not None or n.c >= 3:
                full(eng, n.shift(-3), "rout", "h3", 1)
            elif n.c >= 1:
                full(eng, n.shift(-1), "proj", "vg", TILES - 1)

        def st_slot(n, h, k):
            u = 3 * h + k
            return u % ST_BANKS, n.at(3 * H // ST_BANKS, u // ST_BANKS)

        block = ctx.enter_context(nc.Block())

        @block.sync
        def _(sync):
            sp = Apart(sync, sp_passed)

            def load_x(n):
                wait(sp, xh_ready, n.at(1))
                wait(sp, xl_ready, n.at(1))
                sync.dma_start(xin[:, :, :], g["x_rows"][bass.ds(n.at(N), N), :].rearrange("(t p) d -> p t d", p=P)).then_inc(x_loaded, 16)

            def head(n, h):
                if h == 0 and n.shift(2).in_range() and not (n.i is None and n.c + 2 >= B):
                    load_x(n.shift(2))
                if h == 5:
                    if n.i is not None or n.c > 0:
                        drained(sp, n.shift(-1), "outp", "w", 1)
                    sync.dma_start(xres[:, :, :], g["x_rows"][bass.ds(n.at(N), N), :].rearrange("(t p) d -> p t d", p=P)).then_inc(xres_loaded, 16)

            def proj(n, part):
                if part != "vg":
                    return
                sp.wait_ge(qk_split, n.at(4, 4))
                wait(sp, stack_in[n.par], n.half(192))
                for i in range(2):
                    for w in range(2):
                        sync.dma_start(qk_dram[n.par][2 * w + i].rearrange("(u f) t -> f u t", f=P),
                                     qk16[:, i, 2 * w:2 * w + 2, :]).then_inc(qk_stored, 16)
                sp.wait_ge(qk_stored, n.at(64, 64))
                if n.i is not None or n.c >= 2:
                    bank, before = st_slot(n.shift(-2), H - 1, 2)
                    sp.wait_ge(st_full[bank], before + 1)
                for w, dst, halves in ((0, qs, (0, 1, 0)), (1, ks, (0, 0, 1))):
                    for e in range(2):
                        for t, i in enumerate(halves):
                            src = qk_dram[n.par][2 * w + i].rearrange("(p e d) t -> e d p t", e=2, d=HD)[e]
                            r = STACK * e + HD * t
                            sync.dma_start(dst[n.par][r:r + HD, :, :], src).then_inc(stack_in[n.par], 16)

            def maxp(n, part):
                if part != "t":
                    return
                drained(sp, n, "maxp", "t", 0)
                sync.dma_start(m_dram[n.par], mT[:, :]).then_inc(m_stored, 16)
                sp.wait_ge(m_stored, n.at(16, 16))
                for e in range(2):
                    r = STACK * e + MROW
                    sync.dma_start(qs[n.par][r:r + 1, :, :], m_dram[n.par][PAIRS * e:PAIRS * (e + 1), :].unsqueeze(0)).then_inc(m_in[n.par], 16)

            def outp(n, part):
                if part == "y":
                    sp.wait_ge(y_ready, n.at(4, 4))
                    sync.dma_start(xln[bass.ds(n.at(N), N), :].rearrange("(t p) d -> p t d", p=P), y32[:, :, :]).then_inc(y_stored, 16)

            def nothing(n, part):
                pass

            load_x(Batch(None, 0))
            load_x(Batch(None, 1))
            run_iterations(sync, head, dict(proj=proj, maxp=maxp, outp=outp, rout=nothing), lambda n: None)
            sp.wait_ge(y_stored, 16 * B)

        @block.tensor
        def _(pe):
            def unit(n, stage, part, k):
                bank, before = gp_slot(n, stage, part, k)
                wait(pe, gp_drained[bank], before)
                return gp[bank], gp_full[bank]

            def transposes(n, stage, part, k, src):
                bank, is_full = unit(n, stage, part, k)
                view = bank[:, :].bitcast(F16)
                for c in range(CT):
                    for t in range(TILES):
                        last = nc.tensor.transpose(view[:, c * N + t * P:c * N + (t + 1) * P], src(t, c), ident[:, :])
                last.then_inc(is_full, 1)

            def terms(lhs, rhs, dst):
                todo = [(c, a, b) for c in range(CT) for a, b in ((0, 0), (0, 1), (1, 0))]
                for k, (c, a, b) in enumerate(todo):
                    last = nc.tensor.matmul(dst, lhs(a, c), rhs(b, c), start=(k == 0), stop=(k == len(todo) - 1))
                return last

            def scores(n, h):
                p, e = h // 2, h % 2
                rows = slice(STACK * e, STACK * e + KST)
                if h == 0:
                    pe.wait_ge(m_in[n.par], n.half(32, 32))
                for k, js in enumerate(((0,), (1, 3), (2,))):
                    bank, before = st_slot(n, h, k)
                    wait(pe, st_drained[bank], before)
                    for j in js:
                        w = N - P * j
                        at = COL[j] % 512
                        last = nc.tensor.matmul(st[bank][:, at:at + w], ks[n.par][rows, p, P * j:P * (j + 1)],
                                                qs[n.par][rows, p, P * j:N], start=True, stop=True)
                    last.then_inc(st_full[bank], 1)

            def values(n, h):
                pe.wait_ge(plo_ready, n.at(H, h + 1))
                if h == 0:
                    pe.wait_ge(v_split, n.at(TILES, TILES))
                if h % 2 == 0:
                    wait(pe, o_drained, n.at(PAIRS, h // 2))
                for i in range(TILES):
                    for j in range(i + 1):
                        c = COL[j] + P * (i - j)
                        nc.tensor.matmul(opv[:, h % 2, i, :], p16[:, h % 2, 0, c:c + P], vs[n.par][:, j, h, :],
                                         start=(j == 0), stop=False, skip_group_check=True)
                        last = nc.tensor.matmul(opv[:, h % 2, i, 0:HD + 1], p16[:, h % 2, 1, c:c + P], vs[n.par][:, j, h, 0:HD + 1],
                                                start=False, stop=(j == i), skip_group_check=True)
                last.then_inc(pv_done, 1)

            def head(n, h):
                if h >= 2:
                    values(n, h - 2)
                scores(n, h)

            def proj(n, part):
                if part == "x":
                    pe.wait_ge(xh_ready, n.at(1, 1))
                    transposes(n, "proj", "x", 0, lambda t, c: x16[:, 0, t, P * c:P * (c + 1)])
                    pe.wait_ge(xl_ready, n.at(1, 1))
                    transposes(n, "proj", "x", 1, lambda t, c: x16[:, 1, t, P * c:P * (c + 1)])
                elif part == "qk":
                    drained(pe, n, "proj", "x", 0)
                    drained(pe, n, "proj", "x", 1)
                    for u in range(4):
                        bank, is_full = unit(n, "proj", "qk", u)
                        terms(lambda a, c: wqk[:, a, c, P * u:P * (u + 1)], lambda b, c: featT[:, b, c, :],
                              bank[:, :]).then_inc(is_full, 1)
                else:
                    for t in range(TILES):
                        bank, is_full = unit(n, "proj", "vg", t)
                        last = terms(lambda a, c: featT[:, a, c, P * t:P * (t + 1)], lambda b, c: wvg[:, b, c, :], bank[:, :])
                        last.then_inc(is_full, 1)

            def maxp(n, part):
                if part == "t":
                    bank, is_full = unit(n, "maxp", "t", 0)
                    for k in range(2):
                        drained(pe, n, "maxp", "far0", k)
                        drained(pe, n, "maxp", "far1", k)
                    view = bank[0:H, :].bitcast(F16)
                    for k, src in enumerate((m_near, m_far)):
                        for i in range(TILES):
                            last = nc.tensor.transpose(view[:, k * N + i * P:k * N + (i + 1) * P],
                                                       src[:, i, :, :].rearrange("q e p -> q (e p)"), ident[:, :])
                    last.then_inc(is_full, 1)
                    return
                if part == "near0":
                    pe.wait_ge(stack_in[n.par], n.half(192, 192))
                for e in range(2):
                    bank, is_full = unit(n, "maxp", part, e)
                    r0 = STACK * e
                    q, k = qs[n.par], ks[n.par]
                    if part[:4] == "near":
                        i = int(part[4])
                        rows = slice(r0, r0 + (2 if i == 0 else 1) * 32)
                        sel = sel_first if i == 0 else sel_rest
                        nc.tensor.matmul(bank[:, :], sel[rows, :], near_mask[rows, :, :].rearrange("r p w -> r (p w)"),
                                         start=True, stop=False, skip_group_check=True)
                        for b in range(4):
                            lo = P * i + 32 * b
                            first = 32 if lo == 0 else 0
                            for p in range(PAIRS):
                                last = nc.tensor.matmul(bank[32 * b:32 * b + 32, 64 * p + first:64 * p + 64],
                                                        q[r0:r0 + HD, p, lo:lo + 32], k[r0:r0 + HD, p, lo - 32 + first:lo + 32],
                                                        start=False, stop=(b == 3 and p == PAIRS - 1), skip_group_check=True)
                    else:
                        nc.tensor.matmul(bank[:, :], sel_rest[r0:r0 + 32, :], far_mask[r0:r0 + 32, :, :, :].rearrange("r g p w -> r (g p w)"),
                                         start=True, stop=False, skip_group_check=True)
                        for gg in range(2):
                            for r4 in range(4):
                                r = 4 * (2 * int(part[3]) + gg) + r4
                                for p in range(PAIRS):
                                    c = 256 * gg + 32 * p
                                    last = nc.tensor.matmul(bank[32 * r4:32 * r4 + 32, c:c + 32],
                                                            q[r0:r0 + HD, p, r:N:FAR_STEP], k[r0:r0 + HD, p, r:N:FAR_STEP],
                                                            start=False, stop=(gg == 1 and r4 == 3 and p == PAIRS - 1), skip_group_check=True)
                    last.then_inc(is_full, 1)

            def outp(n, part):
                if part == "t":
                    pe.wait_ge(og_hi, n.at(1, 1))
                    transposes(n, "outp", "t", 0, lambda t, c: og16[:, 0, t, P * c:P * (c + 1)])
                    pe.wait_ge(og_lo, n.at(1, 1))
                    transposes(n, "outp", "t", 1, lambda t, c: og16[:, 1, t, P * c:P * (c + 1)])
                elif part == "w":
                    drained(pe, n, "outp", "t", 0)
                    drained(pe, n, "outp", "t", 1)
                    for u in range(2):
                        bank, is_full = unit(n, "outp", "w", u)
                        for t in (2 * u, 2 * u + 1):
                            last = terms(lambda a, c: featT[:, a, c, P * t:P * (t + 1)], lambda b, c: wout[:, b, c, :],
                                         bank[:, D * (t % 2):D * (t % 2 + 1)])
                        last.then_inc(is_full, 1)

            def rout(n, part):
                if part == "t":
                    pe.wait_ge(yh_ready, n.at(1, 1))
                    transposes(n, "rout", "t", 0, lambda t, c: y16[:, t, P * c:P * (c + 1)])
                    pe.wait_ge(yl_ready, n.at(1, 1))
                    transposes(n, "rout", "t", 1, lambda t, c: y16[:, t, D + P * c:D + P * (c + 1)])
                elif part[0] == "h":
                    if part == "h0":
                        drained(pe, n, "rout", "t", 0)
                        drained(pe, n, "rout", "t", 1)
                    for k in range(2):
                        ht = 2 * int(part[1]) + k
                        bank, is_full = unit(n, "rout", part, k)
                        terms(lambda a, c: wr1[:, a, c, P * ht:P * (ht + 1)], lambda b, c: featT[:, b, c, :],
                              bank[:, :]).then_inc(is_full, 1)
                elif part == "l":
                    bank, is_full = unit(n, "rout", "l", 0)
                    pe.wait_ge(hid_lo, n.at(HT, HT))
                    for t in range(TILES):
                        for ht in range(HT):
                            nc.tensor.matmul(bank[:, 16 * t:16 * t + 16], hid16[:, 0, ht, P * t:P * (t + 1)], wr2[:, ht, :],
                                             start=(ht == 0), stop=False, skip_group_check=True)
                            last = nc.tensor.matmul(bank[:, 16 * t:16 * t + E], hid16[:, 1, ht, P * t:P * (t + 1)], wr2[:, ht, 0:E],
                                                    start=False, stop=(ht == HT - 1), skip_group_check=True)
                    last.then_inc(is_full, 1)
                else:
                    bank, is_full = unit(n, "rout", "c", 0)
                    pe.wait_ge(chosen_ready, n.at(1, 1))
                    for t in range(TILES):
                        for s in range(t + 1):
                            nc.tensor.matmul(bank[:, E * t:E * (t + 1)], (before_mat if s == t else ones_mat)[:, :], chosen[:, s, :],
                                             start=(s == 0), stop=(s == t))
                    for s in range(TILES):
                        last = nc.tensor.matmul(bank[:, E * TILES:E * (TILES + 1)], ones_mat[:, :], chosen[:, s, :],
                                                start=(s == 0), stop=(s == TILES - 1))
                    last.then_inc(is_full, 1)

            def last(n):
                values(n, H - 2)
                values(n, H - 1)

            run_iterations(pe, head, dict(proj=proj, maxp=maxp, outp=outp, rout=rout), last)

        @block.scalar
        def _(act):
            def evacuate_values(n, h):
                act.wait_ge(pv_done, n.at(H, h + 1))
                if h == 1:
                    wait(act, og_ready, n.at(1))
                nc.scalar.copy(ob[:, :, h - 1:h + 1, :].rearrange("q i h c -> q h i c"), opv[:, :, :, :]).then_inc(o_drained, 1)

            def head(n, h):
                bank, before = st_slot(n, h, 2)
                act.wait_ge(st_drained[bank], before + 1)
                wait(act, pv_done, n.at(H, h - 1))
                nc.scalar.activation(p16[:, h % 2, 0, :], sc[:, h % 2, :], ACT.Exp)
                nc.scalar.activation(sc[:, h % 2, :], sc[:, h % 2, :], ACT.Exp).then_inc(exp_ready, 1)
                if h >= 3 and h % 2 == 1:
                    evacuate_values(n, h - 2)

            def proj(n, part):
                if part == "x":
                    act.wait_ge(x_loaded, n.at(16, 16))
                    nc.scalar.copy(x16[:, 0, :, :], xin[:, :, :]).then_inc(xh_ready, 1)
                    bank = full(act, n, "proj", "x", 1)
                    feat_used_before_proj(act, n)
                    gp_done(nc.scalar.copy(featT[:, 1, :, :].rearrange("f c t -> f (c t)"), bank[:, :].bitcast(F16)), n, "proj", "x", 1)
                elif part == "qk":
                    for u in range(4):
                        bank = full(act, n, "proj", "qk", u)
                        wait(act, qk_split, n.at(4, u - 1))
                        scale = HD ** -0.5 / WS if u < 2 else 1.0 / WS
                        gp_done(nc.scalar.activation(qk32[:, u % 2, :], bank[:, :], ACT.Identity, bias=bqk[:, u:u + 1], scale=scale),
                                n, "proj", "qk", u)
                else:
                    for t in range(TILES):
                        drained(act, n, "proj", "vg", t)
                        if t == 0:
                            wait(act, og_ready, n.at(1, -1))
                        nc.scalar.activation(eg[n.par][:, H * t:H * (t + 1), :].rearrange("q h d -> q (h d)"), vg32[:, t % 2, D:2 * D],
                                             ACT.Exp, scale=-1.0).then_inc(eg_ready, 1)

            def outp(n, part):
                if part == "t":
                    bank = full(act, n, "outp", "t", 0)
                    feat_used_by_proj(act, n)
                    gp_done(nc.scalar.copy(featT[:, 0, :, :].rearrange("f c t -> f (c t)"), bank[:, :].bitcast(F16)), n, "outp", "t", 0)
                elif part == "y":
                    act.wait_ge(y_ready, n.at(4, 4))
                    wait(act, scattered, n.at(128))
                    nc.scalar.copy(y16[:, :, 0:D], y32[:, :, :]).then_inc(yh_ready, 1)

            def rout(n, part):
                if part == "t":
                    bank = full(act, n, "rout", "t", 1)
                    full(act, n, "outp", "w", 1)
                    gp_done(nc.scalar.copy(featT[:, 1, :, :].rearrange("f c t -> f (c t)"), bank[:, :].bitcast(F16)), n, "rout", "t", 1)
                elif part[0] == "h":
                    for k in range(2):
                        ht = 2 * int(part[1]) + k
                        bank = full(act, n, "rout", part, k)
                        wait(act, hid_lo, n.at(HT, ht - 1))
                        gp_done(nc.scalar.activation(hid32[:, ht % 2, :], bank[:, :], ACT.Relu, bias=br1[:, ht:ht + 1], scale=1.0 / WS),
                                n, "rout", part, k)
                elif part == "c":
                    act.wait_ge(diff_ready, n.at(1, 1))
                    nc.scalar.activation(rexp[:, :], rdiff[:, :], ACT.Exp).then_inc(rexp_ready, 1)

            def last(n):
                evacuate_values(n, H - 1)

            run_iterations(act, head, dict(proj=proj, maxp=lambda n, part: None, outp=outp, rout=rout), last)

        @block.vector
        def _(dve):
            alone = Apart(dve, dve_passed)

            def residual_of_weights(n, h):
                dve.wait_ge(exp_ready, n.at(H, h + 1))
                nc.vector.tensor_tensor(p16[:, h % 2, 1, :], sc[:, h % 2, :], p16[:, h % 2, 0, :], ALU.subtract).then_inc(plo_ready, 1)

            def head(n, h):
                p, e = h // 2, h % 2
                for k, js in enumerate(((0,), (1, 3), (2,))):
                    bank, before = st_slot(n, h, k)
                    dve.wait_ge(st_full[bank], before + 1)
                    for j in js:
                        w = N - P * j
                        at = COL[j] % 512
                        last = nc.vector.tensor_tensor(sc[:, h % 2, COL[j]:COL[j] + w], st[bank][:, at:at + w], score_bias[:, e, p, 0:w], ALU.add)
                    last.then_inc(st_drained[bank], 1)
                if h:
                    residual_of_weights(n, h - 1)

            def proj(n, part):
                if part == "x":
                    dve.wait_ge(xh_ready, n.at(1, 1))
                    nc.vector.tensor_tensor(x16[:, 1, :, :], xin[:, :, :], x16[:, 0, :, :], ALU.subtract).then_inc(xl_ready, 1)
                    bank = full(dve, n, "proj", "x", 0)
                    feat_used_before_proj(dve, n)
                    gp_done(nc.vector.tensor_copy(featT[:, 0, :, :].rearrange("f c t -> f (c t)"), bank[:, :].bitcast(F16)), n, "proj", "x", 0)
                elif part == "vg":
                    for t in range(TILES):
                        bank = full(dve, n, "proj", "vg", t)
                        wait(dve, v_split, n.at(4, t - 1))
                        wait(dve, eg_ready, n.at(4, t - 1))
                        gp_done(nc.vector.scalar_tensor_tensor(vg32[:, t % 2, :], bank[:, :], 1.0 / WS, bvg[:, :], ALU.mult, ALU.add),
                                n, "proj", "vg", t)

            def maxp(n, part):
                if part == "t":
                    bank = full(dve, n, "maxp", "t", 0)
                    wait(dve, m_stored, n.at(16))
                    view = bank[0:H, :].bitcast(F16)
                    nc.vector.tensor_copy(m_nearT[:, :], view[:, 0:N]).then_inc(m_copied, 1)
                    dve.wait_ge(m_copied, n.at(1, 1))
                    gp_done(nc.vector.tensor_tensor(mT[:, :].rearrange("h (a r) -> h r a", r=FAR_STEP),
                                                    view[:, N:2 * N].rearrange("h (r a) -> h r a", r=FAR_STEP),
                                                    m_nearT[:, :].rearrange("h (a r) -> h r a", r=FAR_STEP), ALU.min), n, "maxp", "t", 0)
                    return
                for e in range(2):
                    bank = full(dve, n, "maxp", part, e)
                    if part[:4] == "near":
                        gp_done(nc.vector.tensor_reduce(m_near[:, int(part[4]), e, :], bank[:, :].rearrange("q (p w) -> q p w", p=PAIRS),
                                                        AX.X, ALU.max, negate=True), n, "maxp", part, e)
                    else:
                        g2 = 2 * int(part[3])
                        gp_done(nc.vector.tensor_reduce(m_far[:, g2:g2 + 2, e, :], bank[:, :].rearrange("q (g p w) -> q g p w", g=2, p=PAIRS),
                                                        AX.X, ALU.max, negate=True), n, "maxp", part, e)

            def outp(n, part):
                if part == "t":
                    bank = full(dve, n, "outp", "t", 1)
                    feat_used_by_proj(dve, n)
                    gp_done(nc.vector.tensor_copy(featT[:, 1, :, :].rearrange("f c t -> f (c t)"), bank[:, :].bitcast(F16)), n, "outp", "t", 1)
                elif part == "w":
                    wait(dve, y_stored, n.at(16))
                    wait(dve, yh_ready, n.at(1))
                    for u in range(2):
                        bank = full(dve, n, "outp", "w", u)
                        dve.wait_ge(xres_ready, n.at(1, 1))
                        gp_done(nc.vector.scalar_tensor_tensor(y32[:, 2 * u:2 * u + 2, :], bank[:, :].rearrange("q (t d) -> q t d", t=2), 1.0 / WS,
                                                               xres[:, 2 * u:2 * u + 2, :], ALU.mult, ALU.add), n, "outp", "w", u)
                    for u in range(2):
                        drained(dve, n, "outp", "w", u)
                    for t in range(TILES):
                        nc.vector.bn_stats(stats[:, t, :], y32[:, t, :]).then_inc(ln_step, 1)
                    alone.wait_ge(ln_step, n.at(TILES, TILES))
                    for t in range(TILES):
                        nc.vector.bn_aggr(mv[:, t, :], stats[:, t, :]).then_inc(var_ready, 1)
                elif part == "y":
                    dve.wait_ge(rstd_ready, n.at(1, 1))
                    for t in range(TILES):
                        nc.vector.tensor_scalar(y32[:, t, :], y32[:, t, :], mv[:, t, 0:1], rstd[:, t:t + 1],
                                                ALU.subtract, ALU.mult).then_inc(y_ready, 1)
                    dve.wait_ge(yh_ready, n.at(1, 1))
                    nc.vector.tensor_tensor(y16[:, :, D:2 * D], y32[:, :, :], y16[:, :, 0:D], ALU.subtract).then_inc(yl_ready, 1)

            def rout(n, part):
                RS = 13

                def step(k, instruction):
                    instruction.then_inc(r_step, 1)
                    (alone if k == 2 else dve).wait_ge(r_step, n.at(RS, k))

                if part == "t":
                    bank = full(dve, n, "rout", "t", 0)
                    full(dve, n, "outp", "w", 1)
                    gp_done(nc.vector.tensor_copy(featT[:, 0, :, :].rearrange("f c t -> f (c t)"), bank[:, :].bitcast(F16)), n, "rout", "t", 0)
                elif part[0] == "h":
                    for k in range(2):
                        ht = 2 * int(part[1]) + k
                        dve.wait_ge(hid_hi, n.at(HT, ht + 1))
                        nc.vector.tensor_tensor(hid16[:, 1, ht, :], hid32[:, ht % 2, :], hid16[:, 0, ht, :], ALU.subtract).then_inc(hid_lo, 1)
                elif part == "l":
                    bank = full(dve, n, "rout", "l", 0)
                    pairs = bank[:, 0:16 * TILES].rearrange("q (t k e) -> q t k e", t=TILES, k=2)
                    step(1, nc.vector.scalar_tensor_tensor(lg[:, :, :], pairs[:, :, 1, :], 1.0 / WS, br2[:, :, :], ALU.mult, ALU.add))
                    gp_done(nc.vector.scalar_tensor_tensor(lg[:, :, :], pairs[:, :, 0, :], 1.0 / WS, lg[:, :, :], ALU.mult, ALU.add), n, "rout", "l", 0)
                    drained(alone, n, "rout", "l", 0)
                    for t in range(TILES):
                        last = nc.vector.max(top[:, t, :], lg[:, t, :])
                    step(2, last)
                    for t in range(TILES):
                        last = nc.vector.max_index(topi[:, t, :], top[:, t, :], lg[:, t, :])
                    step(3, last)
                    step(4, nc.vector.tensor_copy(topf[:, :, :], topi[:, :, 0:2]))
                    step(5, nc.vector.tensor_tensor(onehot[:, :, :, :], expert_id[:, :].unsqueeze(1).unsqueeze(1).to_broadcast([P, TILES, 2, E]),
                                                    topf[:, :, :].unsqueeze(3).to_broadcast([P, TILES, 2, E]), ALU.is_equal))
                    nc.vector.tensor_tensor(chosen[:, :, :], onehot[:, :, 0, :], onehot[:, :, 1, :], ALU.add).then_inc(chosen_ready, 1)
                    nc.vector.tensor_tensor(rdiff[:, :], top[:, :, 1], top[:, :, 0], ALU.subtract).then_inc(diff_ready, 1)
                else:
                    bank = full(dve, n, "rout", "c", 0)
                    step(6, nc.vector.tensor_tensor(rpos[:, :, :], bank[:, 0:E * TILES].rearrange("q (t e) -> q t e", t=TILES),
                                                    taken[:, :].unsqueeze(1).to_broadcast([P, TILES, E]), ALU.add))
                    gp_done(nc.vector.tensor_tensor(taken[:, :], bank[:, E * TILES:E * (TILES + 1)], taken[:, :], ALU.add), n, "rout", "c", 0)
                    step(7, nc.vector.tensor_scalar(rover[:, :, :], rpos[:, :, :], float(CAP), DROPPED, ALU.is_ge, ALU.mult))
                    step(8, nc.vector.tensor_tensor(rpos[:, :, :], rpos[:, :, :], rover[:, :, :], ALU.add))
                    step(9, nc.vector.tensor_tensor(rpos[:, :, :], rpos[:, :, :], expert_row[:, :, :], ALU.add))
                    step(10, nc.vector.tensor_tensor(rprod[:, :, :, :], onehot[:, :, :, :], rpos[:, :, :].unsqueeze(2).to_broadcast([P, TILES, 2, E]), ALU.mult))
                    step(11, nc.vector.tensor_reduce(rslot[:, :, :], rprod[:, :, :, :], AX.X, ALU.add))
                    wait(dve, scattered, n.at(128))
                    nc.vector.tensor_copy(sidx[:, :, :], rslot[:, :, :]).then_inc(sidx_ready, 1)
                    nc.vector.tensor_scalar(gslot[:, bass.ds(n.at(2 * TILES), 2 * TILES)], rslot[:, :, :].rearrange("q t k -> q (t k)"),
                                            float(SLOTS - 1), None, ALU.min)
                    nc.vector.tensor_scalar(rkeep[:, :, :], rslot[:, :, :], float(SLOTS), None, ALU.is_lt)
                    dve.wait_ge(rexp_ready, n.at(1, 1))
                    step(12, nc.vector.tensor_scalar(rdiff[:, :], rexp[:, :], 1.0, None, ALU.add))
                    step(13, nc.vector.reciprocal(rprob[:, :, 0], rdiff[:, :]))
                    nc.vector.tensor_tensor(rprob[:, :, 1], rexp[:, :], rprob[:, :, 0], ALU.mult).then_inc(rprob_ready, 1)
                    dve.wait_ge(rprob_ready, n.at(1, 1))
                    nc.vector.tensor_tensor(gweight[:, bass.ds(n.at(2 * TILES), 2 * TILES)], rprob[:, :, :].rearrange("q t k -> q (t k)"),
                                            rkeep[:, :, :].rearrange("q t k -> q (t k)"), ALU.mult)

            def last(n):
                residual_of_weights(n, H - 1)
                dve.wait_ge(o_drained, n.at(PAIRS, PAIRS))
                wait(dve, og_lo, n.at(1))
                dve.wait_ge(eg_ready, n.at(TILES, TILES))
                o = ob[:, :, :, :].rearrange("q i h c -> q (i h) c")
                nc.vector.tensor_tensor(og[:, :, :], o[:, :, 0:HD], o[:, :, HD + 1:VW], ALU.add)
                nc.vector.scalar_tensor_tensor(oden[:, :, :], eg[n.par][:, :, :], 1.0, o[:, :, HD:HD + 1].to_broadcast([P, TILES * H, HD]),
                                               ALU.add, ALU.mult).then_inc(og_step, 1)
                dve.wait_ge(og_step, n.at(2, 1))
                nc.vector.reciprocal(oden[:, :, :], oden[:, :, :]).then_inc(og_step, 1)
                dve.wait_ge(og_step, n.at(2, 2))
                nc.vector.tensor_tensor(og[:, :, :], og[:, :, :], oden[:, :, :], ALU.mult).then_inc(og_ready, 1)

            rprob_ready = sem("rprob_ready")
            run_iterations(dve, head, dict(proj=proj, maxp=maxp, outp=outp, rout=rout), last)

        @block.gpsimd
        def _(gpsimd):
            pool = Apart(gpsimd, pool_passed)

            def proj(n, part):
                if part == "qk":
                    wait(pool, qk_stored, n.at(64))
                    for u in range(4):
                        drained(pool, n, "proj", "qk", u)
                        nc.gpsimd.tensor_copy(qk16[:, 0, u, :], qk32[:, u % 2, :]).then_inc(qk_hi, 1)
                        pool.wait_ge(qk_hi, n.at(4, u + 1))
                        nc.gpsimd.tensor_tensor(qk16[:, 1, u, :], qk32[:, u % 2, :], qk16[:, 0, u, :], ALU.subtract).then_inc(qk_split, 1)
                elif part == "vg":
                    wait(pool, pv_done, n.at(H, -H))
                    for t in range(TILES):
                        drained(pool, n, "proj", "vg", t)
                        v = vg32[:, t % 2, 0:D].rearrange("q (h d) -> q h d", h=H)
                        nc.gpsimd.tensor_copy(vs[n.par][:, t, :, 0:HD], v).then_inc(v_hi, 1)
                        pool.wait_ge(v_hi, n.at(4, t + 1))
                        nc.gpsimd.tensor_tensor(vs[n.par][:, t, :, HD + 1:VW], v, vs[n.par][:, t, :, 0:HD], ALU.subtract).then_inc(v_split, 1)

            def outp(n, part):
                if part == "t":
                    pool.wait_ge(xres_loaded, n.at(16, 16))
                    nc.gpsimd.tensor_tensor(xres[:, :, :], xres[:, :, :], g_bo, ALU.add).then_inc(xres_ready, 1)
                elif part == "w":
                    pool.wait_ge(var_ready, n.at(TILES, TILES))
                    nc.gpsimd.tensor_scalar(veps[:, :], mv[:, :, 1], LN_EPS, 0.0, ALU.add, ALU.max).then_inc(veps_ready, 1)
                    pool.wait_ge(veps_ready, n.at(1, 1))
                    nc.gpsimd.tensor_tensor(rstd[:, :], veps[:, :], halfneg[:, :], ALU.pow).then_inc(rstd_ready, 1)

            def rout(n, part):
                if part[0] == "h":
                    for k in range(2):
                        ht = 2 * int(part[1]) + k
                        drained(pool, n, "rout", part, k)
                        nc.gpsimd.tensor_copy(hid16[:, 0, ht, :], hid32[:, ht % 2, :]).then_inc(hid_hi, 1)
                elif part == "c":
                    pool.wait_ge(sidx_ready, n.at(1, 1))
                    pool.wait_ge(yh_ready, n.at(1, 1))
                    pool.wait_ge(yl_ready, n.at(1, 1))
                    for t in range(TILES):
                        for k in range(2):
                            nc.gpsimd.indirect_dma_start(
                                out=disp[:, :], out_offset=bass.IndirectOffsetOnAxis(ap=sidx[:, t, k:k + 1], axis=0),
                                in_=y16[:, t, :], in_offset=None, bounds_check=SLOTS - 1, oob_is_err=False).then_inc(scattered, 16)

            def last(n):
                pool.wait_ge(og_ready, n.at(1, 1))
                if n.i is not None or n.c > 0:
                    full(pool, n.shift(-1), "outp", "t", 1)
                nc.gpsimd.tensor_copy(og16[:, 0, :, :].rearrange("q t d -> q (t d)"), og[:, :, :].rearrange("q a d -> q (a d)")).then_inc(og_hi, 1)
                pool.wait_ge(og_hi, n.at(1, 1))
                nc.gpsimd.tensor_tensor(og16[:, 1, :, :].rearrange("q t d -> q (t d)"), og[:, :, :].rearrange("q a d -> q (a d)"),
                                        og16[:, 0, :, :].rearrange("q t d -> q (t d)"), ALU.subtract).then_inc(og_lo, 1)

            g_bo = bo[:, :].unsqueeze(1).to_broadcast([P, TILES, D])
            run_iterations(gpsimd, lambda n, h: None, dict(proj=proj, maxp=lambda n, part: None, outp=outp, rout=rout), last)
            pool.wait_ge(scattered, 128 * B)


def setup(nc, g, a):
    with ExitStack() as ctx:
        def sem(name):
            return ctx.enter_context(nc.semaphore(name))

        ident, zero_rows = g["ident"], a["y16"]
        bias_vec, near_vec, far_vec, disp, pos_bias = g["bias_vec"], g["near_vec"], g["far_vec"], g["disp"], g["pos_bias"]
        score_bias, near_mask, far_mask = a["score_bias"], a["near_mask"], a["far_mask"]
        stage = score_bias[:, :, :, :].rearrange("p e h n -> p (e h n)")
        tiles = lambda w: w.rearrange("(c p) n -> p c n", p=P)
        scratch = a["og"][:, :, :].rearrange("p a d -> p (a d)")
        pb_t, vec_b = scratch[0:H, 0:NOFF], scratch[0:H, P:P + P + N]
        vec_n, vec_f = a["m_nearT"][:, 0:96], a["m_nearT"][:, 128:192]
        qkv_s = stage[:, 0:1536].rearrange("p (c n) -> p c n", c=CT)
        gate_s = stage[:, 1536:2048].rearrange("p (c n) -> p c n", c=CT)
        out_s = stage[:, 2048:2560].rearrange("p (c n) -> p c n", c=CT)
        r1_s = stage[:, 2560:4608].rearrange("p (c n) -> p c n", c=CT)
        r2_s = stage[:, 4608:4672].rearrange("p (c n) -> p c n", c=HT)
        splits = [(qkv_s[:, :, 0:2 * D], a["wqk"][:, 0, :, :], a["wqk"][:, 1, :, :]),
                  (qkv_s[:, :, 2 * D:3 * D], a["wvg"][:, 0, :, 0:D], a["wvg"][:, 1, :, 0:D]),
                  (gate_s, a["wvg"][:, 0, :, D:2 * D], a["wvg"][:, 1, :, D:2 * D]),
                  (out_s, a["wout"][:, 0, :, :], a["wout"][:, 1, :, :]),
                  (r1_s, a["wr1"][:, 0, :, :], a["wr1"][:, 1, :, :]),
                  (r2_s, a["wr2"][:, :, 0:E], a["wr2"][:, :, E:2 * E])]

        loaded, tables_in, stored = sem("setup_loaded"), sem("setup_tables"), sem("setup_stored")
        zeroed, hi, lo = sem("setup_zeroed"), sem("setup_hi"), sem("setup_lo")
        base, vec_base, vec_done, biased = sem("setup_base"), sem("vec_base"), sem("vec_done"), sem("setup_biased")
        loads = [(qkv_s, tiles(g["Wqkv"])), (gate_s, tiles(g["Wgate"])), (out_s, tiles(g["Wout"])), (r1_s, tiles(g["rw1"])),
                 (r2_s, tiles(g["rw2"])), (pb_t, g["pos_bias"].rearrange("o h -> h o")),
                 (a["bqk"][:, :], g["bqkv"][0:2 * D].rearrange("(u p) -> p u", p=P)),
                 (a["bvg"][:, 0:D], g["bqkv"][2 * D:3 * D].partition_broadcast(P)),
                 (a["bvg"][:, D:2 * D], g["bgate"].partition_broadcast(P)),
                 (a["bo"][:, :], g["bout"].partition_broadcast(P)),
                 (a["br1"][:, :], g["rb1"].rearrange("(u p) -> p u", p=P))] + \
                [(a["br2"][:, t, :], g["rb2"].partition_broadcast(P)) for t in range(TILES)]

        with nc.Block() as block:
            @block.sync
            def _(sp):
                for dst, src in loads:
                    sp.dma_start(dst, src, allow_slow_non_contiguous=True).then_inc(loaded, 16)
                sp.wait_ge(zeroed, 1)
                sp.dma_start(disp.rearrange("(b p t) d -> p b (t d)", p=P, t=TILES),
                             zero_rows[:, :, :].rearrange("p t d -> p (t d)").unsqueeze(1).to_broadcast([P, SLOTS // P // TILES, 2 * TILES * D])).then_inc(stored, 16)
                sp.wait_ge(vec_done, 1)
                for vec, copies, src in ((bias_vec, P, vec_b), (near_vec, 32, vec_n), (far_vec, 32, vec_f)):
                    sp.dma_start(vec, src.unsqueeze(1).to_broadcast([H, copies, vec.shape[2]])).then_inc(stored, 16)
                sp.wait_ge(stored, 64)
                sp.wait_ge(lo, len(splits))
                def window(vec, e, first, rows, width):
                    length = vec.shape[2]
                    return bass.AP(vec.tensor, e * rows * length + first, [[length - 1, rows], [2 * rows * length, PAIRS], [1, width]])

                for e in range(2):
                    sp.dma_start(score_bias[:, e, :, :], window(bias_vec, e, P - 1, P, N)).then_inc(tables_in, 16)
                    for part in range(2):
                        r = STACK * e + 32 * part
                        sp.dma_start(near_mask[r:r + 32, :, :], window(near_vec, e, 31, 32, 64)).then_inc(tables_in, 16)
                    for gg in range(2):
                        sp.dma_start(far_mask[STACK * e:STACK * e + 32, gg, :, :], window(far_vec, e, 31, 32, 32)).then_inc(tables_in, 16)
                sp.wait_ge(tables_in, 160)

            @block.gpsimd
            def _(pool):
                nc.gpsimd.memset(zero_rows[:, :, :], 0.0).then_inc(zeroed, 1)
                for t in (ident, a["sel_first"], a["sel_rest"]):
                    last = nc.gpsimd.memset(t[:, :], 0.0)
                for t in (a["ones_mat"], a["before_mat"]):
                    last = nc.gpsimd.memset(t[:, :], 1.0)
                for i in range(2):
                    last = nc.gpsimd.memset(a["vs"][i][:, :, :, HD:HD + 1], 1.0)
                last.then_inc(base, 1)
                pool.wait_ge(base, 1)
                count = 1
                nc.gpsimd.affine_select(out=ident[:, :], in_=ident[:, :], compare_op=ALU.not_equal, fill=1.0,
                                        base=0, pattern=[[-1, P]], channel_multiplier=1)
                nc.gpsimd.affine_select(out=a["before_mat"][:, :], in_=a["before_mat"][:, :], compare_op=ALU.is_gt, fill=0.0,
                                        base=0, pattern=[[1, P]], channel_multiplier=-1).then_inc(base, 1)
                count += 1
                pool.wait_ge(base, count)
                for e in range(2):
                    r = STACK * e
                    for t, rows, c0, blocks in ((a["sel_rest"], slice(r, r + 32), 0, 4), (a["sel_first"], slice(r, r + 32), 32, 3),
                                                (a["sel_first"], slice(r + 32, r + 64), 0, 1)):
                        v = t[rows, c0:c0 + 32 * blocks].rearrange("r (b q) -> r b q", q=32)
                        nc.gpsimd.affine_select(out=v, in_=v, compare_op=ALU.not_equal, fill=1.0, base=0,
                                                pattern=[[0, blocks], [-1, 32]], channel_multiplier=1).then_inc(base, 1)
                        count += 1
                        pool.wait_ge(base, count)
                for e in range(E):
                    nc.gpsimd.memset(a["expert_id"][:, e:e + 1], float(e))
                    nc.gpsimd.memset(a["expert_row"][:, :, e:e + 1], float(e * CAP))
                nc.gpsimd.memset(a["taken"][:, :], 0.0)
                nc.gpsimd.memset(a["halfneg"][:, :], -0.5)

            @block.scalar
            def _(act):
                act.wait_ge(loaded, 16 * len(loads))
                for src, h, _ in splits:
                    nc.scalar.activation(h, src, ACT.Copy, scale=WS).then_inc(hi, 1)
                nc.scalar.mul(a["bqk"][:, 0:2], a["bqk"][:, 0:2], HD ** -0.5)

            @block.vector
            def _(dve):
                for i in range(2):
                    for e in range(2):
                        nc.vector.memset(a["ks"][i][STACK * e + 32:STACK * (e + 1), :, :], 1.0)
                nc.vector.memset(vec_b, NEG)
                nc.vector.memset(vec_n, NEG16)
                nc.vector.memset(vec_f, NEG16).then_inc(vec_base, 1)
                dve.wait_ge(vec_base, 1)
                dve.wait_ge(loaded, 16 * len(loads))
                nc.vector.tensor_copy(vec_b[:, P - 1:P + NEAR], pb_t[:, 0:NEAR + 1])
                for k, off in enumerate(OFFSETS):
                    if off > NEAR:
                        last = nc.vector.tensor_copy(vec_b[:, P - 1 + off:P + off], pb_t[:, k:k + 1])
                    else:
                        nc.vector.tensor_copy(vec_n[:, 63 - off:64 - off], pb_t[:, k:k + 1])
                    if off % FAR_STEP == 0:
                        z = 31 - off // FAR_STEP
                        last = nc.vector.tensor_copy(vec_f[:, z:z + 1], pb_t[:, k:k + 1])
                last.then_inc(vec_done, 1)
                for k, (src, h, l) in enumerate(splits):
                    dve.wait_ge(hi, k + 1)
                    nc.vector.scalar_tensor_tensor(l, src, WS, h, ALU.mult, ALU.subtract).then_inc(lo, 1)
                dve.wait_ge(tables_in, 160)
                for e in range(2):
                    nc.vector.memset(near_mask[STACK * e + 32:STACK * e + 64, :, 0:32], NEG16)


def experts(nc, g):
    ROWS = 512
    GROUPS = CAP // ROWS
    RT = ROWS // P
    with ExitStack() as ctx:
        def sb(name, shape, dt):
            return ctx.enter_context(nc.sbuf_tensor(name, shape, dt))

        def sem(name):
            return ctx.enter_context(nc.semaphore(name))

        ident, disp, eo = g["ident"], g["disp"], g["eo"]
        w1s, w2s = sb("w1s", [P, CT, FF], FP32), sb("w2s", [P, HT, D], FP32)
        w1 = [sb(f"w1_{i}", [P, 2, CT, FF], F16) for i in range(2)]
        w2 = [sb(f"w2_{i}", [P, 2, HT, D], F16) for i in range(2)]
        b1 = sb("b1", [P, E, HT], FP32)
        b2 = sb("b2", [P, E, D], FP32)
        rows = sb("rows", [P, 2, RT, 2 * D], F16)
        rowsT = sb("rowsT", [P, 2, 2, CT, ROWS], F16)
        h32 = sb("h32", [P, 2, ROWS], FP32)
        h16 = sb("h16", [P, 2, 2, HT, ROWS], F16)
        y = sb("y", [P, 2, RT, D], FP32)
        tr = [ctx.enter_context(nc.psum_tensor(f"tr{i}", [P, 512], FP32)) for i in range(2)]
        up = [ctx.enter_context(nc.psum_tensor(f"up{i}", [P, 512], FP32)) for i in range(4)]
        dn = [ctx.enter_context(nc.psum_tensor(f"dn{i}", [P, 512], FP32)) for i in range(2)]

        act_passed, pool_passed = sem("experts_act_passed"), sem("experts_pool_passed")
        biases_in, w1_in, w2_in = sem("biases_in"), sem("w1_in"), sem("w2_in")
        w1_hi, w1_lo, w2_hi, w2_lo = sem("w1_hi"), sem("w1_lo"), sem("w2_hi"), sem("w2_lo")
        rows_in = [sem(f"rows_in{i}") for i in range(2)]
        tr_full = [sem(f"tr_full{i}") for i in range(2)]
        tr_drained = [sem(f"tr_drained{i}") for i in range(2)]
        up_full, up_drained = sem("up_full"), sem("up_drained")
        h_hi, h_lo = sem("h_hi"), sem("h_lo")
        dn_full, dn_drained = sem("dn_full"), sem("dn_drained")
        y_out = [sem(f"y_out{i}") for i in range(2)]

        def run(eng, step):
            for c in range(2):
                step(Batch(None, c), 0)
                step(Batch(None, c), 1)
            with eng.Fori(1, E // 2 - 1) as i:
                for c in range(2):
                    step(Batch(i, c), 0)
                    step(Batch(i, c), 1)
            for c in range(E - 2, E):
                step(Batch(None, c), 0)
                step(Batch(None, c), 1)

        def nxt(e, gr):
            return (e, 1) if gr == 0 else (e.shift(1), 0)

        def prev(e, gr):
            return (e, 0) if gr == 1 else (e.shift(-1), 1)

        def exists(e):
            return e.i is not None or 0 <= e.c < E

        with nc.Block() as block:
            @block.sync
            def _(sp):
                def load_w1(e):
                    wait(sp, w1_lo, e.at(1))
                    sp.dma_start(w1s[:, :, :], g["ew1"].rearrange("e (c p) n -> p (e c) n", p=P)[:, bass.ds(e.at(CT), CT), :]).then_inc(w1_in, 16)

                def load_w2(e):
                    wait(sp, w2_lo, e.at(1))
                    sp.dma_start(w2s[:, :, :], g["ew2"].rearrange("e (c p) n -> p (e c) n", p=P)[:, bass.ds(e.at(HT), HT), :]).then_inc(w2_in, 16)

                def load_rows(e, gr):
                    wait(sp, tr_full[1], e.at(2, gr - 1))
                    sp.dma_start(rows[:, gr, :, :], disp[bass.ds(e.at(CAP, gr * ROWS), ROWS), :].rearrange("(t p) d -> p t d", p=P)).then_inc(rows_in[gr], 16)

                def store(e, gr):
                    sp.wait_ge(dn_drained, e.at(4, 2 * gr + 2))
                    sp.dma_start(eo[bass.ds(e.at(CAP, gr * ROWS), ROWS), :].rearrange("(t p) d -> p t d", p=P), y[:, gr, :, :]).then_inc(y_out[gr], 16)

                load_w1(Batch(None, 0))
                load_rows(Batch(None, 0), 0)
                load_w2(Batch(None, 0))
                sp.dma_start(b1[:, :, :], g["eb1"].rearrange("e (h p) -> p e h", p=P), allow_slow_non_contiguous=True).then_inc(biases_in, 16)
                sp.dma_start(b2[:, :, :].rearrange("p e d -> p (e d)"), g["eb2"].rearrange("e d -> (e d)").partition_broadcast(P)).then_inc(biases_in, 16)
                load_rows(Batch(None, 0), 1)

                def step(e, gr):
                    if exists(e.shift(1)):
                        (load_w1 if gr == 0 else load_w2)(e.shift(1))
                        load_rows(e.shift(1), gr)
                    if exists(prev(e, gr)[0]):
                        store(*prev(e, gr))

                run(sp, step)
                store(Batch(None, E - 1), 1)
                for i in range(2):
                    sp.wait_ge(y_out[i], 16 * E)

            @block.tensor
            def _(pe):
                def transposes(e, gr):
                    pe.wait_ge(rows_in[gr], e.at(16, 16))
                    for i in range(2):
                        wait(pe, tr_drained[i], e.at(2, gr))
                        view = tr[i][:, :].bitcast(F16)
                        for c in range(CT):
                            for t in range(RT):
                                last = nc.tensor.transpose(view[:, c * ROWS + t * P:c * ROWS + (t + 1) * P],
                                                           rows[:, gr, t, D * i + P * c:D * i + P * (c + 1)], ident[:, :])
                        last.then_inc(tr_full[i], 1)

                terms = ((0, 0), (0, 1), (1, 0))

                def up_product(e, gr):
                    for i in range(2):
                        pe.wait_ge(tr_drained[i], e.at(2, gr + 1))
                    pe.wait_ge(w1_lo, e.at(1, 1))
                    for h in range(HT):
                        wait(pe, up_drained, e.at(16, 8 * gr + h - 3))
                        k = 0
                        for c in range(CT):
                            for a, b in terms:
                                last = nc.tensor.matmul(up[h % 4][:, :], w1[e.par][:, a, c, P * h:P * (h + 1)], rowsT[:, gr, b, c, :],
                                                        start=(k == 0), stop=(k == 5))
                                k += 1
                        last.then_inc(up_full, 1)

                def down_product(e, gr):
                    pe.wait_ge(h_lo, e.at(16, 8 * gr + 8))
                    pe.wait_ge(w2_lo, e.at(1, 1))
                    for u in range(2):
                        wait(pe, dn_drained, e.at(4, 2 * gr + u - 1))
                        for t in (2 * u, 2 * u + 1):
                            k = 0
                            for h in range(HT):
                                for a, b in terms:
                                    last = nc.tensor.matmul(dn[u][:, D * (t % 2):D * (t % 2 + 1)], h16[:, gr, a, h, P * t:P * (t + 1)],
                                                            w2[e.par][:, b, h, :], start=(k == 0), stop=(k == 3 * HT - 1))
                                    k += 1
                        last.then_inc(dn_full, 1)

                transposes(Batch(None, 0), 0)

                def step(e, gr):
                    up_product(e, gr)
                    if exists(nxt(e, gr)[0]):
                        transposes(*nxt(e, gr))
                    if exists(prev(e, gr)[0]):
                        down_product(*prev(e, gr))

                run(pe, step)
                down_product(Batch(None, E - 1), 1)

            def row_evacuation(eng, copy, i, e, gr):
                eng.wait_ge(tr_full[i], e.at(2, gr + 1))
                wait(eng, up_full, e.at(16, 8 * (gr - 1)))
                copy(rowsT[:, gr, i, :, :].rearrange("f c t -> f (c t)"), tr[i][:, :].bitcast(F16)).then_inc(tr_drained[i], 1)

            @block.scalar
            def _(act):
                alone = Apart(act, act_passed)

                def split_w1(e):
                    act.wait_ge(w1_in, e.at(16, 16))
                    wait(act, up_full, e.at(16, -16))
                    nc.scalar.activation(w1[e.par][:, 0, :, :], w1s[:, :, :], ACT.Copy, scale=WS).then_inc(w1_hi, 1)

                def split_w2(e):
                    act.wait_ge(w2_in, e.at(16, 16))
                    wait(act, dn_full, e.at(4, -4))
                    nc.scalar.activation(w2[e.par][:, 0, :, :], w2s[:, :, :], ACT.Copy, scale=WS).then_inc(w2_hi, 1)

                split_w1(Batch(None, 0))
                row_evacuation(act, nc.scalar.copy, 1, Batch(None, 0), 0)
                split_w2(Batch(None, 0))
                act.wait_ge(biases_in, 32)

                def step(e, gr):
                    for h in range(HT):
                        alone.wait_ge(up_full, e.at(16, 8 * gr + h + 1))
                        wait(alone, h_lo, e.at(16, 8 * gr + h - 1))
                        nc.scalar.activation(h32[:, h % 2, :], up[h % 4][:, :], ACT.Relu, bias=g_b1(e, h), scale=1.0 / WS).then_inc(up_drained, 1)
                    if exists(nxt(e, gr)[0]):
                        row_evacuation(act, nc.scalar.copy, 1, *nxt(e, gr))
                    if exists(e.shift(1)):
                        (split_w1 if gr == 0 else split_w2)(e.shift(1))

                def g_b1(e, h):
                    return b1[:, bass.ds(e.at(1), 1), h]

                run(act, step)

            @block.vector
            def _(dve):
                def split_w1(e):
                    dve.wait_ge(w1_hi, e.at(1, 1))
                    nc.vector.scalar_tensor_tensor(w1[e.par][:, 1, :, :], w1s[:, :, :], WS, w1[e.par][:, 0, :, :], ALU.mult, ALU.subtract).then_inc(w1_lo, 1)

                def split_w2(e):
                    dve.wait_ge(w2_hi, e.at(1, 1))
                    nc.vector.scalar_tensor_tensor(w2[e.par][:, 1, :, :], w2s[:, :, :], WS, w2[e.par][:, 0, :, :], ALU.mult, ALU.subtract).then_inc(w2_lo, 1)

                def down_evacuation(e, gr):
                    for u in range(2):
                        dve.wait_ge(dn_full, e.at(4, 2 * gr + u + 1))
                        wait(dve, y_out[gr], e.at(16))
                        nc.vector.scalar_tensor_tensor(y[:, gr, 2 * u:2 * u + 2, :], dn[u][:, :].rearrange("p (t d) -> p t d", t=2), 1.0 / WS,
                                                       b2[:, bass.ds(e.at(1), 1), :].to_broadcast([P, 2, D]), ALU.mult, ALU.add).then_inc(dn_drained, 1)

                split_w1(Batch(None, 0))
                row_evacuation(dve, nc.vector.tensor_copy, 0, Batch(None, 0), 0)
                split_w2(Batch(None, 0))
                dve.wait_ge(biases_in, 32)

                def step(e, gr):
                    for h in range(HT):
                        dve.wait_ge(h_hi, e.at(16, 8 * gr + h + 1))
                        nc.vector.tensor_tensor(h16[:, gr, 1, h, :], h32[:, h % 2, :], h16[:, gr, 0, h, :], ALU.subtract).then_inc(h_lo, 1)
                    if exists(nxt(e, gr)[0]):
                        row_evacuation(dve, nc.vector.tensor_copy, 0, *nxt(e, gr))
                    if exists(e.shift(1)):
                        (split_w1 if gr == 0 else split_w2)(e.shift(1))
                    if exists(prev(e, gr)[0]):
                        down_evacuation(*prev(e, gr))

                run(dve, step)
                down_evacuation(Batch(None, E - 1), 1)

            @block.gpsimd
            def _(gpsimd):
                pool = Apart(gpsimd, pool_passed)

                def step(e, gr):
                    wait(pool, dn_full, e.at(4, 2 * gr - 2))
                    for h in range(HT):
                        pool.wait_ge(up_drained, e.at(16, 8 * gr + h + 1))
                        nc.gpsimd.tensor_copy(h16[:, gr, 0, h, :], h32[:, h % 2, :]).then_inc(h_hi, 1)

                run(gpsimd, step)


def combine(nc, g):
    with ExitStack() as ctx:
        def sb(name, shape, dt):
            return ctx.enter_context(nc.sbuf_tensor(name, shape, dt))

        def sem(name):
            return ctx.enter_context(nc.semaphore(name))

        gslot, gweight, xln, eo = g["gslot"], g["gweight"], g["xln"], g["eo"]
        K2 = 2 * TILES
        idx, wt = sb("idx", [P, 2, K2], U32), sb("wt", [P, 2, K2], FP32)
        res = sb("res", [P, 2, TILES, D], FP32)
        got = sb("got", [P, 2, K2, D], FP32)
        stats, mv = sb("stats2", [P, 2, TILES, 6], FP32), sb("mv2", [P, 2, TILES, 2], FP32)
        veps, halfneg, rstd = sb("veps2", [P, TILES], FP32), sb("halfneg2", [P, TILES], FP32), sb("rstd2", [P, 2, TILES], FP32)
        res_in = [sem(f"res_in{i}") for i in range(2)]
        got_in = [sem(f"got_in{i}") for i in range(2)]
        idx_ready, half_ready = sem("idx_ready"), sem("half_ready")
        dve_passed, pool_passed = sem("combine_dve_passed"), sem("combine_pool_passed")
        wt_ready, added, c_stats, c_var, c_veps, c_rstd, c_done = (sem(s) for s in ("wt_ready", "added", "c_stats", "c_var", "c_veps", "c_rstd", "c_done"))
        stored = [sem(f"stored{i}") for i in range(2)]

        def run(eng, step):
            for c in range(2):
                step(Batch(None, c))
            with eng.Fori(1, B // 2 - 1) as i:
                step(Batch(i, 0))
                step(Batch(i, 1))
            for c in range(B - 2, B):
                step(Batch(None, c))

        def rows_of(t, n):
            return t[bass.ds(n.at(N), N), :].rearrange("(t p) d -> p t d", p=P)

        with nc.Block() as block:
            @block.sync
            def _(sp):
                def step(n):
                    wait(sp, stored[n.par], n.half(16))
                    sp.dma_start(res[:, n.par, :, :], rows_of(xln, n)).then_inc(res_in[n.par], 16)
                    if n.i is not None or n.c >= 1:
                        store(n.shift(-1))

                def store(n):
                    sp.wait_ge(c_done, n.at(TILES, TILES))
                    sp.dma_start(rows_of(g["out_rows"], n), res[:, n.par, :, :]).then_inc(stored[n.par], 16)

                run(sp, step)
                store(Batch(None, B - 1))
                for i in range(2):
                    sp.wait_ge(stored[i], 16 * (B // 2))

            @block.gpsimd
            def _(gpsimd):
                pool = Apart(gpsimd, pool_passed)
                nc.gpsimd.memset(halfneg[:, :], -0.5).then_inc(half_ready, 1)
                pool.wait_ge(half_ready, 1)

                def inverse_deviation(n):
                    wait(pool, c_rstd, n.at(1))
                    pool.wait_ge(c_var, n.at(TILES, TILES))
                    nc.gpsimd.tensor_scalar(veps[:, :], mv[:, n.par, :, 1], LN_EPS, 0.0, ALU.add, ALU.max).then_inc(c_veps, 1)
                    pool.wait_ge(c_veps, n.at(1, 1))
                    nc.gpsimd.tensor_tensor(rstd[:, n.par, :], veps[:, :], halfneg[:, :], ALU.pow).then_inc(c_rstd, 1)

                def step(n):
                    wait(pool, added, n.at(K2, -K2))
                    nc.gpsimd.tensor_copy(idx[:, n.par, :], gslot[:, bass.ds(n.at(K2), K2)]).then_inc(idx_ready, 1)
                    pool.wait_ge(idx_ready, n.at(1, 1))
                    for k in range(K2):
                        nc.gpsimd.indirect_dma_start(out=got[:, n.par, k, :], out_offset=None, in_=eo[:, :],
                                                     in_offset=bass.IndirectOffsetOnAxis(ap=idx[:, n.par, k:k + 1], axis=0)).then_inc(got_in[n.par], 16)
                    if n.i is not None or n.c >= 1:
                        inverse_deviation(n.shift(-1))

                run(gpsimd, step)
                inverse_deviation(Batch(None, B - 1))

            @block.vector
            def _(dve):
                alone = Apart(dve, dve_passed)

                def normalise(n):
                    dve.wait_ge(c_rstd, n.at(1, 1))
                    for t in range(TILES):
                        nc.vector.tensor_scalar(res[:, n.par, t, :], res[:, n.par, t, :], mv[:, n.par, t, 0:1], rstd[:, n.par, t:t + 1],
                                                ALU.subtract, ALU.mult).then_inc(c_done, 1)

                def step(n):
                    nc.vector.tensor_copy(wt[:, n.par, :], gweight[:, bass.ds(n.at(K2), K2)]).then_inc(wt_ready, 1)
                    dve.wait_ge(wt_ready, n.at(1, 1))
                    dve.wait_ge(res_in[n.par], n.half(16, 16))
                    dve.wait_ge(got_in[n.par], n.half(16 * K2, 16 * K2))
                    for k in range(2):
                        for t in range(TILES):
                            if k:
                                dve.wait_ge(added, n.at(K2, t + 1))
                            nc.vector.scalar_tensor_tensor(res[:, n.par, t, :], got[:, n.par, 2 * t + k, :], wt[:, n.par, 2 * t + k:2 * t + k + 1],
                                                           res[:, n.par, t, :], ALU.mult, ALU.add).then_inc(added, 1)
                    for t in range(TILES):
                        dve.wait_ge(added, n.at(K2, TILES + t + 1))
                        nc.vector.bn_stats(stats[:, n.par, t, :], res[:, n.par, t, :]).then_inc(c_stats, 1)
                    alone.wait_ge(c_stats, n.at(TILES, TILES))
                    for t in range(TILES):
                        nc.vector.bn_aggr(mv[:, n.par, t, :], stats[:, n.par, t, :]).then_inc(c_var, 1)
                    if n.i is not None or n.c >= 1:
                        normalise(n.shift(-1))

                run(dve, step)
                normalise(Batch(None, B - 1))


_INS = ["x", "Wqkv", "bqkv", "Wout", "bout", "Wgate", "bgate", "pos_bias"]
_FFN = ["rw1", "rb1", "rw2", "rb2", "ew1", "eb1", "ew2", "eb2"]
_NAMES = [f"L0_attn_{n}" for n in _INS] + [f"L0_ffn_{n}" for n in _FFN]


def kernel(**inputs):
    import numpy as _np
    import concourse.bacc as _bacc
    from concourse import mybir as _mybir
    from concourse.bass_utils import run_bass_kernel_spmd as _run

    nc = _bacc.Bacc("TRN2", target_bir_lowering=False, num_devices=1)
    arrays, args = {}, []
    for name in _NAMES:
        a = _np.ascontiguousarray(inputs[name])
        arrays[f"in_{name}"] = a
        args.append(nc.dram_tensor(f"in_{name}", a.shape, _mybir.dt.from_np(a.dtype), kind="ExternalInput").ap())
    args.append(nc.dram_tensor("out_0", (B, N, D), FP32, kind="ExternalOutput").ap())
    build(nc, *args)
    r = _run(nc, [arrays], core_ids=[0])
    return r.results[0]["out_0"]
```

```python
import concourse.bass as bass
from concourse import mybir
from contextlib import ExitStack


FP32 = mybir.dt.float32
F16 = mybir.dt.float16
U32 = mybir.dt.uint32
I32 = mybir.dt.int32
ALU = mybir.AluOpType
ACT = mybir.ActivationFunctionType
AX = mybir.AxisListType

P = 128
B, N, D, H = 16, 512, 256, 16
HD = D // H
TILES = N // P
CT = D // P
OFFSETS = sorted(set(range(0, 33)) | {48, 64, 96, 128, 192, 256, 384})
NOFF = len(OFFSETS)
NEAR = 32
FAR_STEP = 16
E, CAP, FF = 8, 1024, 1024
HT = FF // P
TOK = B * N
SLOTS = E * CAP
LN_EPS = 1e-5
WS = 64.0
NEG = -1e30
NEG16 = -30000.0
DROPPED = 65536.0
PAIRS = H // 2
STACK = 64
MROW = 3 * HD
KST = MROW + 1
VW = 2 * HD + 1
COL = {0: 0, 1: 512, 3: 896, 2: 1024}
SCW = 1280
GP_BANKS, ST_BANKS = 3, 4

SLOTS_OF = {
    0: [("proj", "x")], 1: [("proj", "qk0"), ("gate", "g0")], 2: [("proj", "qk1"), ("gate", "g1"), ("rank", "l")],
    3: [("proj", "vg0"), ("gate", "g2")], 4: [("proj", "vg1"), ("rank", "c")], 5: [("rank", "s0"), ("rank", "s1")],
    6: [("outp", "t"), ("maxp", "near0"), ("rank", "s2")], 7: [("outp", "w"), ("rank", "s3")],
    8: [("maxp", "near1"), ("maxp", "near2")], 9: [("maxp", "near3"), ("maxp", "far0"), ("outp", "y")],
    10: [("maxp", "far1")], 11: [("maxp", "t"), ("rout", "t")], 12: [("rout", "h0")],
    13: [("rout", "h1"), ("split", "x")], 14: [("rout", "h2")], 15: [("rout", "h3")],
}
AHEAD = {"split": 2, "proj": 1, "maxp": 1, "gate": -1, "outp": -1, "rout": -1, "rank": -2}
LATER = {("act", "proj", "vg0"), ("act", "proj", "vg1"), ("act", "gate", "g2"), ("act", "rank", "l"),
         ("pool", "proj", "vg0"), ("pool", "proj", "vg1"), ("pool", "gate", "g2")}
UNITS = {("proj", "x"): 2, ("proj", "qk0"): 2, ("proj", "qk1"): 2, ("proj", "vg0"): 2, ("proj", "vg1"): 2,
         ("outp", "t"): 2, ("outp", "w"): 2, ("maxp", "near0"): 2, ("maxp", "near1"): 2, ("maxp", "near2"): 2,
         ("maxp", "near3"): 2, ("maxp", "far0"): 2, ("maxp", "far1"): 2, ("maxp", "t"): 1,
         ("rout", "t"): 2, ("rout", "h0"): 2, ("rout", "h1"): 2, ("rout", "h2"): 2, ("rout", "h3"): 2,
         ("rank", "l"): 1, ("rank", "c"): 1}
POOL_HEADS = (9, 10, 11, 12, 13, 14)
FIRST_LOOP, LAST_LOOP = 2, 13


class Apart:

    def __init__(self, eng, passed):
        self.eng, self.passed = eng, passed

    def wait_ge(self, sem, value):
        self.eng.wait_ge(sem, value)
        if not isinstance(value, int):
            self.eng.sem_inc(self.passed, 1)


class Batch:

    def __init__(self, i, c):
        self.i, self.c = i, c

    def at(self, k, plus=0):
        v = k * self.c + plus
        return v if self.i is None else self.i * (2 * k) + v

    def half(self, k, plus=0):
        v = k * (self.c // 2) + plus
        return v if self.i is None else self.i * k + v

    @property
    def par(self):
        return self.c % 2

    def shift(self, d):
        return Batch(self.i, self.c + d)

    def in_range(self):
        return self.i is not None or 0 <= self.c < B


def wait(eng, sem, value):
    if not isinstance(value, int) or value > 0:
        eng.wait_ge(sem, value)


def iterations():
    return range(-2, B + 2)


def gp_table():
    table = {}
    count = [0] * GP_BANKS
    for it in iterations():
        u = 0
        for slot in range(H):
            for stage, part in SLOTS_OF[slot]:
                for k in range(UNITS.get((stage, part), 0)):
                    if 0 <= it + AHEAD[stage] < B:
                        table[it, stage, part, k] = (u % GP_BANKS, count[u % GP_BANKS])
                        count[u % GP_BANKS] += 1
                    u += 1
    return table


GP = gp_table()
GP_PER = (GP[3, "proj", "x", 0][1] - GP[2, "proj", "x", 0][1])
assert sum(UNITS.values()) == GP_PER * GP_BANKS


def gp_slot(n, stage, part, k):
    if n.i is None:
        return GP[n.c - AHEAD[stage], stage, part, k]
    bank, before = GP[FIRST_LOOP, stage, part, k]
    it = n.shift(-AHEAD[stage])
    return bank, it.at(GP_PER, before - FIRST_LOOP * GP_PER)


def run_iterations(eng, name, head, part, tail=None):
    plan = [[] for _ in range(H)]
    for slot in range(H):
        for stage, p in SLOTS_OF[slot]:
            if stage in part:
                at = slot + (0 if name == "pe" else 2 if (name, stage, p) in LATER else 1)
                plan[at % H].append((at // H, stage, p))

    def one(it):
        for k in range(H):
            head(it, k)
            for late, stage, p in plan[k]:
                n = it.shift(AHEAD[stage] - late)
                if n.in_range():
                    part[stage](n, p)
            if tail:
                tail(it, k)

    for c in range(-2, FIRST_LOOP):
        one(Batch(None, c))
    with eng.Fori(FIRST_LOOP // 2, (LAST_LOOP + 1) // 2) as i:
        one(Batch(i, 0))
        one(Batch(i, 1))
    for c in range(LAST_LOOP + 1, B + 2):
        one(Batch(None, c))


def head_at(it, k):
    n = it.shift(k // H)
    return (n, k % H) if n.in_range() else None


def build(nc, x, Wqkv, bqkv, Wout, bout, Wgate, bgate, pos_bias,
          rw1, rb1, rw2, rb2, ew1, eb1, ew2, eb2, out):
    x_rows = x.rearrange("b n d -> (b n) d")
    out_rows = out.rearrange("b n d -> (b n) d")

    def dram(name, shape, dt):
        return nc.dram_tensor(name, shape, dt, kind="Internal").ap()

    bias_vec = dram("bias_vec", (H, P, P + N), FP32)
    near_vec = dram("near_vec", (H, 32, 96), F16)
    far_vec = dram("far_vec", (H, 32, 64), F16)
    qk_dram = [dram(f"qk_dram{i}", (4, D, N), F16) for i in range(2)]
    m_dram = [dram(f"m_dram{i}", (H, N), F16) for i in range(2)]
    xln = dram("xln", (TOK, D), FP32)
    disp = dram("disp", (SLOTS, 2 * D), F16)
    eo = dram("eo", (SLOTS, D), FP32)

    outer = ExitStack()
    with outer:
        def keep(name, shape, dt):
            return outer.enter_context(nc.sbuf_tensor(name, shape, dt))

        ident = keep("ident", [P, P], F16)
        gslot = keep("gslot", [P, TOK // P * 2], U32)
        gweight = keep("gweight", [P, TOK // P * 2], FP32)
        attention(nc, locals())
        experts(nc, locals())
        combine(nc, locals())


def attention(nc, g):
    ctx = ExitStack()
    with ctx:
        def sb(name, shape, dt):
            return ctx.enter_context(nc.sbuf_tensor(name, shape, dt))

        def pb(name, shape, dt):
            return ctx.enter_context(nc.psum_tensor(name, shape, dt))

        def sem(name):
            return ctx.enter_context(nc.semaphore(name))

        ident, gslot, gweight = g["ident"], g["gslot"], g["gweight"]
        xln, disp, qk_dram = g["xln"], g["disp"], g["qk_dram"]
        m_dram = g["m_dram"]
        bias_vec, near_vec, far_vec = g["bias_vec"], g["near_vec"], g["far_vec"]
        pos_bias = g["pos_bias"]

        score_bias = sb("score_bias", [P, 2, PAIRS, N], FP32)
        near_mask = sb("near_mask", [P, PAIRS, 2 * NEAR], F16)
        far_mask = sb("far_mask", [P, 2, PAIRS, 32], F16)
        sel_first = sb("sel_first", [P, P], F16)
        sel_rest = sb("sel_rest", [P, P], F16)
        before_mat = sb("before_mat", [P, P], F16)
        ones_mat = sb("ones_mat", [P, P], F16)
        wqk = sb("wqk", [P, 2, CT, 2 * D], F16)
        wvg = sb("wvg", [P, 2, CT, 2 * D], F16)
        wout = sb("wout", [P, 2, CT, D], F16)
        wr1 = sb("wr1", [P, 2, CT, FF], F16)
        wr2 = sb("wr2", [P, HT, 2 * E], F16)
        bqk = sb("bqk", [P, 4], FP32)
        bvg = sb("bvg", [P, 2 * D], FP32)
        bo = sb("bo", [P, D], FP32)
        br1 = sb("br1", [P, HT], FP32)
        br2 = sb("br2", [P, TILES, E], FP32)
        expert_id = sb("expert_id", [P, E], FP32)
        expert_row = sb("expert_row", [P, TILES, E], FP32)
        taken = sb("taken", [P, E], FP32)

        xin = sb("xin", [P, TILES, D], FP32)
        x16 = sb("x16", [P, 2, TILES, D], F16)
        featT = sb("featT", [P, 2, CT, N], F16)
        qk32 = sb("qk32", [P, 2, N], FP32)
        qk16 = sb("qk16", [P, 2, 4, N], F16)
        qs = [sb(f"qs{i}", [P, PAIRS, N], F16) for i in range(2)]
        ks = [sb(f"ks{i}", [P, PAIRS, N], F16) for i in range(2)]
        vg32 = sb("vg32", [P, 2, 2 * D], FP32)
        vs = [sb(f"vs{i}", [P, TILES, H, VW], F16) for i in range(2)]
        eg = [sb(f"eg{i}", [P, TILES * H, HD], FP32) for i in range(2)]
        m_near = sb("m_near", [P, TILES, 2, PAIRS], F16)
        m_far = sb("m_far", [P, TILES, 2, PAIRS], F16)
        m_nearT = sb("m_nearT", [H, N], F16)
        mT = sb("mT", [H, N], F16)
        sc = sb("sc", [P, 2, SCW], FP32)
        p16 = sb("p16", [P, 2, 2, SCW], F16)
        ob = sb("ob", [P, TILES, H, VW], FP32)
        og = sb("og", [P, TILES * H, HD], FP32)
        og16 = x16
        xres = sb("xres", [P, TILES, D], FP32)
        y32 = sb("y32", [P, TILES, D], FP32)
        stats = sb("stats", [P, TILES, 6], FP32)
        mv = sb("mv", [P, TILES, 2], FP32)
        veps = sb("veps", [P, TILES], FP32)
        halfneg = sb("halfneg", [P, TILES], FP32)
        rstd = sb("rstd", [P, TILES], FP32)
        nmr = sb("nmr", [P, TILES], FP32)
        y16 = sb("y16", [P, TILES, 2 * D], F16)
        hid32 = sb("hid32", [P, 2, N], FP32)
        hid16 = sb("hid16", [P, 2, HT, N], F16)
        oden = sb("oden", [P, TILES * H, HD], FP32)
        lg = sb("lg", [P, TILES, E], FP32)
        top = sb("top", [P, TILES, 8], FP32)
        topi = sb("topi", [P, TILES, 8], U32)
        topf = sb("topf", [P, TILES, 2], FP32)
        onehot = sb("onehot", [P, TILES, 2, E], FP32)
        chosen = sb("chosen", [P, TILES, E], F16)
        rpos = sb("rpos", [P, TILES, E], FP32)
        rover = sb("rover", [P, TILES, E], FP32)
        rprod = sb("rprod", [P, TILES, 2, E], FP32)
        rslot = sb("rslot", [P, TILES, 2], FP32)
        sidx = sb("sidx", [P, TILES, 2], U32)
        rkeep = sb("rkeep", [P, TILES, 2], FP32)
        rdiff = sb("rdiff", [P, TILES], FP32)
        rexp = sb("rexp", [P, TILES], FP32)
        rprob = sb("rprob", [P, TILES, 2], FP32)

        gp = [pb(f"gp{i}", [P, 512], FP32) for i in range(GP_BANKS)]
        st = [pb(f"st{i}", [P, 512], FP32) for i in range(ST_BANKS)]
        opv = pb("opv", [P, 2, TILES, VW], FP32)

        setup(nc, g, locals())

        sp_passed, dve_passed, pool_passed = sem("sp_passed"), sem("dve_passed"), sem("pool_passed")
        x_loaded, xres_loaded = sem("x_loaded"), sem("xres_loaded")
        xh_ready, xl_ready = sem("xh_ready"), sem("xl_ready")
        gp_full = [sem(f"gp_full{i}") for i in range(GP_BANKS)]
        gp_drained = [sem(f"gp_drained{i}") for i in range(GP_BANKS)]
        st_full = [sem(f"st_full{i}") for i in range(ST_BANKS)]
        st_drained = [sem(f"st_drained{i}") for i in range(ST_BANKS)]
        qk_split, qk_stored = sem("qk_split"), sem("qk_stored")
        stack_in = [sem(f"stack_in{i}") for i in range(2)]
        v_hi, v_split, eg_ready = sem("v_hi"), sem("v_split"), sem("eg_ready")
        m_copied, m_stored = sem("m_copied"), sem("m_stored")
        m_in = [sem(f"m_in{i}") for i in range(2)]
        exp_ready, pv_done = sem("exp_ready"), sem("pv_done")
        plo_dve, plo_pool = sem("plo_dve"), sem("plo_pool")
        o_drained = sem("o_drained")
        og_step, og_ready, og_hi, og_lo = sem("og_step"), sem("og_ready"), sem("og_hi"), sem("og_lo")
        nmr_ready = sem("nmr_ready")
        xres_ready, ln_step, var_ready, veps_ready = sem("xres_ready"), sem("ln_step"), sem("var_ready"), sem("veps_ready")
        rstd_ready, y_ready = sem("rstd_ready"), sem("y_ready")
        yh_ready, yl_ready, y_stored = sem("yh_ready"), sem("yl_ready"), sem("y_stored")
        hid_lo = sem("hid_lo")
        r_step, chosen_ready = sem("r_step"), sem("chosen_ready")
        diff_ready, rexp_ready, sidx_ready = sem("diff_ready"), sem("rexp_ready"), sem("sidx_ready")
        scattered = sem("scattered")

        def full(eng, n, stage, part, k):
            bank, before = gp_slot(n, stage, part, k)
            eng.wait_ge(gp_full[bank], before + 1)
            return gp[bank]

        def drained(eng, n, stage, part, k):
            bank, before = gp_slot(n, stage, part, k)
            eng.wait_ge(gp_drained[bank], before + 1)

        def gp_done(instruction, n, stage, part, k):
            instruction.then_inc(gp_drained[gp_slot(n, stage, part, k)[0]], 1)

        def feat_used_by_proj(eng, n):
            ahead = n.shift(2)
            full(eng, ahead if ahead.in_range() else Batch(None, B - 1), "proj", "vg1", 1)

        def feat_used_before_proj(eng, n):
            if n.i is not None or n.c >= 3:
                full(eng, n.shift(-3), "rout", "h3", 1)
            elif n.c >= 1:
                full(eng, n.shift(-1), "proj", "vg1", 1)

        def split_done(eng, n, h):
            mine = [g for g in range(H) if (g in POOL_HEADS) == (h in POOL_HEADS)]
            eng.wait_ge(plo_pool if h in POOL_HEADS else plo_dve, n.at(len(mine), mine.index(h) + 1))

        def split_weights(eng, engine, n, h):
            eng.wait_ge(exp_ready, n.at(H, h + 1))
            engine.tensor_tensor(p16[:, h % 2, 1, :], sc[:, h % 2, :], p16[:, h % 2, 0, :],
                                 ALU.subtract).then_inc(plo_pool if h in POOL_HEADS else plo_dve, 1)

        def st_slot(n, h, k):
            u = 3 * h + k
            return u % ST_BANKS, n.at(3 * H // ST_BANKS, u // ST_BANKS)

        block = ctx.enter_context(nc.Block())

        @block.sync
        def _(sync):
            sp = Apart(sync, sp_passed)

            def load_x(n):
                wait(sp, xh_ready, n.at(1))
                wait(sp, xl_ready, n.at(1))
                sync.dma_start(xin[:, :, :], g["x_rows"][bass.ds(n.at(N), N), :].rearrange("(t p) d -> p t d", p=P)).then_inc(x_loaded, 16)

            def head(n, h):
                if not n.in_range():
                    return
                if h == 0 and n.shift(2).in_range() and not (n.i is None and n.c + 2 >= B):
                    load_x(n.shift(2))
                if h == 9:
                    if n.i is not None or n.c > 0:
                        drained(sp, n.shift(-1), "outp", "w", 1)
                    sync.dma_start(xres[:, :, :], g["x_rows"][bass.ds(n.at(N), N), :].rearrange("(t p) d -> p t d", p=P)).then_inc(xres_loaded, 16)

            def proj(n, part):
                if part not in ("qk0", "qk1"):
                    return
                w = int(part[2])
                sp.wait_ge(qk_split, n.at(4, 2 * w + 2))
                if w == 0:
                    wait(sp, stack_in[n.par], n.half(192))
                for i in range(2):
                    sync.dma_start(qk_dram[n.par][2 * w + i].rearrange("(u f) t -> f u t", f=P),
                                   qk16[:, i, 2 * w:2 * w + 2, :]).then_inc(qk_stored, 16)
                if w == 0:
                    return
                sp.wait_ge(qk_stored, n.at(64, 64))
                if n.i is not None or n.c >= 2:
                    bank, before = st_slot(n.shift(-2), H - 1, 2)
                    sp.wait_ge(st_full[bank], before + 1)
                for w, dst, halves in ((0, qs, (0, 1, 0)), (1, ks, (0, 0, 1))):
                    for e in range(2):
                        for t, i in enumerate(halves):
                            src = qk_dram[n.par][2 * w + i].rearrange("(p e d) t -> e d p t", e=2, d=HD)[e]
                            r = STACK * e + HD * t
                            sync.dma_start(dst[n.par][r:r + HD, :, :], src).then_inc(stack_in[n.par], 16)

            def maxp(n, part):
                if part != "t":
                    return
                drained(sp, n, "maxp", "t", 0)
                sync.dma_start(m_dram[n.par], mT[:, :]).then_inc(m_stored, 16)
                sp.wait_ge(m_stored, n.at(16, 16))
                for e in range(2):
                    r = STACK * e + MROW
                    sync.dma_start(qs[n.par][r:r + 1, :, :], m_dram[n.par][PAIRS * e:PAIRS * (e + 1), :].unsqueeze(0)).then_inc(m_in[n.par], 16)

            def outp(n, part):
                if part == "y":
                    sp.wait_ge(y_ready, n.at(4, 4))
                    sync.dma_start(xln[bass.ds(n.at(N), N), :].rearrange("(t p) d -> p t d", p=P), y32[:, :, :]).then_inc(y_stored, 16)

            load_x(Batch(None, 0))
            load_x(Batch(None, 1))
            run_iterations(sync, "sp", head, dict(proj=proj, maxp=maxp, outp=outp))
            sp.wait_ge(y_stored, 16 * B)

        @block.tensor
        def _(pe):
            def unit(n, stage, part, k):
                bank, before = gp_slot(n, stage, part, k)
                wait(pe, gp_drained[bank], before)
                return gp[bank], gp_full[bank]

            def transposes(n, stage, part, k, src):
                bank, is_full = unit(n, stage, part, k)
                view = bank[:, :].bitcast(F16)
                for c in range(CT):
                    for t in range(TILES):
                        last = nc.tensor.transpose(view[:, c * N + t * P:c * N + (t + 1) * P], src(t, c), ident[:, :])
                last.then_inc(is_full, 1)

            def terms(lhs, rhs, dst):
                todo = [(c, a, b) for c in range(CT) for a, b in ((0, 0), (0, 1), (1, 0))]
                for k, (c, a, b) in enumerate(todo):
                    last = nc.tensor.matmul(dst, lhs(a, c), rhs(b, c), start=(k == 0), stop=(k == len(todo) - 1))
                return last

            def scores(n, h):
                p, e = h // 2, h % 2
                rows = slice(STACK * e, STACK * e + KST)
                if h == 0:
                    pe.wait_ge(m_in[n.par], n.half(32, 32))
                for k, js in enumerate(((0,), (1, 3), (2,))):
                    bank, before = st_slot(n, h, k)
                    wait(pe, st_drained[bank], before)
                    for j in js:
                        w = N - P * j
                        at = COL[j] % 512
                        last = nc.tensor.matmul(st[bank][:, at:at + w], ks[n.par][rows, p, P * j:P * (j + 1)],
                                                qs[n.par][rows, p, P * j:N], start=True, stop=True)
                    last.then_inc(st_full[bank], 1)

            def values(n, h):
                split_done(pe, n, h)
                if h == 0:
                    pe.wait_ge(v_split, n.at(TILES, TILES))
                if h % 2 == 0:
                    wait(pe, o_drained, n.at(PAIRS, h // 2))
                for i in range(TILES):
                    for j in range(i + 1):
                        c = COL[j] + P * (i - j)
                        nc.tensor.matmul(opv[:, h % 2, i, :], p16[:, h % 2, 0, c:c + P], vs[n.par][:, j, h, :],
                                         start=(j == 0), stop=False, skip_group_check=True)
                        last = nc.tensor.matmul(opv[:, h % 2, i, 0:HD + 1], p16[:, h % 2, 1, c:c + P], vs[n.par][:, j, h, 0:HD + 1],
                                                start=False, stop=(j == i), skip_group_check=True)
                last.then_inc(pv_done, 1)

            def head(it, k):
                for what, at in ((values, k - 2), (scores, k + 1)):
                    if head_at(it, at):
                        what(*head_at(it, at))

            def proj(n, part):
                if part == "x":
                    pe.wait_ge(xh_ready, n.at(1, 1))
                    transposes(n, "proj", "x", 0, lambda t, c: x16[:, 0, t, P * c:P * (c + 1)])
                    pe.wait_ge(xl_ready, n.at(1, 1))
                    transposes(n, "proj", "x", 1, lambda t, c: x16[:, 1, t, P * c:P * (c + 1)])
                elif part[:2] == "qk":
                    if part == "qk0":
                        drained(pe, n, "proj", "x", 0)
                        drained(pe, n, "proj", "x", 1)
                    for u in range(2 * int(part[2]), 2 * int(part[2]) + 2):
                        bank, is_full = unit(n, "proj", part, u % 2)
                        terms(lambda a, c: wqk[:, a, c, P * u:P * (u + 1)], lambda b, c: featT[:, b, c, :],
                              bank[:, :]).then_inc(is_full, 1)
                else:
                    for t in range(2 * int(part[2]), 2 * int(part[2]) + 2):
                        bank, is_full = unit(n, "proj", part, t % 2)
                        last = terms(lambda a, c: featT[:, a, c, P * t:P * (t + 1)], lambda b, c: wvg[:, b, c, :], bank[:, :])
                        last.then_inc(is_full, 1)

            def maxp(n, part):
                if part == "t":
                    bank, is_full = unit(n, "maxp", "t", 0)
                    drained(pe, n, "maxp", "far1", 1)
                    view = bank[0:H, :].bitcast(F16)
                    for k, src in enumerate((m_near, m_far)):
                        for i in range(TILES):
                            last = nc.tensor.transpose(view[:, k * N + i * P:k * N + (i + 1) * P],
                                                       src[:, i, :, :].rearrange("q e p -> q (e p)"), ident[:, :])
                    last.then_inc(is_full, 1)
                    return
                if part == "near0":
                    pe.wait_ge(stack_in[n.par], n.half(192, 192))
                for e in range(2):
                    bank, is_full = unit(n, "maxp", part, e)
                    r0 = STACK * e
                    q, k = qs[n.par], ks[n.par]
                    if part[:4] == "near":
                        i = int(part[4])
                        rows = slice(r0, r0 + (2 if i == 0 else 1) * 32)
                        sel = sel_first if i == 0 else sel_rest
                        nc.tensor.matmul(bank[:, :], sel[rows, :], near_mask[rows, :, :].rearrange("r p w -> r (p w)"),
                                         start=True, stop=False, skip_group_check=True)
                        for b in range(4):
                            lo = P * i + 32 * b
                            first = 32 if lo == 0 else 0
                            for p in range(PAIRS):
                                last = nc.tensor.matmul(bank[32 * b:32 * b + 32, 64 * p + first:64 * p + 64],
                                                        q[r0:r0 + HD, p, lo:lo + 32], k[r0:r0 + HD, p, lo - 32 + first:lo + 32],
                                                        start=False, stop=(b == 3 and p == PAIRS - 1), skip_group_check=True)
                    else:
                        nc.tensor.matmul(bank[:, :], sel_rest[r0:r0 + 32, :], far_mask[r0:r0 + 32, :, :, :].rearrange("r g p w -> r (g p w)"),
                                         start=True, stop=False, skip_group_check=True)
                        for gg in range(2):
                            for r4 in range(4):
                                r = 4 * (2 * int(part[3]) + gg) + r4
                                for p in range(PAIRS):
                                    c = 256 * gg + 32 * p
                                    last = nc.tensor.matmul(bank[32 * r4:32 * r4 + 32, c:c + 32],
                                                            q[r0:r0 + HD, p, r:N:FAR_STEP], k[r0:r0 + HD, p, r:N:FAR_STEP],
                                                            start=False, stop=(gg == 1 and r4 == 3 and p == PAIRS - 1), skip_group_check=True)
                    last.then_inc(is_full, 1)

            def outp(n, part):
                if part == "t":
                    pe.wait_ge(og_hi, n.at(1, 1))
                    transposes(n, "outp", "t", 0, lambda t, c: og16[:, 0, t, P * c:P * (c + 1)])
                    pe.wait_ge(og_lo, n.at(1, 1))
                    transposes(n, "outp", "t", 1, lambda t, c: og16[:, 1, t, P * c:P * (c + 1)])
                elif part == "w":
                    drained(pe, n, "outp", "t", 0)
                    drained(pe, n, "outp", "t", 1)
                    for u in range(2):
                        bank, is_full = unit(n, "outp", "w", u)
                        for t in (2 * u, 2 * u + 1):
                            last = terms(lambda a, c: featT[:, a, c, P * t:P * (t + 1)], lambda b, c: wout[:, b, c, :],
                                         bank[:, D * (t % 2):D * (t % 2 + 1)])
                        last.then_inc(is_full, 1)

            def rout(n, part):
                if part == "t":
                    pe.wait_ge(yh_ready, n.at(1, 1))
                    transposes(n, "rout", "t", 0, lambda t, c: y16[:, t, P * c:P * (c + 1)])
                    pe.wait_ge(yl_ready, n.at(1, 1))
                    transposes(n, "rout", "t", 1, lambda t, c: y16[:, t, D + P * c:D + P * (c + 1)])
                else:
                    if part == "h0":
                        drained(pe, n, "rout", "t", 0)
                        drained(pe, n, "rout", "t", 1)
                    for k in range(2):
                        ht = 2 * int(part[1]) + k
                        bank, is_full = unit(n, "rout", part, k)
                        terms(lambda a, c: wr1[:, a, c, P * ht:P * (ht + 1)], lambda b, c: featT[:, b, c, :],
                              bank[:, :]).then_inc(is_full, 1)

            def rank(n, part):
                if part == "l":
                    bank, is_full = unit(n, "rank", "l", 0)
                    pe.wait_ge(hid_lo, n.at(HT, HT))
                    for t in range(TILES):
                        for ht in range(HT):
                            nc.tensor.matmul(bank[:, 16 * t:16 * t + 16], hid16[:, 0, ht, P * t:P * (t + 1)], wr2[:, ht, :],
                                             start=(ht == 0), stop=False, skip_group_check=True)
                            last = nc.tensor.matmul(bank[:, 16 * t:16 * t + E], hid16[:, 1, ht, P * t:P * (t + 1)], wr2[:, ht, 0:E],
                                                    start=False, stop=(ht == HT - 1), skip_group_check=True)
                    last.then_inc(is_full, 1)
                elif part == "c":
                    bank, is_full = unit(n, "rank", "c", 0)
                    pe.wait_ge(chosen_ready, n.at(1, 1))
                    for t in range(TILES):
                        for s in range(t + 1):
                            nc.tensor.matmul(bank[:, E * t:E * (t + 1)], (before_mat if s == t else ones_mat)[:, :], chosen[:, s, :],
                                             start=(s == 0), stop=(s == t))
                    for s in range(TILES):
                        last = nc.tensor.matmul(bank[:, E * TILES:E * (TILES + 1)], ones_mat[:, :], chosen[:, s, :],
                                                start=(s == 0), stop=(s == TILES - 1))
                    last.then_inc(is_full, 1)

            run_iterations(pe, "pe", head, dict(proj=proj, maxp=maxp, outp=outp, rout=rout, rank=rank))

        @block.scalar
        def _(act):
            def evacuate_values(n, h):
                act.wait_ge(pv_done, n.at(H, h + 1))
                if h == 1:
                    wait(act, og_step, n.at(2, -1))
                nc.scalar.copy(ob[:, :, h - 1:h + 1, :].rearrange("q i h c -> q h i c"), opv[:, :, :, :]).then_inc(o_drained, 1)

            def weights(n, h):
                bank, before = st_slot(n, h, 2)
                act.wait_ge(st_drained[bank], before + 1)
                wait(act, pv_done, n.at(H, h - 1))
                nc.scalar.activation(p16[:, h % 2, 0, :], sc[:, h % 2, :], ACT.Exp)
                nc.scalar.activation(sc[:, h % 2, :], sc[:, h % 2, :], ACT.Exp).then_inc(exp_ready, 1)

            def tail(it, k):
                if head_at(it, k):
                    weights(*head_at(it, k))
                if k % 2 == 1 and head_at(it, k - 2):
                    evacuate_values(*head_at(it, k - 2))

            def transposed(n, stage, used):
                for i in range(2):
                    bank = full(act, n, stage, PART_OF_T[stage], i)
                    if i == 0:
                        used()
                    gp_done(nc.scalar.copy(featT[:, i, :, :].rearrange("f c t -> f (c t)"), bank[:, :].bitcast(F16)), n, stage, PART_OF_T[stage], i)

            PART_OF_T = {"proj": "x", "outp": "t", "rout": "t"}

            def split(n, part):
                act.wait_ge(x_loaded, n.at(16, 16))
                nc.scalar.copy(x16[:, 0, :, :], xin[:, :, :]).then_inc(xh_ready, 1)

            def proj(n, part):
                if part == "x":
                    transposed(n, "proj", lambda: feat_used_before_proj(act, n))
                elif part[:2] == "qk":
                    for u in range(2 * int(part[2]), 2 * int(part[2]) + 2):
                        bank = full(act, n, "proj", part, u % 2)
                        wait(act, qk_split, n.at(4, u - 1))
                        if u == 0:
                            wait(act, qk_stored, n.at(64))
                        scale = HD ** -0.5 / WS if u < 2 else 1.0 / WS
                        nc.scalar.activation(qk16[:, 0, u, :], bank[:, :], ACT.Identity, bias=bqk[:, u:u + 1], scale=scale)
                        gp_done(nc.scalar.activation(qk32[:, u % 2, :], bank[:, :], ACT.Identity, bias=bqk[:, u:u + 1], scale=scale),
                                n, "proj", part, u % 2)
                else:
                    for t in range(2 * int(part[2]), 2 * int(part[2]) + 2):
                        drained(act, n, "proj", part, t % 2)
                        if t == 0:
                            wait(act, og_ready, n.at(1, -1))
                        nc.scalar.activation(eg[n.par][:, H * t:H * (t + 1), :].rearrange("q h d -> q (h d)"), vg32[:, t % 2, D:2 * D],
                                             ACT.Exp, scale=-1.0).then_inc(eg_ready, 1)

            def gate(n, part):
                if part == "g2":
                    act.wait_ge(og_ready, n.at(1, 1))
                    nc.scalar.copy(og16[:, 0, :, :].rearrange("q t d -> q (t d)"), og[:, :, :].rearrange("q a d -> q (a d)")).then_inc(og_hi, 1)

            def outp(n, part):
                if part == "t":
                    transposed(n, "outp", lambda: feat_used_by_proj(act, n))
                elif part == "y":
                    act.wait_ge(nmr_ready, n.at(1, 1))
                    wait(act, scattered, n.at(128))
                    for t in range(TILES):
                        nc.scalar.activation(y32[:, t, :], y32[:, t, :], ACT.Identity, bias=nmr[:, t:t + 1], scale=rstd[:, t:t + 1]).then_inc(y_ready, 1)
                    act.wait_ge(y_ready, n.at(4, 4))
                    nc.scalar.copy(y16[:, :, 0:D], y32[:, :, :]).then_inc(yh_ready, 1)

            def rout(n, part):
                if part == "t":
                    transposed(n, "rout", lambda: full(act, n, "outp", "w", 1))
                else:
                    for k in range(2):
                        ht = 2 * int(part[1]) + k
                        bank = full(act, n, "rout", part, k)
                        wait(act, hid_lo, n.at(HT, ht - 1))
                        if ht == 0 and (n.i is not None or n.c > 0):
                            full(act, n.shift(-1), "rank", "l", 0)
                        nc.scalar.activation(hid16[:, 0, ht, :], bank[:, :], ACT.Relu, bias=br1[:, ht:ht + 1], scale=1.0 / WS)
                        gp_done(nc.scalar.activation(hid32[:, ht % 2, :], bank[:, :], ACT.Relu, bias=br1[:, ht:ht + 1], scale=1.0 / WS),
                                n, "rout", part, k)

            def rank(n, part):
                if part == "l":
                    act.wait_ge(diff_ready, n.at(1, 1))
                    nc.scalar.activation(rexp[:, :], rdiff[:, :], ACT.Exp).then_inc(rexp_ready, 1)

            run_iterations(act, "act", lambda it, k: None, dict(split=split, proj=proj, gate=gate, outp=outp, rout=rout, rank=rank), tail)

        @block.vector
        def _(dve):
            alone = Apart(dve, dve_passed)

            def biases(n, h):
                p, e = h // 2, h % 2
                if head_at(n, h - 2):
                    split_done(dve, *head_at(n, h - 2))
                for k, js in enumerate(((0,), (1, 3), (2,))):
                    bank, before = st_slot(n, h, k)
                    dve.wait_ge(st_full[bank], before + 1)
                    for j in js:
                        w = N - P * j
                        at = COL[j] % 512
                        last = nc.vector.tensor_tensor(sc[:, h % 2, COL[j]:COL[j] + w], st[bank][:, at:at + w], score_bias[:, e, p, 0:w], ALU.add)
                    last.then_inc(st_drained[bank], 1)

            def head(it, k):
                if head_at(it, k):
                    biases(*head_at(it, k))
                if head_at(it, k - 1) and (k - 1) % H not in POOL_HEADS:
                    split_weights(dve, nc.vector, *head_at(it, k - 1))

            def split(n, part):
                dve.wait_ge(xh_ready, n.at(1, 1))
                nc.vector.tensor_tensor(x16[:, 1, :, :], xin[:, :, :], x16[:, 0, :, :], ALU.subtract).then_inc(xl_ready, 1)

            def proj(n, part):
                if part[:2] == "vg":
                    for t in range(2 * int(part[2]), 2 * int(part[2]) + 2):
                        bank = full(dve, n, "proj", part, t % 2)
                        wait(dve, v_split, n.at(4, t - 1))
                        wait(dve, eg_ready, n.at(4, t - 1))
                        gp_done(nc.vector.scalar_tensor_tensor(vg32[:, t % 2, :], bank[:, :], 1.0 / WS, bvg[:, :], ALU.mult, ALU.add),
                                n, "proj", part, t % 2)

            def gate(n, part):
                o = ob[:, :, :, :].rearrange("q i h c -> q (i h) c")
                if part == "g0":
                    dve.wait_ge(o_drained, n.at(PAIRS, PAIRS))
                    wait(dve, og_lo, n.at(1))
                    dve.wait_ge(eg_ready, n.at(TILES, TILES))
                    nc.vector.tensor_tensor(og[:, :, :], o[:, :, 0:HD], o[:, :, HD + 1:VW], ALU.add)
                    nc.vector.scalar_tensor_tensor(oden[:, :, :], eg[n.par][:, :, :], 1.0, o[:, :, HD:HD + 1].to_broadcast([P, TILES * H, HD]),
                                                   ALU.add, ALU.mult).then_inc(og_step, 1)
                elif part == "g1":
                    dve.wait_ge(og_step, n.at(2, 1))
                    nc.vector.reciprocal(oden[:, :, :], oden[:, :, :]).then_inc(og_step, 1)
                else:
                    dve.wait_ge(og_step, n.at(2, 2))
                    nc.vector.tensor_tensor(og[:, :, :], og[:, :, :], oden[:, :, :], ALU.mult).then_inc(og_ready, 1)

            def maxp(n, part):
                if part == "t":
                    bank = full(dve, n, "maxp", "t", 0)
                    wait(dve, m_stored, n.at(16))
                    view = bank[0:H, :].bitcast(F16)
                    nc.vector.tensor_copy(m_nearT[:, :], view[:, 0:N]).then_inc(m_copied, 1)
                    dve.wait_ge(m_copied, n.at(1, 1))
                    gp_done(nc.vector.tensor_tensor(mT[:, :].rearrange("h (a r) -> h r a", r=FAR_STEP),
                                                    view[:, N:2 * N].rearrange("h (r a) -> h r a", r=FAR_STEP),
                                                    m_nearT[:, :].rearrange("h (a r) -> h r a", r=FAR_STEP), ALU.min), n, "maxp", "t", 0)
                    return
                for e in range(2):
                    bank = full(dve, n, "maxp", part, e)
                    if part[:4] == "near":
                        gp_done(nc.vector.tensor_reduce(m_near[:, int(part[4]), e, :], bank[:, :].rearrange("q (p w) -> q p w", p=PAIRS),
                                                        AX.X, ALU.max, negate=True), n, "maxp", part, e)
                    else:
                        g2 = 2 * int(part[3])
                        gp_done(nc.vector.tensor_reduce(m_far[:, g2:g2 + 2, e, :], bank[:, :].rearrange("q (g p w) -> q g p w", g=2, p=PAIRS),
                                                        AX.X, ALU.max, negate=True), n, "maxp", part, e)

            def outp(n, part):
                if part == "w":
                    wait(dve, y_stored, n.at(16))
                    wait(dve, yh_ready, n.at(1))
                    for u in range(2):
                        bank = full(dve, n, "outp", "w", u)
                        dve.wait_ge(xres_ready, n.at(1, 1))
                        gp_done(nc.vector.scalar_tensor_tensor(y32[:, 2 * u:2 * u + 2, :], bank[:, :].rearrange("q (t d) -> q t d", t=2), 1.0 / WS,
                                                               xres[:, 2 * u:2 * u + 2, :], ALU.mult, ALU.add), n, "outp", "w", u)
                    for u in range(2):
                        drained(dve, n, "outp", "w", u)
                    for t in range(TILES):
                        nc.vector.bn_stats(stats[:, t, :], y32[:, t, :]).then_inc(ln_step, 1)
                    alone.wait_ge(ln_step, n.at(TILES, TILES))
                    for t in range(TILES):
                        nc.vector.bn_aggr(mv[:, t, :], stats[:, t, :]).then_inc(var_ready, 1)
                elif part == "y":
                    dve.wait_ge(yh_ready, n.at(1, 1))
                    nc.vector.tensor_tensor(y16[:, :, D:2 * D], y32[:, :, :], y16[:, :, 0:D], ALU.subtract).then_inc(yl_ready, 1)

            def rout(n, part):
                if part[0] == "h":
                    for k in range(2):
                        ht = 2 * int(part[1]) + k
                        drained(dve, n, "rout", part, k)
                        nc.vector.tensor_tensor(hid16[:, 1, ht, :], hid32[:, ht % 2, :], hid16[:, 0, ht, :], ALU.subtract).then_inc(hid_lo, 1)

            def rank(n, part):
                RS = 13

                def step(k, instruction):
                    instruction.then_inc(r_step, 1)
                    (alone if k == 2 else dve).wait_ge(r_step, n.at(RS, k))

                if part == "l":
                    bank = full(dve, n, "rank", "l", 0)
                    pairs = bank[:, 0:16 * TILES].rearrange("q (t k e) -> q t k e", t=TILES, k=2)
                    step(1, nc.vector.scalar_tensor_tensor(lg[:, :, :], pairs[:, :, 1, :], 1.0 / WS, br2[:, :, :], ALU.mult, ALU.add))
                    gp_done(nc.vector.scalar_tensor_tensor(lg[:, :, :], pairs[:, :, 0, :], 1.0 / WS, lg[:, :, :], ALU.mult, ALU.add), n, "rank", "l", 0)
                    drained(alone, n, "rank", "l", 0)
                    for t in range(TILES):
                        last = nc.vector.max(top[:, t, :], lg[:, t, :])
                    step(2, last)
                    for t in range(TILES):
                        last = nc.vector.max_index(topi[:, t, :], top[:, t, :], lg[:, t, :])
                    step(3, last)
                    step(4, nc.vector.tensor_copy(topf[:, :, :], topi[:, :, 0:2]))
                    step(5, nc.vector.tensor_tensor(onehot[:, :, :, :], expert_id[:, :].unsqueeze(1).unsqueeze(1).to_broadcast([P, TILES, 2, E]),
                                                    topf[:, :, :].unsqueeze(3).to_broadcast([P, TILES, 2, E]), ALU.is_equal))
                    nc.vector.tensor_tensor(chosen[:, :, :], onehot[:, :, 0, :], onehot[:, :, 1, :], ALU.add).then_inc(chosen_ready, 1)
                    nc.vector.tensor_tensor(rdiff[:, :], top[:, :, 1], top[:, :, 0], ALU.subtract).then_inc(diff_ready, 1)
                elif part == "c":
                    bank = full(dve, n, "rank", "c", 0)
                    step(6, nc.vector.tensor_tensor(rpos[:, :, :], bank[:, 0:E * TILES].rearrange("q (t e) -> q t e", t=TILES),
                                                    taken[:, :].unsqueeze(1).to_broadcast([P, TILES, E]), ALU.add))
                    gp_done(nc.vector.tensor_tensor(taken[:, :], bank[:, E * TILES:E * (TILES + 1)], taken[:, :], ALU.add), n, "rank", "c", 0)
                    step(7, nc.vector.tensor_scalar(rover[:, :, :], rpos[:, :, :], float(CAP), DROPPED, ALU.is_ge, ALU.mult))
                    step(8, nc.vector.tensor_tensor(rpos[:, :, :], rpos[:, :, :], rover[:, :, :], ALU.add))
                    step(9, nc.vector.tensor_tensor(rpos[:, :, :], rpos[:, :, :], expert_row[:, :, :], ALU.add))
                    step(10, nc.vector.tensor_tensor(rprod[:, :, :, :], onehot[:, :, :, :], rpos[:, :, :].unsqueeze(2).to_broadcast([P, TILES, 2, E]), ALU.mult))
                    step(11, nc.vector.tensor_reduce(rslot[:, :, :], rprod[:, :, :, :], AX.X, ALU.add))
                    wait(dve, scattered, n.at(128))
                    nc.vector.tensor_copy(sidx[:, :, :], rslot[:, :, :]).then_inc(sidx_ready, 1)
                    nc.vector.tensor_scalar(gslot[:, bass.ds(n.at(2 * TILES), 2 * TILES)], rslot[:, :, :].rearrange("q t k -> q (t k)"),
                                            float(SLOTS - 1), None, ALU.min)
                    nc.vector.tensor_scalar(rkeep[:, :, :], rslot[:, :, :], float(SLOTS), None, ALU.is_lt)
                    dve.wait_ge(rexp_ready, n.at(1, 1))
                    step(12, nc.vector.tensor_scalar(rdiff[:, :], rexp[:, :], 1.0, None, ALU.add))
                    step(13, nc.vector.reciprocal(rprob[:, :, 0], rdiff[:, :]))
                    nc.vector.tensor_tensor(rprob[:, :, 1], rexp[:, :], rprob[:, :, 0], ALU.mult).then_inc(rprob_ready, 1)
                    dve.wait_ge(rprob_ready, n.at(1, 1))
                    nc.vector.tensor_tensor(gweight[:, bass.ds(n.at(2 * TILES), 2 * TILES)], rprob[:, :, :].rearrange("q t k -> q (t k)"),
                                            rkeep[:, :, :].rearrange("q t k -> q (t k)"), ALU.mult)

            rprob_ready = sem("rprob_ready")
            run_iterations(dve, "dve", head, dict(split=split, proj=proj, maxp=maxp, gate=gate, outp=outp, rout=rout, rank=rank))

        @block.gpsimd
        def _(gpsimd):
            pool = Apart(gpsimd, pool_passed)

            def proj(n, part):
                if part[:2] == "qk":
                    for u in range(2 * int(part[2]), 2 * int(part[2]) + 2):
                        drained(pool, n, "proj", part, u % 2)
                        nc.gpsimd.tensor_tensor(qk16[:, 1, u, :], qk32[:, u % 2, :], qk16[:, 0, u, :], ALU.subtract).then_inc(qk_split, 1)
                elif part[:2] == "vg":
                    wait(pool, pv_done, n.at(H, -H))
                    for t in range(2 * int(part[2]), 2 * int(part[2]) + 2):
                        drained(pool, n, "proj", part, t % 2)
                        v = vg32[:, t % 2, 0:D].rearrange("q (h d) -> q h d", h=H)
                        nc.gpsimd.tensor_copy(vs[n.par][:, t, :, 0:HD], v).then_inc(v_hi, 1)
                        pool.wait_ge(v_hi, n.at(4, t + 1))
                        nc.gpsimd.tensor_tensor(vs[n.par][:, t, :, HD + 1:VW], v, vs[n.par][:, t, :, 0:HD], ALU.subtract).then_inc(v_split, 1)

            def outp(n, part):
                if part == "t":
                    pool.wait_ge(xres_loaded, n.at(16, 16))
                    nc.gpsimd.tensor_tensor(xres[:, :, :], xres[:, :, :], g_bo, ALU.add).then_inc(xres_ready, 1)
                elif part == "w":
                    pool.wait_ge(var_ready, n.at(TILES, TILES))
                    nc.gpsimd.tensor_scalar(veps[:, :], mv[:, :, 1], LN_EPS, 0.0, ALU.add, ALU.max)
                    nc.gpsimd.tensor_scalar(nmr[:, :], mv[:, :, 0], -1.0, 0.0, ALU.mult, ALU.add).then_inc(veps_ready, 1)
                    pool.wait_ge(veps_ready, n.at(1, 1))
                    nc.gpsimd.tensor_tensor(rstd[:, :], veps[:, :], halfneg[:, :], ALU.pow).then_inc(rstd_ready, 1)
                    pool.wait_ge(rstd_ready, n.at(1, 1))
                    nc.gpsimd.tensor_tensor(nmr[:, :], nmr[:, :], rstd[:, :], ALU.mult).then_inc(nmr_ready, 1)

            def rank(n, part):
                if part[0] == "s":
                    if part == "s0":
                        pool.wait_ge(sidx_ready, n.at(1, 1))
                        pool.wait_ge(yh_ready, n.at(1, 1))
                        pool.wait_ge(yl_ready, n.at(1, 1))
                    t = int(part[1])
                    for k in range(2):
                        nc.gpsimd.indirect_dma_start(
                            out=disp[:, :], out_offset=bass.IndirectOffsetOnAxis(ap=sidx[:, t, k:k + 1], axis=0),
                            in_=y16[:, t, :], in_offset=None, bounds_check=SLOTS - 1, oob_is_err=False).then_inc(scattered, 16)

            def gate(n, part):
                if part == "g2":
                    pool.wait_ge(og_hi, n.at(1, 1))
                    nc.gpsimd.tensor_tensor(og16[:, 1, :, :].rearrange("q t d -> q (t d)"), og[:, :, :].rearrange("q a d -> q (a d)"),
                                            og16[:, 0, :, :].rearrange("q t d -> q (t d)"), ALU.subtract).then_inc(og_lo, 1)

            def head(it, k):
                if head_at(it, k - 1) and (k - 1) % H in POOL_HEADS:
                    split_weights(pool, nc.gpsimd, *head_at(it, k - 1))

            g_bo = bo[:, :].unsqueeze(1).to_broadcast([P, TILES, D])
            run_iterations(gpsimd, "pool", head, dict(proj=proj, gate=gate, outp=outp, rank=rank))
            pool.wait_ge(scattered, 128 * B)


def setup(nc, g, a):
    with ExitStack() as ctx:
        def sem(name):
            return ctx.enter_context(nc.semaphore(name))

        ident, zero_rows = g["ident"], a["y16"]
        bias_vec, near_vec, far_vec, disp, pos_bias = g["bias_vec"], g["near_vec"], g["far_vec"], g["disp"], g["pos_bias"]
        score_bias, near_mask, far_mask = a["score_bias"], a["near_mask"], a["far_mask"]
        stage = score_bias[:, :, :, :].rearrange("p e h n -> p (e h n)")
        tiles = lambda w: w.rearrange("(c p) n -> p c n", p=P)
        scratch = a["og"][:, :, :].rearrange("p a d -> p (a d)")
        pb_t, vec_b = scratch[0:H, 0:NOFF], scratch[0:H, P:P + P + N]
        vec_n, vec_f = a["m_nearT"][:, 0:96], a["m_nearT"][:, 128:192]
        qkv_s = stage[:, 0:1536].rearrange("p (c n) -> p c n", c=CT)
        gate_s = stage[:, 1536:2048].rearrange("p (c n) -> p c n", c=CT)
        out_s = stage[:, 2048:2560].rearrange("p (c n) -> p c n", c=CT)
        r1_s = stage[:, 2560:4608].rearrange("p (c n) -> p c n", c=CT)
        r2_s = stage[:, 4608:4672].rearrange("p (c n) -> p c n", c=HT)
        splits = [(qkv_s[:, :, 0:2 * D], a["wqk"][:, 0, :, :], a["wqk"][:, 1, :, :]),
                  (qkv_s[:, :, 2 * D:3 * D], a["wvg"][:, 0, :, 0:D], a["wvg"][:, 1, :, 0:D]),
                  (gate_s, a["wvg"][:, 0, :, D:2 * D], a["wvg"][:, 1, :, D:2 * D]),
                  (out_s, a["wout"][:, 0, :, :], a["wout"][:, 1, :, :]),
                  (r1_s, a["wr1"][:, 0, :, :], a["wr1"][:, 1, :, :]),
                  (r2_s, a["wr2"][:, :, 0:E], a["wr2"][:, :, E:2 * E])]

        loaded, tables_in, stored = sem("setup_loaded"), sem("setup_tables"), sem("setup_stored")
        zeroed, hi, lo = sem("setup_zeroed"), sem("setup_hi"), sem("setup_lo")
        base, vec_base, vec_done, biased = sem("setup_base"), sem("vec_base"), sem("vec_done"), sem("setup_biased")
        loads = [(qkv_s, tiles(g["Wqkv"])), (gate_s, tiles(g["Wgate"])), (out_s, tiles(g["Wout"])), (r1_s, tiles(g["rw1"])),
                 (r2_s, tiles(g["rw2"])), (pb_t, g["pos_bias"].rearrange("o h -> h o")),
                 (a["bqk"][:, :], g["bqkv"][0:2 * D].rearrange("(u p) -> p u", p=P)),
                 (a["bvg"][:, 0:D], g["bqkv"][2 * D:3 * D].partition_broadcast(P)),
                 (a["bvg"][:, D:2 * D], g["bgate"].partition_broadcast(P)),
                 (a["bo"][:, :], g["bout"].partition_broadcast(P)),
                 (a["br1"][:, :], g["rb1"].rearrange("(u p) -> p u", p=P))] + \
                [(a["br2"][:, t, :], g["rb2"].partition_broadcast(P)) for t in range(TILES)]

        with nc.Block() as block:
            @block.sync
            def _(sp):
                for dst, src in loads:
                    sp.dma_start(dst, src, allow_slow_non_contiguous=True).then_inc(loaded, 16)
                sp.wait_ge(zeroed, 1)
                sp.dma_start(disp.rearrange("(b p t) d -> p b (t d)", p=P, t=TILES),
                             zero_rows[:, :, :].rearrange("p t d -> p (t d)").unsqueeze(1).to_broadcast([P, SLOTS // P // TILES, 2 * TILES * D])).then_inc(stored, 16)
                sp.wait_ge(vec_done, 1)
                for vec, copies, src in ((bias_vec, P, vec_b), (near_vec, 32, vec_n), (far_vec, 32, vec_f)):
                    sp.dma_start(vec, src.unsqueeze(1).to_broadcast([H, copies, vec.shape[2]])).then_inc(stored, 16)
                sp.wait_ge(stored, 64)
                sp.wait_ge(lo, len(splits))
                def window(vec, e, first, rows, width):
                    length = vec.shape[2]
                    return bass.AP(vec.tensor, e * rows * length + first, [[length - 1, rows], [2 * rows * length, PAIRS], [1, width]])

                for e in range(2):
                    sp.dma_start(score_bias[:, e, :, :], window(bias_vec, e, P - 1, P, N)).then_inc(tables_in, 16)
                    for part in range(2):
                        r = STACK * e + 32 * part
                        sp.dma_start(near_mask[r:r + 32, :, :], window(near_vec, e, 31, 32, 64)).then_inc(tables_in, 16)
                    for gg in range(2):
                        sp.dma_start(far_mask[STACK * e:STACK * e + 32, gg, :, :], window(far_vec, e, 31, 32, 32)).then_inc(tables_in, 16)
                sp.wait_ge(tables_in, 160)

            @block.gpsimd
            def _(pool):
                nc.gpsimd.memset(zero_rows[:, :, :], 0.0).then_inc(zeroed, 1)
                for t in (ident, a["sel_first"], a["sel_rest"]):
                    last = nc.gpsimd.memset(t[:, :], 0.0)
                for t in (a["ones_mat"], a["before_mat"]):
                    last = nc.gpsimd.memset(t[:, :], 1.0)
                for i in range(2):
                    last = nc.gpsimd.memset(a["vs"][i][:, :, :, HD:HD + 1], 1.0)
                last.then_inc(base, 1)
                pool.wait_ge(base, 1)
                count = 1
                nc.gpsimd.affine_select(out=ident[:, :], in_=ident[:, :], compare_op=ALU.not_equal, fill=1.0,
                                        base=0, pattern=[[-1, P]], channel_multiplier=1)
                nc.gpsimd.affine_select(out=a["before_mat"][:, :], in_=a["before_mat"][:, :], compare_op=ALU.is_gt, fill=0.0,
                                        base=0, pattern=[[1, P]], channel_multiplier=-1).then_inc(base, 1)
                count += 1
                pool.wait_ge(base, count)
                for e in range(2):
                    r = STACK * e
                    for t, rows, c0, blocks in ((a["sel_rest"], slice(r, r + 32), 0, 4), (a["sel_first"], slice(r, r + 32), 32, 3),
                                                (a["sel_first"], slice(r + 32, r + 64), 0, 1)):
                        v = t[rows, c0:c0 + 32 * blocks].rearrange("r (b q) -> r b q", q=32)
                        nc.gpsimd.affine_select(out=v, in_=v, compare_op=ALU.not_equal, fill=1.0, base=0,
                                                pattern=[[0, blocks], [-1, 32]], channel_multiplier=1).then_inc(base, 1)
                        count += 1
                        pool.wait_ge(base, count)
                for e in range(E):
                    nc.gpsimd.memset(a["expert_id"][:, e:e + 1], float(e))
                    nc.gpsimd.memset(a["expert_row"][:, :, e:e + 1], float(e * CAP))
                nc.gpsimd.memset(a["taken"][:, :], 0.0)
                nc.gpsimd.memset(a["halfneg"][:, :], -0.5)

            @block.scalar
            def _(act):
                act.wait_ge(loaded, 16 * len(loads))
                for src, h, _ in splits:
                    nc.scalar.activation(h, src, ACT.Copy, scale=WS).then_inc(hi, 1)
                nc.scalar.mul(a["bqk"][:, 0:2], a["bqk"][:, 0:2], HD ** -0.5)

            @block.vector
            def _(dve):
                for i in range(2):
                    for e in range(2):
                        nc.vector.memset(a["ks"][i][STACK * e + 32:STACK * (e + 1), :, :], 1.0)
                nc.vector.memset(vec_b, NEG)
                nc.vector.memset(vec_n, NEG16)
                nc.vector.memset(vec_f, NEG16).then_inc(vec_base, 1)
                dve.wait_ge(vec_base, 1)
                dve.wait_ge(loaded, 16 * len(loads))
                nc.vector.tensor_copy(vec_b[:, P - 1:P + NEAR], pb_t[:, 0:NEAR + 1])
                for k, off in enumerate(OFFSETS):
                    if off > NEAR:
                        last = nc.vector.tensor_copy(vec_b[:, P - 1 + off:P + off], pb_t[:, k:k + 1])
                    else:
                        nc.vector.tensor_copy(vec_n[:, 63 - off:64 - off], pb_t[:, k:k + 1])
                    if off % FAR_STEP == 0:
                        z = 31 - off // FAR_STEP
                        last = nc.vector.tensor_copy(vec_f[:, z:z + 1], pb_t[:, k:k + 1])
                last.then_inc(vec_done, 1)
                for k, (src, h, l) in enumerate(splits):
                    dve.wait_ge(hi, k + 1)
                    nc.vector.scalar_tensor_tensor(l, src, WS, h, ALU.mult, ALU.subtract).then_inc(lo, 1)
                dve.wait_ge(tables_in, 160)
                for e in range(2):
                    nc.vector.memset(near_mask[STACK * e + 32:STACK * e + 64, :, 0:32], NEG16)


def experts(nc, g):
    ROWS = 512
    GROUPS = CAP // ROWS
    RT = ROWS // P
    with ExitStack() as ctx:
        def sb(name, shape, dt):
            return ctx.enter_context(nc.sbuf_tensor(name, shape, dt))

        def sem(name):
            return ctx.enter_context(nc.semaphore(name))

        ident, disp, eo = g["ident"], g["disp"], g["eo"]
        w1s, w2s = sb("w1s", [P, CT, FF], FP32), sb("w2s", [P, HT, D], FP32)
        w1 = [sb(f"w1_{i}", [P, 2, CT, FF], F16) for i in range(2)]
        w2 = [sb(f"w2_{i}", [P, 2, HT, D], F16) for i in range(2)]
        b1 = sb("b1", [P, E, HT], FP32)
        b2 = sb("b2", [P, E, D], FP32)
        rows = sb("rows", [P, 2, RT, 2 * D], F16)
        rowsT = sb("rowsT", [P, 2, 2, CT, ROWS], F16)
        h32 = sb("h32", [P, 2, ROWS], FP32)
        h16 = sb("h16", [P, 2, 2, HT, ROWS], F16)
        y = sb("y", [P, 2, RT, D], FP32)
        tr = [ctx.enter_context(nc.psum_tensor(f"tr{i}", [P, 512], FP32)) for i in range(2)]
        up = [ctx.enter_context(nc.psum_tensor(f"up{i}", [P, 512], FP32)) for i in range(4)]
        dn = [ctx.enter_context(nc.psum_tensor(f"dn{i}", [P, 512], FP32)) for i in range(2)]

        act_passed, pool_passed = sem("experts_act_passed"), sem("experts_pool_passed")
        biases_in, w1_in, w2_in = sem("biases_in"), sem("w1_in"), sem("w2_in")
        w1_hi, w1_lo, w2_hi, w2_lo = sem("w1_hi"), sem("w1_lo"), sem("w2_hi"), sem("w2_lo")
        rows_in = [sem(f"rows_in{i}") for i in range(2)]
        tr_full = [sem(f"tr_full{i}") for i in range(2)]
        tr_drained = [sem(f"tr_drained{i}") for i in range(2)]
        up_full, up_drained = sem("up_full"), sem("up_drained")
        h_hi, h_lo = sem("h_hi"), sem("h_lo")
        dn_full, dn_drained = sem("dn_full"), sem("dn_drained")
        y_out = [sem(f"y_out{i}") for i in range(2)]

        def run(eng, step):
            for c in range(2):
                step(Batch(None, c), 0)
                step(Batch(None, c), 1)
            with eng.Fori(1, E // 2 - 1) as i:
                for c in range(2):
                    step(Batch(i, c), 0)
                    step(Batch(i, c), 1)
            for c in range(E - 2, E):
                step(Batch(None, c), 0)
                step(Batch(None, c), 1)

        def nxt(e, gr):
            return (e, 1) if gr == 0 else (e.shift(1), 0)

        def prev(e, gr):
            return (e, 0) if gr == 1 else (e.shift(-1), 1)

        def exists(e):
            return e.i is not None or 0 <= e.c < E

        with nc.Block() as block:
            @block.sync
            def _(sp):
                def load_w1(e):
                    wait(sp, w1_lo, e.at(1))
                    sp.dma_start(w1s[:, :, :], g["ew1"].rearrange("e (c p) n -> p (e c) n", p=P)[:, bass.ds(e.at(CT), CT), :]).then_inc(w1_in, 16)

                def load_w2(e):
                    wait(sp, w2_lo, e.at(1))
                    sp.dma_start(w2s[:, :, :], g["ew2"].rearrange("e (c p) n -> p (e c) n", p=P)[:, bass.ds(e.at(HT), HT), :]).then_inc(w2_in, 16)

                def load_rows(e, gr):
                    wait(sp, tr_full[1], e.at(2, gr - 1))
                    sp.dma_start(rows[:, gr, :, :], disp[bass.ds(e.at(CAP, gr * ROWS), ROWS), :].rearrange("(t p) d -> p t d", p=P)).then_inc(rows_in[gr], 16)

                def store(e, gr):
                    sp.wait_ge(dn_drained, e.at(4, 2 * gr + 2))
                    sp.dma_start(eo[bass.ds(e.at(CAP, gr * ROWS), ROWS), :].rearrange("(t p) d -> p t d", p=P), y[:, gr, :, :]).then_inc(y_out[gr], 16)

                load_w1(Batch(None, 0))
                load_rows(Batch(None, 0), 0)
                load_w2(Batch(None, 0))
                sp.dma_start(b1[:, :, :], g["eb1"].rearrange("e (h p) -> p e h", p=P), allow_slow_non_contiguous=True).then_inc(biases_in, 16)
                sp.dma_start(b2[:, :, :].rearrange("p e d -> p (e d)"), g["eb2"].rearrange("e d -> (e d)").partition_broadcast(P)).then_inc(biases_in, 16)
                load_rows(Batch(None, 0), 1)

                def step(e, gr):
                    if exists(e.shift(1)):
                        (load_w1 if gr == 0 else load_w2)(e.shift(1))
                        load_rows(e.shift(1), gr)
                    if exists(prev(e, gr)[0]):
                        store(*prev(e, gr))

                run(sp, step)
                store(Batch(None, E - 1), 1)
                for i in range(2):
                    sp.wait_ge(y_out[i], 16 * E)

            @block.tensor
            def _(pe):
                def transposes(e, gr):
                    pe.wait_ge(rows_in[gr], e.at(16, 16))
                    for i in range(2):
                        wait(pe, tr_drained[i], e.at(2, gr))
                        view = tr[i][:, :].bitcast(F16)
                        for c in range(CT):
                            for t in range(RT):
                                last = nc.tensor.transpose(view[:, c * ROWS + t * P:c * ROWS + (t + 1) * P],
                                                           rows[:, gr, t, D * i + P * c:D * i + P * (c + 1)], ident[:, :])
                        last.then_inc(tr_full[i], 1)

                terms = ((0, 0), (0, 1), (1, 0))

                def up_product(e, gr):
                    for i in range(2):
                        pe.wait_ge(tr_drained[i], e.at(2, gr + 1))
                    pe.wait_ge(w1_lo, e.at(1, 1))
                    for h in range(HT):
                        wait(pe, up_drained, e.at(16, 8 * gr + h - 3))
                        k = 0
                        for c in range(CT):
                            for a, b in terms:
                                last = nc.tensor.matmul(up[h % 4][:, :], w1[e.par][:, a, c, P * h:P * (h + 1)], rowsT[:, gr, b, c, :],
                                                        start=(k == 0), stop=(k == 5))
                                k += 1
                        last.then_inc(up_full, 1)

                def down_product(e, gr):
                    pe.wait_ge(h_lo, e.at(16, 8 * gr + 8))
                    pe.wait_ge(w2_lo, e.at(1, 1))
                    for u in range(2):
                        wait(pe, dn_drained, e.at(4, 2 * gr + u - 1))
                        for t in (2 * u, 2 * u + 1):
                            k = 0
                            for h in range(HT):
                                for a, b in terms:
                                    last = nc.tensor.matmul(dn[u][:, D * (t % 2):D * (t % 2 + 1)], h16[:, gr, a, h, P * t:P * (t + 1)],
                                                            w2[e.par][:, b, h, :], start=(k == 0), stop=(k == 3 * HT - 1))
                                    k += 1
                        last.then_inc(dn_full, 1)

                transposes(Batch(None, 0), 0)

                def step(e, gr):
                    up_product(e, gr)
                    if exists(nxt(e, gr)[0]):
                        transposes(*nxt(e, gr))
                    if exists(prev(e, gr)[0]):
                        down_product(*prev(e, gr))

                run(pe, step)
                down_product(Batch(None, E - 1), 1)

            def row_evacuation(eng, copy, i, e, gr):
                eng.wait_ge(tr_full[i], e.at(2, gr + 1))
                wait(eng, up_full, e.at(16, 8 * (gr - 1)))
                copy(rowsT[:, gr, i, :, :].rearrange("f c t -> f (c t)"), tr[i][:, :].bitcast(F16)).then_inc(tr_drained[i], 1)

            @block.scalar
            def _(act):
                alone = Apart(act, act_passed)

                def split_w1(e):
                    act.wait_ge(w1_in, e.at(16, 16))
                    wait(act, up_full, e.at(16, -16))
                    nc.scalar.activation(w1[e.par][:, 0, :, :], w1s[:, :, :], ACT.Copy, scale=WS).then_inc(w1_hi, 1)

                def split_w2(e):
                    act.wait_ge(w2_in, e.at(16, 16))
                    wait(act, dn_full, e.at(4, -4))
                    nc.scalar.activation(w2[e.par][:, 0, :, :], w2s[:, :, :], ACT.Copy, scale=WS).then_inc(w2_hi, 1)

                split_w1(Batch(None, 0))
                row_evacuation(act, nc.scalar.copy, 1, Batch(None, 0), 0)
                split_w2(Batch(None, 0))
                act.wait_ge(biases_in, 32)

                def step(e, gr):
                    for h in range(HT):
                        alone.wait_ge(up_full, e.at(16, 8 * gr + h + 1))
                        wait(alone, h_lo, e.at(16, 8 * gr + h - 1))
                        nc.scalar.activation(h32[:, h % 2, :], up[h % 4][:, :], ACT.Relu, bias=g_b1(e, h), scale=1.0 / WS).then_inc(up_drained, 1)
                    if exists(nxt(e, gr)[0]):
                        row_evacuation(act, nc.scalar.copy, 1, *nxt(e, gr))
                    if exists(e.shift(1)):
                        (split_w1 if gr == 0 else split_w2)(e.shift(1))

                def g_b1(e, h):
                    return b1[:, bass.ds(e.at(1), 1), h]

                run(act, step)

            @block.vector
            def _(dve):
                def split_w1(e):
                    dve.wait_ge(w1_hi, e.at(1, 1))
                    nc.vector.scalar_tensor_tensor(w1[e.par][:, 1, :, :], w1s[:, :, :], WS, w1[e.par][:, 0, :, :], ALU.mult, ALU.subtract).then_inc(w1_lo, 1)

                def split_w2(e):
                    dve.wait_ge(w2_hi, e.at(1, 1))
                    nc.vector.scalar_tensor_tensor(w2[e.par][:, 1, :, :], w2s[:, :, :], WS, w2[e.par][:, 0, :, :], ALU.mult, ALU.subtract).then_inc(w2_lo, 1)

                def down_evacuation(e, gr):
                    for u in range(2):
                        dve.wait_ge(dn_full, e.at(4, 2 * gr + u + 1))
                        wait(dve, y_out[gr], e.at(16))
                        nc.vector.scalar_tensor_tensor(y[:, gr, 2 * u:2 * u + 2, :], dn[u][:, :].rearrange("p (t d) -> p t d", t=2), 1.0 / WS,
                                                       b2[:, bass.ds(e.at(1), 1), :].to_broadcast([P, 2, D]), ALU.mult, ALU.add).then_inc(dn_drained, 1)

                split_w1(Batch(None, 0))
                row_evacuation(dve, nc.vector.tensor_copy, 0, Batch(None, 0), 0)
                split_w2(Batch(None, 0))
                dve.wait_ge(biases_in, 32)

                def step(e, gr):
                    for h in range(HT):
                        dve.wait_ge(h_hi, e.at(16, 8 * gr + h + 1))
                        nc.vector.tensor_tensor(h16[:, gr, 1, h, :], h32[:, h % 2, :], h16[:, gr, 0, h, :], ALU.subtract).then_inc(h_lo, 1)
                    if exists(nxt(e, gr)[0]):
                        row_evacuation(dve, nc.vector.tensor_copy, 0, *nxt(e, gr))
                    if exists(e.shift(1)):
                        (split_w1 if gr == 0 else split_w2)(e.shift(1))
                    if exists(prev(e, gr)[0]):
                        down_evacuation(*prev(e, gr))

                run(dve, step)
                down_evacuation(Batch(None, E - 1), 1)

            @block.gpsimd
            def _(gpsimd):
                pool = Apart(gpsimd, pool_passed)

                def step(e, gr):
                    wait(pool, dn_full, e.at(4, 2 * gr - 2))
                    for h in range(HT):
                        pool.wait_ge(up_drained, e.at(16, 8 * gr + h + 1))
                        nc.gpsimd.tensor_copy(h16[:, gr, 0, h, :], h32[:, h % 2, :]).then_inc(h_hi, 1)

                run(gpsimd, step)


def combine(nc, g):
    with ExitStack() as ctx:
        def sb(name, shape, dt):
            return ctx.enter_context(nc.sbuf_tensor(name, shape, dt))

        def sem(name):
            return ctx.enter_context(nc.semaphore(name))

        gslot, gweight, xln, eo = g["gslot"], g["gweight"], g["xln"], g["eo"]
        K2 = 2 * TILES
        idx, wt = sb("idx", [P, 2, K2], U32), sb("wt", [P, 2, K2], FP32)
        res = sb("res", [P, 2, TILES, D], FP32)
        got = sb("got", [P, 2, K2, D], FP32)
        stats, mv = sb("stats2", [P, 2, TILES, 6], FP32), sb("mv2", [P, 2, TILES, 2], FP32)
        veps, halfneg, rstd = sb("veps2", [P, TILES], FP32), sb("halfneg2", [P, TILES], FP32), sb("rstd2", [P, 2, TILES], FP32)
        res_in = [sem(f"res_in{i}") for i in range(2)]
        got_in = [sem(f"got_in{i}") for i in range(2)]
        idx_ready, half_ready = sem("idx_ready"), sem("half_ready")
        dve_passed, pool_passed = sem("combine_dve_passed"), sem("combine_pool_passed")
        wt_ready, added, c_stats, c_var, c_veps, c_rstd, c_done = (sem(s) for s in ("wt_ready", "added", "c_stats", "c_var", "c_veps", "c_rstd", "c_done"))
        stored = [sem(f"stored{i}") for i in range(2)]

        def run(eng, step):
            for c in range(2):
                step(Batch(None, c))
            with eng.Fori(1, B // 2 - 1) as i:
                step(Batch(i, 0))
                step(Batch(i, 1))
            for c in range(B - 2, B):
                step(Batch(None, c))

        def rows_of(t, n):
            return t[bass.ds(n.at(N), N), :].rearrange("(t p) d -> p t d", p=P)

        with nc.Block() as block:
            @block.sync
            def _(sp):
                def step(n):
                    wait(sp, stored[n.par], n.half(16))
                    sp.dma_start(res[:, n.par, :, :], rows_of(xln, n)).then_inc(res_in[n.par], 16)
                    if n.i is not None or n.c >= 1:
                        store(n.shift(-1))

                def store(n):
                    sp.wait_ge(c_done, n.at(TILES, TILES))
                    sp.dma_start(rows_of(g["out_rows"], n), res[:, n.par, :, :]).then_inc(stored[n.par], 16)

                run(sp, step)
                store(Batch(None, B - 1))
                for i in range(2):
                    sp.wait_ge(stored[i], 16 * (B // 2))

            @block.gpsimd
            def _(gpsimd):
                pool = Apart(gpsimd, pool_passed)
                nc.gpsimd.memset(halfneg[:, :], -0.5).then_inc(half_ready, 1)
                pool.wait_ge(half_ready, 1)

                def inverse_deviation(n):
                    wait(pool, c_rstd, n.at(1))
                    pool.wait_ge(c_var, n.at(TILES, TILES))
                    nc.gpsimd.tensor_scalar(veps[:, :], mv[:, n.par, :, 1], LN_EPS, 0.0, ALU.add, ALU.max).then_inc(c_veps, 1)
                    pool.wait_ge(c_veps, n.at(1, 1))
                    nc.gpsimd.tensor_tensor(rstd[:, n.par, :], veps[:, :], halfneg[:, :], ALU.pow).then_inc(c_rstd, 1)

                def step(n):
                    wait(pool, added, n.at(K2, -K2))
                    nc.gpsimd.tensor_copy(idx[:, n.par, :], gslot[:, bass.ds(n.at(K2), K2)]).then_inc(idx_ready, 1)
                    pool.wait_ge(idx_ready, n.at(1, 1))
                    for k in range(K2):
                        nc.gpsimd.indirect_dma_start(out=got[:, n.par, k, :], out_offset=None, in_=eo[:, :],
                                                     in_offset=bass.IndirectOffsetOnAxis(ap=idx[:, n.par, k:k + 1], axis=0)).then_inc(got_in[n.par], 16)
                    if n.i is not None or n.c >= 1:
                        inverse_deviation(n.shift(-1))

                run(gpsimd, step)
                inverse_deviation(Batch(None, B - 1))

            @block.vector
            def _(dve):
                alone = Apart(dve, dve_passed)

                def normalise(n):
                    dve.wait_ge(c_rstd, n.at(1, 1))
                    for t in range(TILES):
                        nc.vector.tensor_scalar(res[:, n.par, t, :], res[:, n.par, t, :], mv[:, n.par, t, 0:1], rstd[:, n.par, t:t + 1],
                                                ALU.subtract, ALU.mult).then_inc(c_done, 1)

                def step(n):
                    nc.vector.tensor_copy(wt[:, n.par, :], gweight[:, bass.ds(n.at(K2), K2)]).then_inc(wt_ready, 1)
                    dve.wait_ge(wt_ready, n.at(1, 1))
                    dve.wait_ge(res_in[n.par], n.half(16, 16))
                    dve.wait_ge(got_in[n.par], n.half(16 * K2, 16 * K2))
                    for k in range(2):
                        for t in range(TILES):
                            if k:
                                dve.wait_ge(added, n.at(K2, t + 1))
                            nc.vector.scalar_tensor_tensor(res[:, n.par, t, :], got[:, n.par, 2 * t + k, :], wt[:, n.par, 2 * t + k:2 * t + k + 1],
                                                           res[:, n.par, t, :], ALU.mult, ALU.add).then_inc(added, 1)
                    for t in range(TILES):
                        dve.wait_ge(added, n.at(K2, TILES + t + 1))
                        nc.vector.bn_stats(stats[:, n.par, t, :], res[:, n.par, t, :]).then_inc(c_stats, 1)
                    alone.wait_ge(c_stats, n.at(TILES, TILES))
                    for t in range(TILES):
                        nc.vector.bn_aggr(mv[:, n.par, t, :], stats[:, n.par, t, :]).then_inc(c_var, 1)
                    if n.i is not None or n.c >= 1:
                        normalise(n.shift(-1))

                run(dve, step)
                normalise(Batch(None, B - 1))


_INS = ["x", "Wqkv", "bqkv", "Wout", "bout", "Wgate", "bgate", "pos_bias"]
_FFN = ["rw1", "rb1", "rw2", "rb2", "ew1", "eb1", "ew2", "eb2"]
_NAMES = [f"L0_attn_{n}" for n in _INS] + [f"L0_ffn_{n}" for n in _FFN]


def kernel(**inputs):
    import numpy as _np
    import concourse.bacc as _bacc
    from concourse import mybir as _mybir
    from concourse.bass_utils import run_bass_kernel_spmd as _run

    nc = _bacc.Bacc("TRN2", target_bir_lowering=False, num_devices=1)
    arrays, args = {}, []
    for name in _NAMES:
        a = _np.ascontiguousarray(inputs[name])
        arrays[f"in_{name}"] = a
        args.append(nc.dram_tensor(f"in_{name}", a.shape, _mybir.dt.from_np(a.dtype), kind="ExternalInput").ap())
    args.append(nc.dram_tensor("out_0", (B, N, D), FP32, kind="ExternalOutput").ap())
    build(nc, *args)
    r = _run(nc, [arrays], core_ids=[0])
    return r.results[0]["out_0"]
```

```python
import concourse.bass as bass
from concourse import mybir
from contextlib import ExitStack


FP32 = mybir.dt.float32
F16 = mybir.dt.float16
U32 = mybir.dt.uint32
I32 = mybir.dt.int32
ALU = mybir.AluOpType
ACT = mybir.ActivationFunctionType
AX = mybir.AxisListType

P = 128
B, N, D, H = 16, 512, 256, 16
HD = D // H
TILES = N // P
CT = D // P
OFFSETS = sorted(set(range(0, 33)) | {48, 64, 96, 128, 192, 256, 384})
NOFF = len(OFFSETS)
NEAR = 32
FAR_STEP = 16
E, CAP, FF = 8, 1024, 1024
HT = FF // P
TOK = B * N
SLOTS = E * CAP
LN_EPS = 1e-5
WS = 64.0
NEG = -1e30
NEG16 = -30000.0
DROPPED = 65536.0
PAIRS = H // 2
STACK = 64
MROW = 3 * HD
KST = MROW + 1
VW = 2 * HD + 1
COL = {0: 0, 1: 512, 3: 896, 2: 1024}
SCW = 1280
GP_BANKS, ST_BANKS = 3, 4
CLEARINGS = 8

SLOTS_OF = {
    0: [("proj", "qk0"), ("gate", "inv1")], 1: [("proj", "qk1"), ("gate", "sum1")], 2: [("proj", "vg0"), ("gate", "inv2")],
    3: [("rank", "l"), ("proj", "vg1"), ("gate", "mul")], 4: [("maxp", "near0")], 5: [("rank", "c"), ("maxp", "near1")],
    6: [("outp", "t"), ("maxp", "near2"), ("rank", "s0"), ("rank", "s1")],
    7: [("rank", "s2"), ("rank", "s3"), ("outp", "w")], 8: [("maxp", "near3")],
    9: [("maxp", "far0"), ("outp", "y")], 10: [("maxp", "far1"), ("maxp", "far2"), ("split", "x")],
    11: [("maxp", "far3"), ("rout", "t")], 12: [("maxp", "t"), ("rout", "h0")],
    13: [("rout", "h1"), ("gate0", "sum0")], 14: [("rout", "h2"), ("gate0", "inv0")],
    15: [("rout", "h3"), ("feat", "x")],
}
AHEAD = {"split": 2, "feat": 2, "proj": 1, "maxp": 1, "gate0": 0, "gate": -1, "outp": -1, "rout": -1, "rank": -2}
LATER = {("act", "proj", "vg0"): 2, ("act", "proj", "vg1"): 2, ("act", "gate", "mul"): 2, ("act", "rank", "l"): 3,
         ("pool", "gate", "mul"): 2,
         ("dve", "rout", "h0"): 2, ("dve", "rout", "h1"): 2, ("dve", "rout", "h2"): 2, ("dve", "rout", "h3"): 2}
UNITS = {("feat", "x"): 2, ("proj", "qk0"): 2, ("proj", "qk1"): 2, ("proj", "vg0"): 2, ("proj", "vg1"): 2,
         ("outp", "t"): 2, ("outp", "w"): 2, ("maxp", "near0"): 2, ("maxp", "near1"): 2, ("maxp", "near2"): 2,
         ("maxp", "near3"): 2, ("maxp", "far0"): 1, ("maxp", "far1"): 1, ("maxp", "far2"): 1, ("maxp", "far3"): 1,
         ("maxp", "t"): 1,
         ("rout", "t"): 2, ("rout", "h0"): 2, ("rout", "h1"): 2, ("rout", "h2"): 2, ("rout", "h3"): 2,
         ("rank", "l"): 1, ("rank", "c"): 1}
POOL_HEADS = (0, 2, 3, 5, 9, 11, 13, 14)
GATED = {"sum0": (0, 12), "inv0": (0, 6), "inv1": (6, 12), "sum1": (12, 16), "inv2": (12, 16)}
GATE_STEPS = len(GATED)
FIRST_LOOP, LAST_LOOP = 2, 13


class Apart:

    def __init__(self, eng, passed):
        self.eng, self.passed = eng, passed

    def wait_ge(self, sem, value):
        self.eng.wait_ge(sem, value)
        if not isinstance(value, int):
            self.eng.sem_inc(self.passed, 1)


class Batch:

    def __init__(self, i, c, width=2):
        self.i, self.c, self.width = i, c, width

    def at(self, k, plus=0):
        v = k * self.c + plus
        return v if self.i is None else self.i * (self.width * k) + v

    def half(self, k, plus=0):
        v = k * (self.c // self.width) + plus
        return v if self.i is None else self.i * k + v

    @property
    def par(self):
        return self.c % self.width

    def shift(self, d):
        return Batch(self.i, self.c + d, self.width)

    def in_range(self):
        return self.i is not None or 0 <= self.c < B


def wait(eng, sem, value):
    if not isinstance(value, int) or value > 0:
        eng.wait_ge(sem, value)


def iterations():
    return range(-2, B + 2)


def gp_table():
    table = {}
    count = [0] * GP_BANKS
    for it in iterations():
        u = 0
        for slot in range(H):
            for stage, part in SLOTS_OF[slot]:
                for k in range(UNITS.get((stage, part), 0)):
                    if 0 <= it + AHEAD[stage] < B:
                        table[it, stage, part, k] = (u % GP_BANKS, count[u % GP_BANKS])
                        count[u % GP_BANKS] += 1
                    u += 1
    return table


GP = gp_table()
GP_PER = (GP[3, "feat", "x", 0][1] - GP[2, "feat", "x", 0][1])
assert sum(UNITS.values()) == GP_PER * GP_BANKS


def gp_slot(n, stage, part, k):
    if n.i is None:
        return GP[n.c - AHEAD[stage], stage, part, k]
    bank, before = GP[FIRST_LOOP, stage, part, k]
    it = n.shift(-AHEAD[stage])
    return bank, it.at(GP_PER, before - FIRST_LOOP * GP_PER)


def run_iterations(eng, name, head, part, tail=None):
    plan = [[] for _ in range(H)]
    for slot in range(H):
        for stage, p in SLOTS_OF[slot]:
            if stage in part:
                at = slot + (0 if name == "pe" else LATER.get((name, stage, p), 1))
                plan[at % H].append((at // H, stage, p))

    def one(it):
        for k in range(H):
            head(it, k)
            for late, stage, p in plan[k]:
                n = it.shift(AHEAD[stage] - late)
                if n.in_range():
                    part[stage](n, p)
            if tail:
                tail(it, k)

    for c in range(-2, FIRST_LOOP):
        one(Batch(None, c))
    with eng.Fori(FIRST_LOOP // 2, (LAST_LOOP + 1) // 2) as i:
        one(Batch(i, 0))
        one(Batch(i, 1))
    for c in range(LAST_LOOP + 1, B + 2):
        one(Batch(None, c))


def head_at(it, k):
    n = it.shift(k // H)
    return (n, k % H) if n.in_range() else None


def build(nc, x, Wqkv, bqkv, Wout, bout, Wgate, bgate, pos_bias,
          rw1, rb1, rw2, rb2, ew1, eb1, ew2, eb2, out):
    x_rows = x.rearrange("b n d -> (b n) d")
    out_rows = out.rearrange("b n d -> (b n) d")

    def dram(name, shape, dt):
        return nc.dram_tensor(name, shape, dt, kind="Internal").ap()

    bias_vec = dram("bias_vec", (H, P, P + N), FP32)
    near_vec = dram("near_vec", (H, 32, 96), F16)
    far_vec = dram("far_vec", (H, 32, 64), F16)
    qk_dram = [dram(f"qk_dram{i}", (4, D, N), F16) for i in range(2)]
    m_dram = [dram(f"m_dram{i}", (H, N), F16) for i in range(2)]
    xln = dram("xln", (TOK, D), FP32)
    disp = dram("disp", (SLOTS, 2 * D), F16)
    eo = dram("eo", (SLOTS, D), FP32)

    outer = ExitStack()
    with outer:
        def keep(name, shape, dt):
            return outer.enter_context(nc.sbuf_tensor(name, shape, dt))

        ident = keep("ident", [P, P], F16)
        gslot = keep("gslot", [P, TOK // P * 2], U32)
        gweight = keep("gweight", [P, TOK // P * 2], FP32)
        attention(nc, locals())
        experts(nc, locals())
        combine(nc, locals())


def attention(nc, g):
    ctx = ExitStack()
    with ctx:
        def sb(name, shape, dt):
            return ctx.enter_context(nc.sbuf_tensor(name, shape, dt))

        def pb(name, shape, dt):
            return ctx.enter_context(nc.psum_tensor(name, shape, dt))

        def sem(name):
            return ctx.enter_context(nc.semaphore(name))

        ident, gslot, gweight = g["ident"], g["gslot"], g["gweight"]
        xln, disp, qk_dram = g["xln"], g["disp"], g["qk_dram"]
        m_dram = g["m_dram"]
        bias_vec, near_vec, far_vec = g["bias_vec"], g["near_vec"], g["far_vec"]
        pos_bias = g["pos_bias"]

        score_bias = sb("score_bias", [P, 2, PAIRS, N], FP32)
        near_mask = sb("near_mask", [P, PAIRS, 2 * NEAR], F16)
        far_mask = sb("far_mask", [P, 2, PAIRS, 32], F16)
        sel_first = sb("sel_first", [P, P], F16)
        sel_rest = sb("sel_rest", [P, P], F16)
        before_mat = sb("before_mat", [P, P], F16)
        ones_mat = sb("ones_mat", [P, P], F16)
        wqk = sb("wqk", [P, 2, CT, 2 * D], F16)
        wvg = sb("wvg", [P, 2, CT, 2 * D], F16)
        wout = sb("wout", [P, 2, CT, D], F16)
        wr1 = sb("wr1", [P, 2, CT, FF], F16)
        wr2 = sb("wr2", [P, HT, 2 * E], F16)
        bqk = sb("bqk", [P, 4], FP32)
        bvg = sb("bvg", [P, 2 * D], FP32)
        bo = sb("bo", [P, D], FP32)
        br1 = sb("br1", [P, HT], FP32)
        br2 = sb("br2", [P, TILES, E], FP32)
        expert_id = sb("expert_id", [P, E], FP32)
        expert_row = sb("expert_row", [P, TILES, E], FP32)
        taken = sb("taken", [P, E], FP32)

        xin = sb("xin", [P, TILES, D], FP32)
        x16 = sb("x16", [P, 2, TILES, D], F16)
        featT = sb("featT", [P, 2, CT, N], F16)
        rows32 = sb("rows32", [P, 4, N], FP32)
        qk16 = sb("qk16", [P, 2, 4, N], F16)
        qs = [sb(f"qs{i}", [P, PAIRS, N], F16) for i in range(2)]
        ks = [sb(f"ks{i}", [P, PAIRS, N], F16) for i in range(2)]
        vg32 = sb("vg32", [P, 2, 2 * D], FP32)
        vs = [sb(f"vs{i}", [P, TILES, H, VW], F16) for i in range(2)]
        eg = [sb(f"eg{i}", [P, TILES * H, HD], FP32) for i in range(2)]
        m_near = sb("m_near", [P, TILES, 2, PAIRS], F16)
        m_far = sb("m_far", [P, TILES, 2, PAIRS], F16)
        m_nearT = sb("m_nearT", [H, N], F16)
        mT = sb("mT", [H, N], F16)
        sc = sb("sc", [P, 2, SCW], FP32)
        p16 = sb("p16", [P, 2, 2, SCW], F16)
        ob = sb("ob", [P, TILES, H, VW], FP32)
        og = sb("og", [P, TILES * H, HD], FP32)
        og16 = x16
        xres = sb("xres", [P, TILES, D], FP32)
        y32 = sb("y32", [P, TILES, D], FP32)
        stats = sb("stats", [P, TILES, 6], FP32)
        mv = sb("mv", [P, TILES, 2], FP32)
        veps = sb("veps", [P, TILES], FP32)
        halfneg = sb("halfneg", [P, TILES], FP32)
        rstd = sb("rstd", [P, TILES], FP32)
        nmr = sb("nmr", [P, TILES], FP32)
        y16 = sb("y16", [P, TILES, 2 * D], F16)
        hid16 = sb("hid16", [P, 2, HT, N], F16)
        oden = sb("oden", [P, TILES * H, HD], FP32)
        lg = sb("lg", [P, TILES, E], FP32)
        top = sb("top", [P, TILES, 8], FP32)
        topi = sb("topi", [P, TILES, 8], U32)
        topf = sb("topf", [P, TILES, 2], FP32)
        onehot = sb("onehot", [P, TILES, 2, E], FP32)
        chosen = sb("chosen", [P, TILES, E], F16)
        rpos = sb("rpos", [P, TILES, E], FP32)
        rover = sb("rover", [P, TILES, E], FP32)
        rprod = sb("rprod", [P, TILES, 2, E], FP32)
        rslot = sb("rslot", [P, TILES, 2], FP32)
        sidx = sb("sidx", [P, TILES, 2], U32)
        rkeep = sb("rkeep", [P, TILES, 2], FP32)
        rdiff = sb("rdiff", [P, TILES], FP32)
        rexp = sb("rexp", [P, TILES], FP32)
        rprob = sb("rprob", [P, TILES, 2], FP32)

        gp = [pb(f"gp{i}", [P, 512], FP32) for i in range(GP_BANKS)]
        st = [pb(f"st{i}", [P, 512], FP32) for i in range(ST_BANKS)]
        opv = pb("opv", [P, 2, TILES, VW], FP32)

        setup(nc, g, locals())

        sp_passed, dve_passed, pool_passed = sem("sp_passed"), sem("dve_passed"), sem("pool_passed")
        x_loaded, xres_loaded = sem("x_loaded"), sem("xres_loaded")
        xh_ready, xl_ready = sem("xh_ready"), sem("xl_ready")
        gp_full = [sem(f"gp_full{i}") for i in range(GP_BANKS)]
        gp_drained = [sem(f"gp_drained{i}") for i in range(GP_BANKS)]
        st_full = [sem(f"st_full{i}") for i in range(ST_BANKS)]
        st_drained = [sem(f"st_drained{i}") for i in range(ST_BANKS)]
        qk_split, qk_stored = sem("qk_split"), sem("qk_stored")
        stack_in = [sem(f"stack_in{i}") for i in range(2)]
        v_hi, v_split, eg_ready = sem("v_hi"), sem("v_split"), sem("eg_ready")
        m_copied, m_stored = sem("m_copied"), sem("m_stored")
        m_in = [sem(f"m_in{i}") for i in range(2)]
        exp_ready, pv_done = sem("exp_ready"), sem("pv_done")
        plo_dve, plo_pool = sem("plo_dve"), sem("plo_pool")
        o_drained = sem("o_drained")
        og_step, og_ready, og_hi, og_lo = sem("og_step"), sem("og_ready"), sem("og_hi"), sem("og_lo")
        nmr_ready = sem("nmr_ready")
        xres_ready, ln_step, var_ready, veps_ready = sem("xres_ready"), sem("ln_step"), sem("var_ready"), sem("veps_ready")
        rstd_ready, y_ready = sem("rstd_ready"), sem("y_ready")
        yh_ready, yl_ready, y_stored = sem("yh_ready"), sem("yl_ready"), sem("y_stored")
        hid_lo = sem("hid_lo")
        r_step, w_step, chosen_ready = sem("r_step"), sem("w_step"), sem("chosen_ready")
        diff_ready, rexp_ready, sidx_ready = sem("diff_ready"), sem("rexp_ready"), sem("sidx_ready")
        scattered, cleared = sem("scattered"), sem("cleared")
        tables_in, mask_ready = sem("tables_in"), sem("mask_ready")

        def full(eng, n, stage, part, k):
            bank, before = gp_slot(n, stage, part, k)
            eng.wait_ge(gp_full[bank], before + 1)
            return gp[bank]

        def drained(eng, n, stage, part, k):
            bank, before = gp_slot(n, stage, part, k)
            eng.wait_ge(gp_drained[bank], before + 1)

        def gp_done(instruction, n, stage, part, k):
            instruction.then_inc(gp_drained[gp_slot(n, stage, part, k)[0]], 1)

        def feat_used_by_proj(eng, n):
            ahead = n.shift(2)
            full(eng, ahead if ahead.in_range() else Batch(None, B - 1), "proj", "vg1", 1)

        def feat_used_before_proj(eng, n):
            if n.i is not None or n.c >= 3:
                full(eng, n.shift(-3), "rout", "h3", 1)
            elif n.c >= 1:
                full(eng, n.shift(-1), "proj", "vg1", 1)

        def split_done(eng, n, h):
            mine = [g for g in range(H) if (g in POOL_HEADS) == (h in POOL_HEADS)]
            eng.wait_ge(plo_pool if h in POOL_HEADS else plo_dve, n.at(len(mine), mine.index(h) + 1))

        def split_weights(eng, engine, n, h):
            eng.wait_ge(exp_ready, n.at(H, h + 1))
            engine.tensor_tensor(p16[:, h % 2, 1, :], sc[:, h % 2, :], p16[:, h % 2, 0, :],
                                 ALU.subtract).then_inc(plo_pool if h in POOL_HEADS else plo_dve, 1)

        def st_slot(n, h, k):
            u = 3 * h + k
            return u % ST_BANKS, n.at(3 * H // ST_BANKS, u // ST_BANKS)

        block = ctx.enter_context(nc.Block())

        @block.sync
        def _(sync):
            sp = Apart(sync, sp_passed)

            def load_x(n):
                wait(sp, xh_ready, n.at(1))
                wait(sp, xl_ready, n.at(1))
                sync.dma_start(xin[:, :, :], g["x_rows"][bass.ds(n.at(N), N), :].rearrange("(t p) d -> p t d", p=P)).then_inc(x_loaded, 16)

            def head(n, h):
                if not n.in_range():
                    return
                if n.i is None and n.c == 0 and 1 <= h <= CLEARINGS:
                    rows = slice((h - 1) * SLOTS // CLEARINGS, h * SLOTS // CLEARINGS)
                    sync.dma_start(disp[rows, :].rearrange("(b p t) d -> p b (t d)", p=P, t=TILES),
                                   y16[:, :, :].rearrange("p t d -> p (t d)").unsqueeze(1).to_broadcast([P, SLOTS // CLEARINGS // P // TILES, 2 * TILES * D])).then_inc(cleared, 16)
                if h == 0 and n.shift(2).in_range() and not (n.i is None and n.c + 2 >= B):
                    load_x(n.shift(2))
                if h == 9:
                    if n.i is not None or n.c > 0:
                        drained(sp, n.shift(-1), "outp", "w", 1)
                    sync.dma_start(xres[:, :, :], g["x_rows"][bass.ds(n.at(N), N), :].rearrange("(t p) d -> p t d", p=P)).then_inc(xres_loaded, 16)

            def proj(n, part):
                if part not in ("qk0", "qk1"):
                    return
                w = int(part[2])
                sp.wait_ge(qk_split, n.at(4, 2 * w + 2))
                if w == 0:
                    wait(sp, stack_in[n.par], n.half(192))
                for i in range(2):
                    sync.dma_start(qk_dram[n.par][2 * w + i].rearrange("(u f) t -> f u t", f=P),
                                   qk16[:, i, 2 * w:2 * w + 2, :]).then_inc(qk_stored, 16)
                if w == 0:
                    return
                sp.wait_ge(qk_stored, n.at(64, 64))
                if n.i is not None or n.c >= 2:
                    bank, before = st_slot(n.shift(-2), H - 1, 2)
                    sp.wait_ge(st_full[bank], before + 1)
                for w, dst, halves in ((0, qs, (0, 1, 0)), (1, ks, (0, 0, 1))):
                    for e in range(2):
                        for t, i in enumerate(halves):
                            src = qk_dram[n.par][2 * w + i].rearrange("(p e d) t -> e d p t", e=2, d=HD)[e]
                            r = STACK * e + HD * t
                            sync.dma_start(dst[n.par][r:r + HD, :, :], src).then_inc(stack_in[n.par], 16)

            def maxp(n, part):
                if part != "t":
                    return
                drained(sp, n, "maxp", "t", 0)
                sync.dma_start(m_dram[n.par], mT[:, :]).then_inc(m_stored, 16)
                sp.wait_ge(m_stored, n.at(16, 16))
                for e in range(2):
                    r = STACK * e + MROW
                    sync.dma_start(qs[n.par][r:r + 1, :, :], m_dram[n.par][PAIRS * e:PAIRS * (e + 1), :].unsqueeze(0)).then_inc(m_in[n.par], 16)

            def outp(n, part):
                if part == "y":
                    sp.wait_ge(y_ready, n.at(4, 4))
                    sync.dma_start(xln[bass.ds(n.at(N), N), :].rearrange("(t p) d -> p t d", p=P), y32[:, :, :]).then_inc(y_stored, 16)

            def window(vec, e, first, rows, width):
                length = vec.shape[2]
                return bass.AP(vec.tensor, e * rows * length + first, [[length - 1, rows], [2 * rows * length, PAIRS], [1, width]])

            def load_tables():
                for e in range(2):
                    for half in range(2):
                        r = STACK * e + 32 * half
                        sync.dma_start(near_mask[r:r + 32, :, :], window(near_vec, e, 31, 32, 64)).then_inc(tables_in, 16)
                    for gg in range(2):
                        sync.dma_start(far_mask[STACK * e:STACK * e + 32, gg, :, :], window(far_vec, e, 31, 32, 32)).then_inc(tables_in, 16)
                for e in range(2):
                    sync.dma_start(score_bias[:, e, :, :], window(bias_vec, e, P - 1, P, N)).then_inc(tables_in, 16)

            load_x(Batch(None, 0))
            load_tables()
            load_x(Batch(None, 1))
            run_iterations(sync, "sp", head, dict(proj=proj, maxp=maxp, outp=outp))
            sp.wait_ge(y_stored, 16 * B)

        @block.tensor
        def _(pe):
            def unit(n, stage, part, k):
                bank, before = gp_slot(n, stage, part, k)
                wait(pe, gp_drained[bank], before)
                return gp[bank], gp_full[bank]

            def transposes(n, stage, part, k, src):
                bank, is_full = unit(n, stage, part, k)
                view = bank[:, :].bitcast(F16)
                for c in range(CT):
                    for t in range(TILES):
                        last = nc.tensor.transpose(view[:, c * N + t * P:c * N + (t + 1) * P], src(t, c), ident[:, :])
                last.then_inc(is_full, 1)

            def terms(lhs, rhs, dst):
                todo = [(c, a, b) for c in range(CT) for a, b in ((0, 0), (0, 1), (1, 0))]
                for k, (c, a, b) in enumerate(todo):
                    last = nc.tensor.matmul(dst, lhs(a, c), rhs(b, c), start=(k == 0), stop=(k == len(todo) - 1))
                return last

            def scores(n, h):
                p, e = h // 2, h % 2
                rows = slice(STACK * e, STACK * e + KST)
                if h == 0:
                    pe.wait_ge(m_in[n.par], n.half(32, 32))
                for k, js in enumerate(((0,), (1, 3), (2,))):
                    bank, before = st_slot(n, h, k)
                    wait(pe, st_drained[bank], before)
                    for j in js:
                        w = N - P * j
                        at = COL[j] % 512
                        last = nc.tensor.matmul(st[bank][:, at:at + w], ks[n.par][rows, p, P * j:P * (j + 1)],
                                                qs[n.par][rows, p, P * j:N], start=True, stop=True)
                    last.then_inc(st_full[bank], 1)

            def values(n, h):
                split_done(pe, n, h)
                if h == 0:
                    pe.wait_ge(v_split, n.at(TILES, TILES))
                if h % 2 == 0:
                    wait(pe, o_drained, n.at(PAIRS, h // 2))
                for i in range(TILES):
                    for j in range(i + 1):
                        c = COL[j] + P * (i - j)
                        nc.tensor.matmul(opv[:, h % 2, i, :], p16[:, h % 2, 0, c:c + P], vs[n.par][:, j, h, :],
                                         start=(j == 0), stop=False, skip_group_check=True)
                        last = nc.tensor.matmul(opv[:, h % 2, i, 0:HD + 1], p16[:, h % 2, 1, c:c + P], vs[n.par][:, j, h, 0:HD + 1],
                                                start=False, stop=(j == i), skip_group_check=True)
                last.then_inc(pv_done, 1)

            def head(it, k):
                for what, at in ((values, k - 2), (scores, k + 1)):
                    if head_at(it, at):
                        what(*head_at(it, at))

            def feat(n, part):
                pe.wait_ge(xh_ready, n.at(1, 1))
                transposes(n, "feat", "x", 0, lambda t, c: x16[:, 0, t, P * c:P * (c + 1)])
                pe.wait_ge(xl_ready, n.at(1, 1))
                transposes(n, "feat", "x", 1, lambda t, c: x16[:, 1, t, P * c:P * (c + 1)])

            def proj(n, part):
                if part[:2] == "qk":
                    if part == "qk0":
                        drained(pe, n, "feat", "x", 0)
                        drained(pe, n, "feat", "x", 1)
                    for u in range(2 * int(part[2]), 2 * int(part[2]) + 2):
                        bank, is_full = unit(n, "proj", part, u % 2)
                        terms(lambda a, c: wqk[:, a, c, P * u:P * (u + 1)], lambda b, c: featT[:, b, c, :],
                              bank[:, :]).then_inc(is_full, 1)
                else:
                    for t in range(2 * int(part[2]), 2 * int(part[2]) + 2):
                        bank, is_full = unit(n, "proj", part, t % 2)
                        last = terms(lambda a, c: featT[:, a, c, P * t:P * (t + 1)], lambda b, c: wvg[:, b, c, :], bank[:, :])
                        last.then_inc(is_full, 1)

            def maxp(n, part):
                if part == "t":
                    bank, is_full = unit(n, "maxp", "t", 0)
                    drained(pe, n, "maxp", "far3", 0)
                    view = bank[0:H, :].bitcast(F16)
                    for k, src in enumerate((m_near, m_far)):
                        for i in range(TILES):
                            last = nc.tensor.transpose(view[:, k * N + i * P:k * N + (i + 1) * P],
                                                       src[:, i, :, :].rearrange("q e p -> q (e p)"), ident[:, :])
                    last.then_inc(is_full, 1)
                    return
                if part == "near0":
                    if n.i is None and n.c == 0:
                        pe.wait_ge(mask_ready, 1)
                    pe.wait_ge(stack_in[n.par], n.half(192, 192))
                for e in (range(2) if part[:4] == "near" else (int(part[3]) % 2,)):
                    bank, is_full = unit(n, "maxp", part, e if part[:4] == "near" else 0)
                    r0 = STACK * e
                    q, k = qs[n.par], ks[n.par]
                    if part[:4] == "near":
                        i = int(part[4])
                        rows = slice(r0, r0 + (2 if i == 0 else 1) * 32)
                        sel = sel_first if i == 0 else sel_rest
                        nc.tensor.matmul(bank[:, :], sel[rows, :], near_mask[rows, :, :].rearrange("r p w -> r (p w)"),
                                         start=True, stop=False, skip_group_check=True)
                        for b in range(4):
                            lo = P * i + 32 * b
                            first = 32 if lo == 0 else 0
                            for p in range(PAIRS):
                                last = nc.tensor.matmul(bank[32 * b:32 * b + 32, 64 * p + first:64 * p + 64],
                                                        q[r0:r0 + HD, p, lo:lo + 32], k[r0:r0 + HD, p, lo - 32 + first:lo + 32],
                                                        start=False, stop=(b == 3 and p == PAIRS - 1), skip_group_check=True)
                    else:
                        nc.tensor.matmul(bank[:, :], sel_rest[r0:r0 + 32, :], far_mask[r0:r0 + 32, :, :, :].rearrange("r g p w -> r (g p w)"),
                                         start=True, stop=False, skip_group_check=True)
                        for gg in range(2):
                            for r4 in range(4):
                                r = 4 * (2 * (int(part[3]) // 2) + gg) + r4
                                for p in range(PAIRS):
                                    c = 256 * gg + 32 * p
                                    last = nc.tensor.matmul(bank[32 * r4:32 * r4 + 32, c:c + 32],
                                                            q[r0:r0 + HD, p, r:N:FAR_STEP], k[r0:r0 + HD, p, r:N:FAR_STEP],
                                                            start=False, stop=(gg == 1 and r4 == 3 and p == PAIRS - 1), skip_group_check=True)
                    last.then_inc(is_full, 1)

            def outp(n, part):
                if part == "t":
                    pe.wait_ge(og_hi, n.at(1, 1))
                    transposes(n, "outp", "t", 0, lambda t, c: og16[:, 0, t, P * c:P * (c + 1)])
                    pe.wait_ge(og_lo, n.at(1, 1))
                    transposes(n, "outp", "t", 1, lambda t, c: og16[:, 1, t, P * c:P * (c + 1)])
                elif part == "w":
                    drained(pe, n, "outp", "t", 0)
                    drained(pe, n, "outp", "t", 1)
                    for u in range(2):
                        bank, is_full = unit(n, "outp", "w", u)
                        for t in (2 * u, 2 * u + 1):
                            last = terms(lambda a, c: featT[:, a, c, P * t:P * (t + 1)], lambda b, c: wout[:, b, c, :],
                                         bank[:, D * (t % 2):D * (t % 2 + 1)])
                        last.then_inc(is_full, 1)

            def rout(n, part):
                if part == "t":
                    pe.wait_ge(yh_ready, n.at(1, 1))
                    transposes(n, "rout", "t", 0, lambda t, c: y16[:, t, P * c:P * (c + 1)])
                    pe.wait_ge(yl_ready, n.at(1, 1))
                    transposes(n, "rout", "t", 1, lambda t, c: y16[:, t, D + P * c:D + P * (c + 1)])
                else:
                    if part == "h0":
                        drained(pe, n, "rout", "t", 0)
                        drained(pe, n, "rout", "t", 1)
                    for k in range(2):
                        ht = 2 * int(part[1]) + k
                        bank, is_full = unit(n, "rout", part, k)
                        terms(lambda a, c: wr1[:, a, c, P * ht:P * (ht + 1)], lambda b, c: featT[:, b, c, :],
                              bank[:, :]).then_inc(is_full, 1)

            def rank(n, part):
                if part == "l":
                    bank, is_full = unit(n, "rank", "l", 0)
                    pe.wait_ge(hid_lo, n.at(HT, HT))
                    for t in range(TILES):
                        for ht in range(HT):
                            nc.tensor.matmul(bank[:, 16 * t:16 * t + 16], hid16[:, 0, ht, P * t:P * (t + 1)], wr2[:, ht, :],
                                             start=(ht == 0), stop=False, skip_group_check=True)
                            last = nc.tensor.matmul(bank[:, 16 * t:16 * t + E], hid16[:, 1, ht, P * t:P * (t + 1)], wr2[:, ht, 0:E],
                                                    start=False, stop=(ht == HT - 1), skip_group_check=True)
                    last.then_inc(is_full, 1)
                elif part == "c":
                    bank, is_full = unit(n, "rank", "c", 0)
                    pe.wait_ge(chosen_ready, n.at(1, 1))
                    for t in range(TILES):
                        for s in range(t + 1):
                            nc.tensor.matmul(bank[:, E * t:E * (t + 1)], (before_mat if s == t else ones_mat)[:, :], chosen[:, s, :],
                                             start=(s == 0), stop=(s == t))
                    for s in range(TILES):
                        last = nc.tensor.matmul(bank[:, E * TILES:E * (TILES + 1)], ones_mat[:, :], chosen[:, s, :],
                                                start=(s == 0), stop=(s == TILES - 1))
                    last.then_inc(is_full, 1)

            run_iterations(pe, "pe", head, dict(feat=feat, proj=proj, maxp=maxp, outp=outp, rout=rout, rank=rank))

        @block.scalar
        def _(act):
            def evacuate_values(n, h):
                act.wait_ge(pv_done, n.at(H, h + 1))
                if h == 1:
                    wait(act, og_step, n.at(GATE_STEPS, -1))
                nc.scalar.copy(ob[:, :, h - 1:h + 1, :].rearrange("q i h c -> q h i c"), opv[:, :, :, :]).then_inc(o_drained, 1)

            def weights(n, h):
                bank, before = st_slot(n, h, 2)
                act.wait_ge(st_drained[bank], before + 1)
                wait(act, pv_done, n.at(H, h - 1))
                nc.scalar.activation(p16[:, h % 2, 0, :], sc[:, h % 2, :], ACT.Exp)
                nc.scalar.activation(sc[:, h % 2, :], sc[:, h % 2, :], ACT.Exp).then_inc(exp_ready, 1)

            def tail(it, k):
                if head_at(it, k):
                    weights(*head_at(it, k))
                if k % 2 == 1 and head_at(it, k - 2):
                    evacuate_values(*head_at(it, k - 2))

            def transposed(n, stage, used):
                for i in range(2):
                    bank = full(act, n, stage, PART_OF_T[stage], i)
                    if i == 0:
                        used()
                    gp_done(nc.scalar.copy(featT[:, i, :, :].rearrange("f c t -> f (c t)"), bank[:, :].bitcast(F16)), n, stage, PART_OF_T[stage], i)

            PART_OF_T = {"feat": "x", "outp": "t", "rout": "t"}

            def split(n, part):
                act.wait_ge(x_loaded, n.at(16, 16))
                nc.scalar.copy(x16[:, 0, :, :], xin[:, :, :]).then_inc(xh_ready, 1)

            def feat(n, part):
                transposed(n, "feat", lambda: feat_used_before_proj(act, n))

            def proj(n, part):
                if part[:2] == "qk":
                    for u in range(2 * int(part[2]), 2 * int(part[2]) + 2):
                        bank = full(act, n, "proj", part, u % 2)
                        if n.i is not None or n.c >= 3:
                            act.wait_ge(hid_lo, n.at(HT, u + 5 - 3 * HT))
                        if u == 0:
                            wait(act, qk_stored, n.at(64))
                        scale = HD ** -0.5 / WS if u < 2 else 1.0 / WS
                        nc.scalar.activation(qk16[:, 0, u, :], bank[:, :], ACT.Identity, bias=bqk[:, u:u + 1], scale=scale)
                        gp_done(nc.scalar.activation(rows32[:, u, :], bank[:, :], ACT.Identity, bias=bqk[:, u:u + 1], scale=scale),
                                n, "proj", part, u % 2)
                else:
                    for t in range(2 * int(part[2]), 2 * int(part[2]) + 2):
                        drained(act, n, "proj", part, t % 2)
                        if t == 0:
                            wait(act, og_step, n.at(GATE_STEPS, -GATE_STEPS - 1))
                            wait(act, pv_done, n.at(H, -H))
                        nc.scalar.copy(vs[n.par][:, t, :, 0:HD], vg32[:, t % 2, 0:D].rearrange("q (h d) -> q h d", h=H)).then_inc(v_hi, 1)
                        nc.scalar.activation(eg[n.par][:, H * t:H * (t + 1), :].rearrange("q h d -> q (h d)"), vg32[:, t % 2, D:2 * D],
                                             ACT.Exp, scale=-1.0).then_inc(eg_ready, 1)

            def gate(n, part):
                if part == "mul":
                    act.wait_ge(og_ready, n.at(1, 1))
                    nc.scalar.copy(og16[:, 0, :, :].rearrange("q t d -> q (t d)"), og[:, :, :].rearrange("q a d -> q (a d)")).then_inc(og_hi, 1)

            def outp(n, part):
                if part == "t":
                    transposed(n, "outp", lambda: feat_used_by_proj(act, n))
                elif part == "y":
                    act.wait_ge(nmr_ready, n.at(1, 1))
                    for t in range(TILES):
                        nc.scalar.activation(y32[:, t, :], y32[:, t, :], ACT.Identity, bias=nmr[:, t:t + 1], scale=rstd[:, t:t + 1]).then_inc(y_ready, 1)
                    wait(act, scattered, n.at(128))
                    if n.i is None and n.c == 0:
                        act.wait_ge(cleared, 16 * CLEARINGS)
                    act.wait_ge(y_ready, n.at(4, 4))
                    nc.scalar.copy(y16[:, :, 0:D], y32[:, :, :]).then_inc(yh_ready, 1)

            def rout(n, part):
                if part == "t":
                    transposed(n, "rout", lambda: full(act, n, "outp", "w", 1))
                else:
                    for k in range(2):
                        ht = 2 * int(part[1]) + k
                        bank = full(act, n, "rout", part, k)
                        wait(act, hid_lo, n.at(HT, ht - 3))
                        if ht == 0:
                            act.wait_ge(qk_split, n.at(4, 12) if n.i is not None else min(n.at(4, 12), 4 * B))
                        if ht == 0 and (n.i is not None or n.c > 0):
                            full(act, n.shift(-1), "rank", "l", 0)
                        nc.scalar.activation(hid16[:, 0, ht, :], bank[:, :], ACT.Relu, bias=br1[:, ht:ht + 1], scale=1.0 / WS)
                        gp_done(nc.scalar.activation(rows32[:, ht % 4, :], bank[:, :], ACT.Relu, bias=br1[:, ht:ht + 1], scale=1.0 / WS),
                                n, "rout", part, k)

            def rank(n, part):
                if part == "l":
                    act.wait_ge(diff_ready, n.at(1, 1))
                    nc.scalar.activation(rexp[:, :], rdiff[:, :], ACT.Exp).then_inc(rexp_ready, 1)

            run_iterations(act, "act", lambda it, k: None, dict(split=split, feat=feat, proj=proj, gate=gate, outp=outp, rout=rout, rank=rank), tail)

        @block.vector
        def _(dve):
            alone = Apart(dve, dve_passed)

            def biases(n, h):
                p, e = h // 2, h % 2
                if head_at(n, h - 2):
                    split_done(dve, *head_at(n, h - 2))
                for k, js in enumerate(((0,), (1, 3), (2,))):
                    bank, before = st_slot(n, h, k)
                    dve.wait_ge(st_full[bank], before + 1)
                    for j in js:
                        w = N - P * j
                        at = COL[j] % 512
                        last = nc.vector.tensor_tensor(sc[:, h % 2, COL[j]:COL[j] + w], st[bank][:, at:at + w], score_bias[:, e, p, 0:w], ALU.add)
                    last.then_inc(st_drained[bank], 1)

            def head(it, k):
                if head_at(it, k):
                    biases(*head_at(it, k))
                if head_at(it, k - 1) and (k - 1) % H not in POOL_HEADS:
                    split_weights(dve, nc.vector, *head_at(it, k - 1))

            def proj(n, part):
                if part[:2] == "vg":
                    for t in range(2 * int(part[2]), 2 * int(part[2]) + 2):
                        bank = full(dve, n, "proj", part, t % 2)
                        wait(dve, v_split, n.at(4, t - 1))
                        wait(dve, eg_ready, n.at(4, t - 1))
                        gp_done(nc.vector.scalar_tensor_tensor(vg32[:, t % 2, :], bank[:, :], 1.0 / WS, bvg[:, :], ALU.mult, ALU.add),
                                n, "proj", part, t % 2)

            def gate(n, part):
                split4 = lambda t: t[:, :, :].rearrange("q (i h) d -> q i h d", h=H)
                if part != "mul":
                    h0, h1 = GATED[part]
                    heads = slice(h0, h1)
                if part[:3] == "sum":
                    if h0 == 0:
                        wait(dve, og_lo, n.at(1))
                        dve.wait_ge(eg_ready, n.at(TILES, TILES))
                    dve.wait_ge(o_drained, n.at(PAIRS, h1 // 2))
                    nc.vector.tensor_tensor(split4(og)[:, :, heads, :], ob[:, :, heads, 0:HD], ob[:, :, heads, HD + 1:VW], ALU.add)
                    for i in range(TILES):
                        last = nc.vector.scalar_tensor_tensor(split4(oden)[:, i, heads, :], split4(eg[n.par])[:, i, heads, :], 1.0,
                                                              ob[:, i, heads, HD:HD + 1].to_broadcast([P, h1 - h0, HD]), ALU.add, ALU.mult)
                    last.then_inc(og_step, 1)
                elif part[:3] == "inv":
                    dve.wait_ge(og_step, n.at(GATE_STEPS, list(GATED).index(part)))
                    v = oden[:, :, :].rearrange("q (i h) d -> q i (h d)", h=H)[:, :, HD * h0:HD * h1]
                    nc.vector.reciprocal(v, v).then_inc(og_step, 1)
                else:
                    dve.wait_ge(og_step, n.at(GATE_STEPS, GATE_STEPS))
                    nc.vector.tensor_tensor(og[:, :, :], og[:, :, :], oden[:, :, :], ALU.mult).then_inc(og_ready, 1)

            def maxp(n, part):
                if part == "t":
                    bank = full(dve, n, "maxp", "t", 0)
                    wait(dve, m_stored, n.at(16))
                    view = bank[0:H, :].bitcast(F16)
                    nc.vector.tensor_copy(m_nearT[:, :], view[:, 0:N]).then_inc(m_copied, 1)
                    dve.wait_ge(m_copied, n.at(1, 1))
                    gp_done(nc.vector.tensor_tensor(mT[:, :].rearrange("h (a r) -> h r a", r=FAR_STEP),
                                                    view[:, N:2 * N].rearrange("h (r a) -> h r a", r=FAR_STEP),
                                                    m_nearT[:, :].rearrange("h (a r) -> h r a", r=FAR_STEP), ALU.min), n, "maxp", "t", 0)
                    return
                for e in (range(2) if part[:4] == "near" else (int(part[3]) % 2,)):
                    bank = full(dve, n, "maxp", part, e if part[:4] == "near" else 0)
                    if part[:4] == "near":
                        gp_done(nc.vector.tensor_reduce(m_near[:, int(part[4]), e, :], bank[:, :].rearrange("q (p w) -> q p w", p=PAIRS),
                                                        AX.X, ALU.max, negate=True), n, "maxp", part, e)
                    else:
                        g2 = 2 * (int(part[3]) // 2)
                        gp_done(nc.vector.tensor_reduce(m_far[:, g2:g2 + 2, e, :], bank[:, :].rearrange("q (g p w) -> q g p w", g=2, p=PAIRS),
                                                        AX.X, ALU.max, negate=True), n, "maxp", part, 0)

            def outp(n, part):
                if part == "w":
                    wait(dve, y_stored, n.at(16))
                    wait(dve, yh_ready, n.at(1))
                    for u in range(2):
                        bank = full(dve, n, "outp", "w", u)
                        dve.wait_ge(xres_ready, n.at(1, 1))
                        gp_done(nc.vector.scalar_tensor_tensor(y32[:, 2 * u:2 * u + 2, :], bank[:, :].rearrange("q (t d) -> q t d", t=2), 1.0 / WS,
                                                               xres[:, 2 * u:2 * u + 2, :], ALU.mult, ALU.add), n, "outp", "w", u)
                    for u in range(2):
                        drained(dve, n, "outp", "w", u)
                    for t in range(TILES):
                        nc.vector.bn_stats(stats[:, t, :], y32[:, t, :]).then_inc(ln_step, 1)
                    alone.wait_ge(ln_step, n.at(TILES, TILES))
                    for t in range(TILES):
                        nc.vector.bn_aggr(mv[:, t, :], stats[:, t, :]).then_inc(var_ready, 1)
                elif part == "y":
                    dve.wait_ge(yh_ready, n.at(1, 1))
                    nc.vector.tensor_tensor(y16[:, :, D:2 * D], y32[:, :, :], y16[:, :, 0:D], ALU.subtract).then_inc(yl_ready, 1)

            def rout(n, part):
                if part[0] == "h":
                    for k in range(2):
                        ht = 2 * int(part[1]) + k
                        drained(dve, n, "rout", part, k)
                        nc.vector.tensor_tensor(hid16[:, 1, ht, :], rows32[:, ht % 4, :], hid16[:, 0, ht, :], ALU.subtract).then_inc(hid_lo, 1)

            def rank(n, part):
                RS = 12

                def step(k, instruction):
                    instruction.then_inc(r_step, 1)
                    (alone if k == 2 else dve).wait_ge(r_step, n.at(RS, k))

                if part == "l":
                    bank = full(dve, n, "rank", "l", 0)
                    pairs = bank[:, 0:16 * TILES].rearrange("q (t k e) -> q t k e", t=TILES, k=2)
                    step(1, nc.vector.scalar_tensor_tensor(lg[:, :, :], pairs[:, :, 1, :], 1.0 / WS, br2[:, :, :], ALU.mult, ALU.add))
                    gp_done(nc.vector.scalar_tensor_tensor(lg[:, :, :], pairs[:, :, 0, :], 1.0 / WS, lg[:, :, :], ALU.mult, ALU.add), n, "rank", "l", 0)
                    drained(alone, n, "rank", "l", 0)
                    for t in range(TILES):
                        last = nc.vector.max(top[:, t, :], lg[:, t, :])
                    step(2, last)
                    for t in range(TILES):
                        last = nc.vector.max_index(topi[:, t, :], top[:, t, :], lg[:, t, :])
                    step(3, last)
                    step(4, nc.vector.tensor_copy(topf[:, :, :], topi[:, :, 0:2]))
                    step(5, nc.vector.tensor_tensor(onehot[:, :, :, :], expert_id[:, :].unsqueeze(1).unsqueeze(1).to_broadcast([P, TILES, 2, E]),
                                                    topf[:, :, :].unsqueeze(3).to_broadcast([P, TILES, 2, E]), ALU.is_equal))
                    nc.vector.tensor_tensor(chosen[:, :, :], onehot[:, :, 0, :], onehot[:, :, 1, :], ALU.add).then_inc(chosen_ready, 1)
                    nc.vector.tensor_tensor(rdiff[:, :], top[:, :, 1], top[:, :, 0], ALU.subtract).then_inc(diff_ready, 1)
                elif part == "c":
                    bank = full(dve, n, "rank", "c", 0)
                    dve.wait_ge(rexp_ready, n.at(1, 1))
                    nc.vector.tensor_scalar(rdiff[:, :], rexp[:, :], 1.0, None, ALU.add).then_inc(w_step, 1)
                    nc.vector.tensor_tensor(rpos[:, :, :], bank[:, 0:E * TILES].rearrange("q (t e) -> q t e", t=TILES),
                                            taken[:, :].unsqueeze(1).to_broadcast([P, TILES, E]), ALU.add).then_inc(r_step, 1)
                    dve.wait_ge(w_step, n.at(2, 1))
                    nc.vector.reciprocal(rprob[:, :, 0], rdiff[:, :]).then_inc(w_step, 1)
                    dve.wait_ge(r_step, n.at(RS, 6))
                    nc.vector.tensor_scalar(rover[:, :, :], rpos[:, :, :], float(CAP), DROPPED, ALU.is_ge, ALU.mult).then_inc(r_step, 1)
                    gp_done(nc.vector.tensor_tensor(taken[:, :], bank[:, E * TILES:E * (TILES + 1)], taken[:, :], ALU.add), n, "rank", "c", 0)
                    dve.wait_ge(w_step, n.at(2, 2))
                    nc.vector.tensor_tensor(rprob[:, :, 1], rexp[:, :], rprob[:, :, 0], ALU.mult).then_inc(rprob_ready, 1)
                    dve.wait_ge(r_step, n.at(RS, 7))
                    step(8, nc.vector.tensor_tensor(rpos[:, :, :], rpos[:, :, :], rover[:, :, :], ALU.add))
                    step(9, nc.vector.tensor_tensor(rpos[:, :, :], rpos[:, :, :], expert_row[:, :, :], ALU.add))
                    step(10, nc.vector.tensor_tensor(rprod[:, :, :, :], onehot[:, :, :, :], rpos[:, :, :].unsqueeze(2).to_broadcast([P, TILES, 2, E]), ALU.mult))
                    step(11, nc.vector.tensor_reduce(rslot[:, :, :], rprod[:, :, :, :], AX.X, ALU.add))
                    wait(dve, scattered, n.at(128))
                    nc.vector.tensor_copy(sidx[:, :, :], rslot[:, :, :]).then_inc(sidx_ready, 1)
                    nc.vector.tensor_scalar(gslot[:, bass.ds(n.at(2 * TILES), 2 * TILES)], rslot[:, :, :].rearrange("q t k -> q (t k)"),
                                            float(SLOTS - 1), None, ALU.min)
                    nc.vector.tensor_scalar(rkeep[:, :, :], rslot[:, :, :], float(SLOTS), None, ALU.is_lt).then_inc(r_step, 1)
                    dve.wait_ge(r_step, n.at(RS, 12))
                    dve.wait_ge(rprob_ready, n.at(1, 1))
                    nc.vector.tensor_tensor(gweight[:, bass.ds(n.at(2 * TILES), 2 * TILES)], rprob[:, :, :].rearrange("q t k -> q (t k)"),
                                            rkeep[:, :, :].rearrange("q t k -> q (t k)"), ALU.mult)

            rprob_ready = sem("rprob_ready")
            dve.wait_ge(tables_in, 160)
            for e in range(2):
                last = nc.vector.memset(near_mask[STACK * e + 32:STACK * e + 64, :, 0:32], NEG16)
            last.then_inc(mask_ready, 1)
            run_iterations(dve, "dve", head, dict(proj=proj, maxp=maxp, gate0=gate, gate=gate, outp=outp, rout=rout, rank=rank))

        @block.gpsimd
        def _(gpsimd):
            pool = Apart(gpsimd, pool_passed)

            def proj(n, part):
                if part[:2] == "qk":
                    for u in range(2 * int(part[2]), 2 * int(part[2]) + 2):
                        drained(pool, n, "proj", part, u % 2)
                        nc.gpsimd.tensor_tensor(qk16[:, 1, u, :], rows32[:, u, :], qk16[:, 0, u, :], ALU.subtract).then_inc(qk_split, 1)
                elif part[:2] == "vg":
                    for t in range(2 * int(part[2]), 2 * int(part[2]) + 2):
                        v = vg32[:, t % 2, 0:D].rearrange("q (h d) -> q h d", h=H)
                        pool.wait_ge(v_hi, n.at(4, t + 1))
                        nc.gpsimd.tensor_tensor(vs[n.par][:, t, :, HD + 1:VW], v, vs[n.par][:, t, :, 0:HD], ALU.subtract).then_inc(v_split, 1)

            def outp(n, part):
                if part == "t":
                    pool.wait_ge(xres_loaded, n.at(16, 16))
                    nc.gpsimd.tensor_tensor(xres[:, :, :], xres[:, :, :], g_bo, ALU.add).then_inc(xres_ready, 1)
                elif part == "w":
                    pool.wait_ge(var_ready, n.at(TILES, TILES))
                    nc.gpsimd.tensor_scalar(veps[:, :], mv[:, :, 1], LN_EPS, 0.0, ALU.add, ALU.max)
                    nc.gpsimd.tensor_scalar(nmr[:, :], mv[:, :, 0], -1.0, 0.0, ALU.mult, ALU.add).then_inc(veps_ready, 1)
                    pool.wait_ge(veps_ready, n.at(1, 1))
                    nc.gpsimd.tensor_tensor(rstd[:, :], veps[:, :], halfneg[:, :], ALU.pow).then_inc(rstd_ready, 1)
                    pool.wait_ge(rstd_ready, n.at(1, 1))
                    nc.gpsimd.tensor_tensor(nmr[:, :], nmr[:, :], rstd[:, :], ALU.mult).then_inc(nmr_ready, 1)

            def split(n, part):
                pool.wait_ge(xh_ready, n.at(1, 1))
                nc.gpsimd.tensor_tensor(x16[:, 1, :, :], xin[:, :, :], x16[:, 0, :, :], ALU.subtract).then_inc(xl_ready, 1)

            def rank(n, part):
                if part[0] == "s":
                    if part == "s0":
                        if n.i is None and n.c == 0:
                            pool.wait_ge(cleared, 16 * CLEARINGS)
                        pool.wait_ge(sidx_ready, n.at(1, 1))
                        pool.wait_ge(yh_ready, n.at(1, 1))
                        pool.wait_ge(yl_ready, n.at(1, 1))
                    t = int(part[1])
                    for k in range(2):
                        nc.gpsimd.indirect_dma_start(
                            out=disp[:, :], out_offset=bass.IndirectOffsetOnAxis(ap=sidx[:, t, k:k + 1], axis=0),
                            in_=y16[:, t, :], in_offset=None, bounds_check=SLOTS - 1, oob_is_err=False).then_inc(scattered, 16)

            def gate(n, part):
                if part == "mul":
                    pool.wait_ge(og_hi, n.at(1, 1))
                    nc.gpsimd.tensor_tensor(og16[:, 1, :, :].rearrange("q t d -> q (t d)"), og[:, :, :].rearrange("q a d -> q (a d)"),
                                            og16[:, 0, :, :].rearrange("q t d -> q (t d)"), ALU.subtract).then_inc(og_lo, 1)

            def head(it, k):
                if head_at(it, k - 1) and (k - 1) % H in POOL_HEADS:
                    split_weights(pool, nc.gpsimd, *head_at(it, k - 1))

            g_bo = bo[:, :].unsqueeze(1).to_broadcast([P, TILES, D])
            run_iterations(gpsimd, "pool", head, dict(split=split, proj=proj, gate=gate, outp=outp, rank=rank))
            pool.wait_ge(scattered, 128 * B)


def setup(nc, g, a):
    with ExitStack() as ctx:
        def sem(name):
            return ctx.enter_context(nc.semaphore(name))

        ident, zero_rows = g["ident"], a["y16"]
        bias_vec, near_vec, far_vec, disp, pos_bias = g["bias_vec"], g["near_vec"], g["far_vec"], g["disp"], g["pos_bias"]
        score_bias = a["score_bias"]
        stage = score_bias[:, :, :, :].rearrange("p e h n -> p (e h n)")
        tiles = lambda w: w.rearrange("(c p) n -> p c n", p=P)
        scratch = a["og"][:, :, :].rearrange("p a d -> p (a d)")
        pb_t, vec_b = scratch[0:H, 0:NOFF], scratch[0:H, P:P + P + N]
        vec_n, vec_f = a["m_nearT"][:, 0:96], a["m_nearT"][:, 128:192]
        qkv_s = stage[:, 0:1536].rearrange("p (c n) -> p c n", c=CT)
        gate_s = stage[:, 1536:2048].rearrange("p (c n) -> p c n", c=CT)
        out_s = stage[:, 2048:2560].rearrange("p (c n) -> p c n", c=CT)
        r1_s = stage[:, 2560:4608].rearrange("p (c n) -> p c n", c=CT)
        r2_s = stage[:, 4608:4672].rearrange("p (c n) -> p c n", c=HT)
        splits = [(qkv_s[:, :, 0:2 * D], a["wqk"][:, 0, :, :], a["wqk"][:, 1, :, :]),
                  (qkv_s[:, :, 2 * D:3 * D], a["wvg"][:, 0, :, 0:D], a["wvg"][:, 1, :, 0:D]),
                  (gate_s, a["wvg"][:, 0, :, D:2 * D], a["wvg"][:, 1, :, D:2 * D]),
                  (out_s, a["wout"][:, 0, :, :], a["wout"][:, 1, :, :]),
                  (r1_s, a["wr1"][:, 0, :, :], a["wr1"][:, 1, :, :]),
                  (r2_s, a["wr2"][:, :, 0:E], a["wr2"][:, :, E:2 * E])]

        loaded, stored = sem("setup_loaded"), sem("setup_stored")
        hi, lo = sem("setup_hi"), sem("setup_lo")
        base, vec_base, vec_done, biased = sem("setup_base"), sem("vec_base"), sem("vec_done"), sem("setup_biased")
        loads = [(qkv_s, tiles(g["Wqkv"])), (gate_s, tiles(g["Wgate"])), (out_s, tiles(g["Wout"])), (r1_s, tiles(g["rw1"])),
                 (r2_s, tiles(g["rw2"])), (pb_t, g["pos_bias"].rearrange("o h -> h o")),
                 (a["bqk"][:, :], g["bqkv"][0:2 * D].rearrange("(u p) -> p u", p=P)),
                 (a["bvg"][:, 0:D], g["bqkv"][2 * D:3 * D].partition_broadcast(P)),
                 (a["bvg"][:, D:2 * D], g["bgate"].partition_broadcast(P)),
                 (a["bo"][:, :], g["bout"].partition_broadcast(P)),
                 (a["br1"][:, :], g["rb1"].rearrange("(u p) -> p u", p=P))] + \
                [(a["br2"][:, t, :], g["rb2"].partition_broadcast(P)) for t in range(TILES)]

        with nc.Block() as block:
            @block.sync
            def _(sp):
                for dst, src in loads:
                    sp.dma_start(dst, src, allow_slow_non_contiguous=True).then_inc(loaded, 16)
                sp.wait_ge(vec_done, 1)
                for vec, copies, src in ((bias_vec, P, vec_b), (near_vec, 32, vec_n), (far_vec, 32, vec_f)):
                    sp.dma_start(vec, src.unsqueeze(1).to_broadcast([H, copies, vec.shape[2]])).then_inc(stored, 16)
                sp.wait_ge(stored, 48)

            @block.gpsimd
            def _(pool):
                nc.gpsimd.memset(zero_rows[:, :, :], 0.0)
                for t in (ident, a["sel_first"], a["sel_rest"]):
                    last = nc.gpsimd.memset(t[:, :], 0.0)
                for t in (a["ones_mat"], a["before_mat"]):
                    last = nc.gpsimd.memset(t[:, :], 1.0)
                for i in range(2):
                    last = nc.gpsimd.memset(a["vs"][i][:, :, :, HD:HD + 1], 1.0)
                last.then_inc(base, 1)
                pool.wait_ge(base, 1)
                count = 1
                nc.gpsimd.affine_select(out=ident[:, :], in_=ident[:, :], compare_op=ALU.not_equal, fill=1.0,
                                        base=0, pattern=[[-1, P]], channel_multiplier=1)
                nc.gpsimd.affine_select(out=a["before_mat"][:, :], in_=a["before_mat"][:, :], compare_op=ALU.is_gt, fill=0.0,
                                        base=0, pattern=[[1, P]], channel_multiplier=-1).then_inc(base, 1)
                count += 1
                pool.wait_ge(base, count)
                for e in range(2):
                    r = STACK * e
                    for t, rows, c0, blocks in ((a["sel_rest"], slice(r, r + 32), 0, 4), (a["sel_first"], slice(r, r + 32), 32, 3),
                                                (a["sel_first"], slice(r + 32, r + 64), 0, 1)):
                        v = t[rows, c0:c0 + 32 * blocks].rearrange("r (b q) -> r b q", q=32)
                        nc.gpsimd.affine_select(out=v, in_=v, compare_op=ALU.not_equal, fill=1.0, base=0,
                                                pattern=[[0, blocks], [-1, 32]], channel_multiplier=1).then_inc(base, 1)
                        count += 1
                        pool.wait_ge(base, count)
                for e in range(E):
                    nc.gpsimd.memset(a["expert_id"][:, e:e + 1], float(e))
                    nc.gpsimd.memset(a["expert_row"][:, :, e:e + 1], float(e * CAP))
                nc.gpsimd.memset(a["taken"][:, :], 0.0)
                nc.gpsimd.memset(a["halfneg"][:, :], -0.5)

            @block.scalar
            def _(act):
                act.wait_ge(loaded, 16 * len(loads))
                for src, h, _ in splits:
                    nc.scalar.activation(h, src, ACT.Copy, scale=WS).then_inc(hi, 1)
                nc.scalar.mul(a["bqk"][:, 0:2], a["bqk"][:, 0:2], HD ** -0.5)

            @block.vector
            def _(dve):
                nc.vector.memset(vec_b, NEG)
                nc.vector.memset(vec_n, NEG16)
                nc.vector.memset(vec_f, NEG16).then_inc(vec_base, 1)
                dve.wait_ge(vec_base, 1)
                dve.wait_ge(loaded, 16 * len(loads))
                nc.vector.tensor_copy(vec_b[:, P - 1:P + NEAR], pb_t[:, 0:NEAR + 1])
                for k, off in enumerate(OFFSETS):
                    if off > NEAR:
                        last = nc.vector.tensor_copy(vec_b[:, P - 1 + off:P + off], pb_t[:, k:k + 1])
                    else:
                        nc.vector.tensor_copy(vec_n[:, 63 - off:64 - off], pb_t[:, k:k + 1])
                    if off % FAR_STEP == 0:
                        z = 31 - off // FAR_STEP
                        last = nc.vector.tensor_copy(vec_f[:, z:z + 1], pb_t[:, k:k + 1])
                last.then_inc(vec_done, 1)
                for k, (src, h, l) in enumerate(splits):
                    dve.wait_ge(hi, k + 1)
                    nc.vector.scalar_tensor_tensor(l, src, WS, h, ALU.mult, ALU.subtract).then_inc(lo, 1)
                for i in range(2):
                    for e in range(2):
                        nc.vector.memset(a["ks"][i][STACK * e + 32:STACK * (e + 1), :, :], 1.0)


def experts(nc, g):
    ROWS = 512
    GROUPS = CAP // ROWS
    RT = ROWS // P
    with ExitStack() as ctx:
        def sb(name, shape, dt):
            return ctx.enter_context(nc.sbuf_tensor(name, shape, dt))

        def sem(name):
            return ctx.enter_context(nc.semaphore(name))

        ident, disp, eo = g["ident"], g["disp"], g["eo"]
        w1s, w2s = sb("w1s", [P, CT, FF], FP32), sb("w2s", [P, HT, D], FP32)
        w1 = [sb(f"w1_{i}", [P, 2, CT, FF], F16) for i in range(2)]
        w2 = [sb(f"w2_{i}", [P, 2, HT, D], F16) for i in range(2)]
        b1 = sb("b1", [P, E, HT], FP32)
        b2 = sb("b2", [P, E, D], FP32)
        rows = sb("rows", [P, 2, RT, 2 * D], F16)
        rowsT = sb("rowsT", [P, 2, 2, CT, ROWS], F16)
        h32 = sb("h32", [P, 2, ROWS], FP32)
        h16 = sb("h16", [P, 2, 2, HT, ROWS], F16)
        y = sb("y", [P, 2, RT, D], FP32)
        tr = [ctx.enter_context(nc.psum_tensor(f"tr{i}", [P, 512], FP32)) for i in range(2)]
        up = [ctx.enter_context(nc.psum_tensor(f"up{i}", [P, 512], FP32)) for i in range(4)]
        dn = [ctx.enter_context(nc.psum_tensor(f"dn{i}", [P, 512], FP32)) for i in range(2)]

        act_passed = sem("experts_act_passed")
        b1_in, b2_in, w1_in, w2_in = sem("b1_in"), sem("b2_in"), sem("w1_in"), sem("w2_in")
        w1_hi, w1_lo, w2_hi, w2_lo = sem("w1_hi"), sem("w1_lo"), sem("w2_hi"), sem("w2_lo")
        rows_in = [sem(f"rows_in{i}") for i in range(2)]
        tr_full = [sem(f"tr_full{i}") for i in range(2)]
        tr_drained = [sem(f"tr_drained{i}") for i in range(2)]
        up_full, up_drained = sem("up_full"), sem("up_drained")
        h_lo = sem("h_lo")
        dn_full, dn_drained = sem("dn_full"), sem("dn_drained")
        y_out = [sem(f"y_out{i}") for i in range(2)]

        def run(eng, step):
            for c in range(2):
                step(Batch(None, c), 0)
                step(Batch(None, c), 1)
            with eng.Fori(1, E // 2 - 1) as i:
                for c in range(2):
                    step(Batch(i, c), 0)
                    step(Batch(i, c), 1)
            for c in range(E - 2, E):
                step(Batch(None, c), 0)
                step(Batch(None, c), 1)

        def nxt(e, gr):
            return (e, 1) if gr == 0 else (e.shift(1), 0)

        def prev(e, gr):
            return (e, 0) if gr == 1 else (e.shift(-1), 1)

        def exists(e):
            return e.i is not None or 0 <= e.c < E

        with nc.Block() as block:
            @block.sync
            def _(sp):
                def load_w1(e):
                    wait(sp, w1_lo, e.at(1))
                    sp.dma_start(w1s[:, :, :], g["ew1"].rearrange("e (c p) n -> p (e c) n", p=P)[:, bass.ds(e.at(CT), CT), :]).then_inc(w1_in, 16)

                def load_w2(e):
                    wait(sp, w2_lo, e.at(1))
                    sp.dma_start(w2s[:, :, :], g["ew2"].rearrange("e (c p) n -> p (e c) n", p=P)[:, bass.ds(e.at(HT), HT), :]).then_inc(w2_in, 16)

                def load_rows(e, gr):
                    wait(sp, tr_full[1], e.at(2, gr - 1))
                    sp.dma_start(rows[:, gr, :, :], disp[bass.ds(e.at(CAP, gr * ROWS), ROWS), :].rearrange("(t p) d -> p t d", p=P)).then_inc(rows_in[gr], 16)

                def store(e, gr):
                    sp.wait_ge(dn_drained, e.at(4, 2 * gr + 2))
                    sp.dma_start(eo[bass.ds(e.at(CAP, gr * ROWS), ROWS), :].rearrange("(t p) d -> p t d", p=P), y[:, gr, :, :]).then_inc(y_out[gr], 16)

                load_rows(Batch(None, 0), 0)
                load_w1(Batch(None, 0))
                sp.dma_start(b1[:, :, :], g["eb1"].rearrange("e (h p) -> p e h", p=P), allow_slow_non_contiguous=True).then_inc(b1_in, 16)
                load_w2(Batch(None, 0))
                load_rows(Batch(None, 0), 1)
                sp.dma_start(b2[:, :, :].rearrange("p e d -> p (e d)"), g["eb2"].rearrange("e d -> (e d)").partition_broadcast(P)).then_inc(b2_in, 16)

                def step(e, gr):
                    if exists(e.shift(1)):
                        (load_w1 if gr == 0 else load_w2)(e.shift(1))
                        load_rows(e.shift(1), gr)
                    if exists(prev(e, gr)[0]):
                        store(*prev(e, gr))

                run(sp, step)
                store(Batch(None, E - 1), 1)
                for i in range(2):
                    sp.wait_ge(y_out[i], 16 * E)

            @block.tensor
            def _(pe):
                def transposes(e, gr):
                    pe.wait_ge(rows_in[gr], e.at(16, 16))
                    for i in range(2):
                        wait(pe, tr_drained[i], e.at(2, gr))
                        view = tr[i][:, :].bitcast(F16)
                        for c in range(CT):
                            for t in range(RT):
                                last = nc.tensor.transpose(view[:, c * ROWS + t * P:c * ROWS + (t + 1) * P],
                                                           rows[:, gr, t, D * i + P * c:D * i + P * (c + 1)], ident[:, :])
                        last.then_inc(tr_full[i], 1)

                terms = ((0, 0), (0, 1), (1, 0))

                def up_product(e, gr):
                    for i in range(2):
                        pe.wait_ge(tr_drained[i], e.at(2, gr + 1))
                    pe.wait_ge(w1_lo, e.at(1, 1))
                    for h in range(HT):
                        wait(pe, up_drained, e.at(16, 8 * gr + h - 3))
                        k = 0
                        for c in range(CT):
                            for a, b in terms:
                                last = nc.tensor.matmul(up[h % 4][:, :], w1[e.par][:, a, c, P * h:P * (h + 1)], rowsT[:, gr, b, c, :],
                                                        start=(k == 0), stop=(k == 5))
                                k += 1
                        last.then_inc(up_full, 1)

                def down_product(e, gr):
                    pe.wait_ge(h_lo, e.at(16, 8 * gr + 8))
                    pe.wait_ge(w2_lo, e.at(1, 1))
                    for u in range(2):
                        wait(pe, dn_drained, e.at(4, 2 * gr + u - 1))
                        for t in (2 * u, 2 * u + 1):
                            k = 0
                            for h in range(HT):
                                for a, b in terms:
                                    last = nc.tensor.matmul(dn[u][:, D * (t % 2):D * (t % 2 + 1)], h16[:, gr, a, h, P * t:P * (t + 1)],
                                                            w2[e.par][:, b, h, :], start=(k == 0), stop=(k == 3 * HT - 1))
                                    k += 1
                        last.then_inc(dn_full, 1)

                transposes(Batch(None, 0), 0)

                def step(e, gr):
                    up_product(e, gr)
                    if exists(nxt(e, gr)[0]):
                        transposes(*nxt(e, gr))
                    if exists(prev(e, gr)[0]):
                        down_product(*prev(e, gr))

                run(pe, step)
                down_product(Batch(None, E - 1), 1)

            def row_evacuation(eng, copy, i, e, gr):
                eng.wait_ge(tr_full[i], e.at(2, gr + 1))
                wait(eng, up_full, e.at(16, 8 * (gr - 1)))
                copy(rowsT[:, gr, i, :, :].rearrange("f c t -> f (c t)"), tr[i][:, :].bitcast(F16)).then_inc(tr_drained[i], 1)

            @block.scalar
            def _(act):
                alone = Apart(act, act_passed)

                def split_w1(e):
                    act.wait_ge(w1_in, e.at(16, 16))
                    wait(act, up_full, e.at(16, -16))
                    nc.scalar.activation(w1[e.par][:, 0, :, :], w1s[:, :, :], ACT.Copy, scale=WS).then_inc(w1_hi, 1)

                def split_w2(e):
                    act.wait_ge(w2_in, e.at(16, 16))
                    wait(act, dn_full, e.at(4, -4))
                    nc.scalar.activation(w2[e.par][:, 0, :, :], w2s[:, :, :], ACT.Copy, scale=WS).then_inc(w2_hi, 1)

                row_evacuation(act, nc.scalar.copy, 1, Batch(None, 0), 0)
                split_w1(Batch(None, 0))
                split_w2(Batch(None, 0))
                act.wait_ge(b1_in, 16)

                def step(e, gr):
                    wait(alone, dn_full, e.at(4, 2 * gr - 2))
                    for h in range(HT):
                        alone.wait_ge(up_full, e.at(16, 8 * gr + h + 1))
                        wait(alone, h_lo, e.at(16, 8 * gr + h - 1))
                        nc.scalar.activation(h16[:, gr, 0, h, :], up[h % 4][:, :], ACT.Relu, bias=g_b1(e, h), scale=1.0 / WS)
                        nc.scalar.activation(h32[:, h % 2, :], up[h % 4][:, :], ACT.Relu, bias=g_b1(e, h), scale=1.0 / WS).then_inc(up_drained, 1)
                    if exists(nxt(e, gr)[0]):
                        row_evacuation(act, nc.scalar.copy, 1, *nxt(e, gr))
                    if exists(e.shift(1)):
                        (split_w1 if gr == 0 else split_w2)(e.shift(1))

                def g_b1(e, h):
                    return b1[:, bass.ds(e.at(1), 1), h]

                run(act, step)

            @block.vector
            def _(dve):
                def split_w1(e):
                    dve.wait_ge(w1_hi, e.at(1, 1))
                    nc.vector.scalar_tensor_tensor(w1[e.par][:, 1, :, :], w1s[:, :, :], WS, w1[e.par][:, 0, :, :], ALU.mult, ALU.subtract).then_inc(w1_lo, 1)

                def split_w2(e):
                    dve.wait_ge(w2_hi, e.at(1, 1))
                    nc.vector.scalar_tensor_tensor(w2[e.par][:, 1, :, :], w2s[:, :, :], WS, w2[e.par][:, 0, :, :], ALU.mult, ALU.subtract).then_inc(w2_lo, 1)

                def down_evacuation(e, gr):
                    for u in range(2):
                        dve.wait_ge(dn_full, e.at(4, 2 * gr + u + 1))
                        wait(dve, y_out[gr], e.at(16))
                        nc.vector.scalar_tensor_tensor(y[:, gr, 2 * u:2 * u + 2, :], dn[u][:, :].rearrange("p (t d) -> p t d", t=2), 1.0 / WS,
                                                       b2[:, bass.ds(e.at(1), 1), :].to_broadcast([P, 2, D]), ALU.mult, ALU.add).then_inc(dn_drained, 1)

                row_evacuation(dve, nc.vector.tensor_copy, 0, Batch(None, 0), 0)
                split_w1(Batch(None, 0))
                split_w2(Batch(None, 0))
                dve.wait_ge(b2_in, 16)

                def step(e, gr):
                    for h in range(HT):
                        dve.wait_ge(up_drained, e.at(16, 8 * gr + h + 1))
                        nc.vector.tensor_tensor(h16[:, gr, 1, h, :], h32[:, h % 2, :], h16[:, gr, 0, h, :], ALU.subtract).then_inc(h_lo, 1)
                    if exists(nxt(e, gr)[0]):
                        row_evacuation(dve, nc.vector.tensor_copy, 0, *nxt(e, gr))
                    if exists(e.shift(1)):
                        (split_w1 if gr == 0 else split_w2)(e.shift(1))
                    if exists(prev(e, gr)[0]):
                        down_evacuation(*prev(e, gr))

                run(dve, step)
                down_evacuation(Batch(None, E - 1), 1)


def combine(nc, g):
    BUFS = 4
    with ExitStack() as ctx:
        def sb(name, shape, dt):
            return ctx.enter_context(nc.sbuf_tensor(name, shape, dt))

        def sem(name):
            return ctx.enter_context(nc.semaphore(name))

        gslot, gweight, xln, eo = g["gslot"], g["gweight"], g["xln"], g["eo"]
        K2 = 2 * TILES
        idx, wt = sb("idx", [P, BUFS, K2], U32), sb("wt", [P, BUFS, K2], FP32)
        res = sb("res", [P, BUFS, TILES, D], FP32)
        got = sb("got", [P, BUFS, K2, D], FP32)
        stats, mv = sb("stats2", [P, BUFS, TILES, 6], FP32), sb("mv2", [P, BUFS, TILES, 2], FP32)
        veps, halfneg = sb("veps2", [P, BUFS, TILES], FP32), sb("halfneg2", [P, TILES], FP32)
        rstd = sb("rstd2", [P, BUFS, TILES], FP32)
        res_in = [sem(f"res_in{i}") for i in range(BUFS)]
        got_in = [sem(f"got_in{i}") for i in range(BUFS)]
        stored = [sem(f"stored{i}") for i in range(BUFS)]
        idx_ready, half_ready = sem("idx_ready"), sem("half_ready")
        dve_passed, pool_passed = sem("combine_dve_passed"), sem("combine_pool_passed")
        wt_ready, added, c_stats, c_var, c_veps, c_rstd, c_done = (sem(s) for s in ("wt_ready", "added", "c_stats", "c_var", "c_veps", "c_rstd", "c_done"))

        def run(eng, step):
            for c in range(BUFS):
                step(Batch(None, c, BUFS))
            with eng.Fori(1, B // BUFS - 1) as i:
                for c in range(BUFS):
                    step(Batch(i, c, BUFS))
            for c in range(B - BUFS, B + 2):
                step(Batch(None, c, BUFS))

        def rows_of(t, n):
            return t[bass.ds(n.at(N), N), :].rearrange("(t p) d -> p t d", p=P)

        with nc.Block() as block:
            @block.sync
            def _(sp):
                def load(n):
                    wait(sp, stored[n.par], n.half(16))
                    sp.dma_start(res[:, n.par, :, :], rows_of(xln, n)).then_inc(res_in[n.par], 16)

                def store(n):
                    sp.wait_ge(c_done, n.at(TILES, TILES))
                    sp.dma_start(rows_of(g["out_rows"], n), res[:, n.par, :, :]).then_inc(stored[n.par], 16)

                def step(n):
                    if n.shift(-2).in_range():
                        store(n.shift(-2))
                    if n.i is not None or n.c + 2 < B:
                        load(n.shift(2))

                for c in range(2):
                    load(Batch(None, c, BUFS))
                run(sp, step)
                for i in range(BUFS):
                    sp.wait_ge(stored[i], 16 * (B // BUFS))

            @block.gpsimd
            def _(gpsimd):
                pool = Apart(gpsimd, pool_passed)
                nc.gpsimd.memset(halfneg[:, :], -0.5).then_inc(half_ready, 1)
                pool.wait_ge(half_ready, 1)

                def inverse_deviation(n):
                    wait(pool, c_rstd, n.at(1))
                    pool.wait_ge(c_var, n.at(TILES, TILES))
                    nc.gpsimd.tensor_scalar(veps[:, n.par, :], mv[:, n.par, :, 1], LN_EPS, 0.0, ALU.add, ALU.max).then_inc(c_veps, 1)
                    pool.wait_ge(c_veps, n.at(1, 1))
                    nc.gpsimd.tensor_tensor(rstd[:, n.par, :], veps[:, n.par, :], halfneg[:, :], ALU.pow).then_inc(c_rstd, 1)

                def step(n):
                    if n.in_range():
                        wait(pool, added, n.at(K2, -(BUFS - 1) * K2))
                        nc.gpsimd.tensor_copy(idx[:, n.par, :], gslot[:, bass.ds(n.at(K2), K2)]).then_inc(idx_ready, 1)
                        pool.wait_ge(idx_ready, n.at(1, 1))
                        for k in range(K2):
                            nc.gpsimd.indirect_dma_start(out=got[:, n.par, k, :], out_offset=None, in_=eo[:, :],
                                                         in_offset=bass.IndirectOffsetOnAxis(ap=idx[:, n.par, k:k + 1], axis=0)).then_inc(got_in[n.par], 16)
                    if n.shift(-2).in_range():
                        inverse_deviation(n.shift(-2))

                run(gpsimd, step)

            @block.vector
            def _(dve):
                alone = Apart(dve, dve_passed)

                def normalise(n):
                    dve.wait_ge(c_rstd, n.at(1, 1))
                    for t in range(TILES):
                        nc.vector.tensor_scalar(res[:, n.par, t, :], res[:, n.par, t, :], mv[:, n.par, t, 0:1], rstd[:, n.par, t:t + 1],
                                                ALU.subtract, ALU.mult).then_inc(c_done, 1)

                def add(n):
                    nc.vector.tensor_copy(wt[:, n.par, :], gweight[:, bass.ds(n.at(K2), K2)]).then_inc(wt_ready, 1)
                    dve.wait_ge(wt_ready, n.at(1, 1))
                    dve.wait_ge(res_in[n.par], n.half(16, 16))
                    dve.wait_ge(got_in[n.par], n.half(16 * K2, 16 * K2))
                    for k in range(2):
                        for t in range(TILES):
                            if k:
                                dve.wait_ge(added, n.at(K2, t + 1))
                            nc.vector.scalar_tensor_tensor(res[:, n.par, t, :], got[:, n.par, 2 * t + k, :], wt[:, n.par, 2 * t + k:2 * t + k + 1],
                                                           res[:, n.par, t, :], ALU.mult, ALU.add).then_inc(added, 1)
                    for t in range(TILES):
                        dve.wait_ge(added, n.at(K2, TILES + t + 1))
                        nc.vector.bn_stats(stats[:, n.par, t, :], res[:, n.par, t, :]).then_inc(c_stats, 1)
                    alone.wait_ge(c_stats, n.at(TILES, TILES))
                    for t in range(TILES):
                        nc.vector.bn_aggr(mv[:, n.par, t, :], stats[:, n.par, t, :]).then_inc(c_var, 1)

                def step(n):
                    if n.in_range():
                        add(n)
                    if n.shift(-2).in_range():
                        normalise(n.shift(-2))

                run(dve, step)


_INS = ["x", "Wqkv", "bqkv", "Wout", "bout", "Wgate", "bgate", "pos_bias"]
_FFN = ["rw1", "rb1", "rw2", "rb2", "ew1", "eb1", "ew2", "eb2"]
_NAMES = [f"L0_attn_{n}" for n in _INS] + [f"L0_ffn_{n}" for n in _FFN]


def kernel(**inputs):
    import numpy as _np
    import concourse.bacc as _bacc
    from concourse import mybir as _mybir
    from concourse.bass_utils import run_bass_kernel_spmd as _run

    nc = _bacc.Bacc("TRN2", target_bir_lowering=False, num_devices=1)
    arrays, args = {}, []
    for name in _NAMES:
        a = _np.ascontiguousarray(inputs[name])
        arrays[f"in_{name}"] = a
        args.append(nc.dram_tensor(f"in_{name}", a.shape, _mybir.dt.from_np(a.dtype), kind="ExternalInput").ap())
    args.append(nc.dram_tensor("out_0", (B, N, D), FP32, kind="ExternalOutput").ap())
    build(nc, *args)
    r = _run(nc, [arrays], core_ids=[0])
    return r.results[0]["out_0"]
```
